# Optimizing a Trainium2 kernel written in Bass

```python
import numpy as np
import jax
import jax.numpy as jnp

def _softmax(x, axis=-1):
    return jax.nn.softmax(x, axis=axis)

def _gelu(x):
    return jax.nn.gelu(x, approximate=True)

def _silu(x):
    return jax.nn.silu(x)

def _sigmoid(x):
    return jax.nn.sigmoid(x)

def _layernorm(x, axis=-1, eps=1e-05):
    m = jnp.mean(x, axis=axis, keepdims=True)
    v = jnp.var(x, axis=axis, keepdims=True)
    return (x - m) / jnp.sqrt(v + eps)

def _scatter_add(tgt, idx, src, axis=0):
    return tgt.at[idx].add(src)

def _segment_sum(src, seg, n):
    return jax.ops.segment_sum(src, seg, n)
kernel_name = 'mk_prb_d1_jaxref_r4_6aeeba'

def setup_inputs(seed: int=0):
    np.random.seed(seed)
    _w = jnp.asarray

    def _L0_attn_setup():
        import jax, jax.numpy as jnp
        import numpy as np
        D_MODEL, D_K, D_V, H = (256, 64, 64, 16)
        B, N = (2, 512)
        key = jax.random.key(seed)
        ks = jax.random.split(key, 5)
        y = jax.random.normal(ks[0], (B, N, D_MODEL), dtype=jnp.float32)
        Wq = 0.001 * jax.random.normal(ks[1], (H * D_K, D_MODEL), dtype=jnp.float32)
        Wk = 0.001 * jax.random.normal(ks[2], (H * D_K, D_MODEL), dtype=jnp.float32)
        Wv = 0.001 * jax.random.normal(ks[3], (H * D_V, D_MODEL), dtype=jnp.float32)
        Wo = 0.001 * jax.random.normal(ks[4], (D_MODEL, H * D_V), dtype=jnp.float32)
        bq = jnp.zeros((H * D_K,), jnp.float32)
        bk = jnp.zeros((H * D_K,), jnp.float32)
        bv = jnp.zeros((H * D_V,), jnp.float32)
        bo = jnp.zeros((D_MODEL,), jnp.float32)
        return {'y': y, 'Wq': Wq, 'bq': bq, 'Wk': Wk, 'bk': bk, 'Wv': Wv, 'bv': bv, 'Wo': Wo, 'bo': bo}
    _L0_attn_in = _L0_attn_setup()

    def _L0_ffn_setup():
        import jax, jax.numpy as jnp
        import numpy as np
        B, S, D = (1, 512, 256)
        E, K, F = (64, 8, 192)
        SF = 192
        C = 128
        ROUTED_SCALE = 1.0

        def _moe_forward(x, router_w, w_gate, w_up, w_down, ws_gate_up, ws_down):
            T = x.shape[0]
            logits = x.astype(jnp.float32) @ router_w.T
            probs = jax.nn.softmax(logits, axis=-1)
            topk_w, topk_ids = jax.lax.top_k(probs, K)
            topk_w = topk_w / jnp.sum(topk_w, axis=-1, keepdims=True)
            topk_w = topk_w.astype(x.dtype)
            N = T * K
            flat_e = topk_ids.reshape(-1)
            flat_w = topk_w.reshape(-1)
            tok = jnp.arange(N) // K
            onehot = flat_e[:, None] == jnp.arange(E)[None, :]
            pos = jnp.cumsum(onehot, axis=0)[jnp.arange(N), flat_e] - 1
            valid = pos < C
            idx = jnp.where(valid, flat_e * C + pos, E * C)
            x_buf = jnp.zeros((E * C + 1, x.shape[1]), x.dtype).at[idx].set(x[tok])
            xb = x_buf[:E * C].reshape(E, C, -1)
            g = jnp.einsum('ecd,edf->ecf', xb, w_gate)
            u = jnp.einsum('ecd,edf->ecf', xb, w_up)
            h = jax.nn.silu(g) * u
            y = jnp.einsum('ecf,efd->ecd', h, w_down).reshape(E * C, -1)
            safe = jnp.where(valid, idx, 0)
            contrib = y[safe] * (flat_w * valid.astype(flat_w.dtype))[:, None]
            routed = jax.ops.segment_sum(contrib, tok, num_segments=T)
            routed = routed * ROUTED_SCALE
            gu = x @ ws_gate_up
            sg, su = (gu[:, :SF], gu[:, SF:])
            shared = jax.nn.silu(sg) * su @ ws_down
            return routed + shared
        key = jax.random.key(seed)
        ks = jax.random.split(key, 7)
        w = 0.02
        return {'hidden_states': jax.random.normal(ks[0], (B, S, D), jnp.float32), 'router_w': jax.random.normal(ks[1], (E, D), jnp.float32) * w, 'w_gate': jax.random.normal(ks[2], (E, D, F), jnp.float32) * w, 'w_up': jax.random.normal(ks[3], (E, D, F), jnp.float32) * w, 'w_down': jax.random.normal(ks[4], (E, F, D), jnp.float32) * w, 'ws_gate_up': jax.random.normal(ks[5], (D, 2 * SF), jnp.float32) * w, 'ws_down': jax.random.normal(ks[6], (SF, D), jnp.float32) * w}
    _L0_ffn_in = _L0_ffn_setup()
    _d = {'L0_attn_y': _L0_attn_in['y'], 'L0_attn_Wq': _L0_attn_in['Wq'], 'L0_attn_bq': _L0_attn_in['bq'], 'L0_attn_Wk': _L0_attn_in['Wk'], 'L0_attn_bk': _L0_attn_in['bk'], 'L0_attn_Wv': _L0_attn_in['Wv'], 'L0_attn_bv': _L0_attn_in['bv'], 'L0_attn_Wo': _L0_attn_in['Wo'], 'L0_attn_bo': _L0_attn_in['bo'], 'L0_ffn_router_w': _L0_ffn_in['router_w'], 'L0_ffn_w_gate': _L0_ffn_in['w_gate'], 'L0_ffn_w_up': _L0_ffn_in['w_up'], 'L0_ffn_w_down': _L0_ffn_in['w_down'], 'L0_ffn_ws_gate_up': _L0_ffn_in['ws_gate_up'], 'L0_ffn_ws_down': _L0_ffn_in['ws_down']}
    _x0 = _d['L0_attn_y']
    _d['L0_attn_y'] = jax.random.normal(jax.random.fold_in(jax.random.key(seed), 1), (8, 1024, 256), dtype=_x0.dtype)
    del _x0
    return _d

def reference(L0_attn_y, L0_attn_Wq, L0_attn_bq, L0_attn_Wk, L0_attn_bk, L0_attn_Wv, L0_attn_bv, L0_attn_Wo, L0_attn_bo, L0_ffn_router_w, L0_ffn_w_gate, L0_ffn_w_up, L0_ffn_w_down, L0_ffn_ws_gate_up, L0_ffn_ws_down):

    def _L0_attn_ref(y, Wq, bq, Wk, bk, Wv, bv, Wo, bo):
        import jax, jax.numpy as jnp
        import numpy as np
        D_MODEL, D_K, D_V, H = (256, 64, 64, 16)
        B, N = (2, 512)
        b_s, n, _ = y.shape
        scale = 1.0 / np.sqrt(D_K).astype(np.float32)
        q = (jnp.einsum('bnd,ed->bne', y, Wq) + bq).reshape(b_s, n, H, D_K).transpose(0, 2, 1, 3)
        k = (jnp.einsum('bnd,ed->bne', y, Wk) + bk).reshape(b_s, n, H, D_K).transpose(0, 2, 1, 3)
        v = (jnp.einsum('bnd,ed->bne', y, Wv) + bv).reshape(b_s, n, H, D_V).transpose(0, 2, 1, 3)
        att = jnp.einsum('bhqd,bhkd->bhqk', q, k) * scale
        att = jax.nn.softmax(att, axis=-1)
        out = jnp.einsum('bhqk,bhkd->bhqd', att, v)
        out = out.transpose(0, 2, 1, 3).reshape(b_s, n, H * D_V)
        out = jnp.einsum('bne,de->bnd', out, Wo) + bo
        return out

    def _L0_ffn_ref(hidden_states, router_w, w_gate, w_up, w_down, ws_gate_up, ws_down):
        import jax, jax.numpy as jnp
        import numpy as np
        B, S, D = (1, 512, 256)
        E, K, F = (64, 8, 192)
        SF = 192
        C = 128
        ROUTED_SCALE = 1.0

        def _moe_forward(x, router_w, w_gate, w_up, w_down, ws_gate_up, ws_down):
            T = x.shape[0]
            logits = x.astype(jnp.float32) @ router_w.T
            probs = jax.nn.softmax(logits, axis=-1)
            topk_w, topk_ids = jax.lax.top_k(probs, K)
            topk_w = topk_w / jnp.sum(topk_w, axis=-1, keepdims=True)
            topk_w = topk_w.astype(x.dtype)
            N = T * K
            flat_e = topk_ids.reshape(-1)
            flat_w = topk_w.reshape(-1)
            tok = jnp.arange(N) // K
            onehot = flat_e[:, None] == jnp.arange(E)[None, :]
            pos = jnp.cumsum(onehot, axis=0)[jnp.arange(N), flat_e] - 1
            valid = pos < C
            idx = jnp.where(valid, flat_e * C + pos, E * C)
            x_buf = jnp.zeros((E * C + 1, x.shape[1]), x.dtype).at[idx].set(x[tok])
            xb = x_buf[:E * C].reshape(E, C, -1)
            g = jnp.einsum('ecd,edf->ecf', xb, w_gate)
            u = jnp.einsum('ecd,edf->ecf', xb, w_up)
            h = jax.nn.silu(g) * u
            y = jnp.einsum('ecf,efd->ecd', h, w_down).reshape(E * C, -1)
            safe = jnp.where(valid, idx, 0)
            contrib = y[safe] * (flat_w * valid.astype(flat_w.dtype))[:, None]
            routed = jax.ops.segment_sum(contrib, tok, num_segments=T)
            routed = routed * ROUTED_SCALE
            gu = x @ ws_gate_up
            sg, su = (gu[:, :SF], gu[:, SF:])
            shared = jax.nn.silu(sg) * su @ ws_down
            return routed + shared
        b, s, d = hidden_states.shape
        x = hidden_states.reshape(-1, d)
        out = _moe_forward(x, router_w, w_gate, w_up, w_down, ws_gate_up, ws_down)
        return out.reshape(b, s, d)
    x = L0_attn_y
    xn = _layernorm(x, axis=-1)
    x = x + _L0_attn_ref(xn, L0_attn_Wq, L0_attn_bq, L0_attn_Wk, L0_attn_bk, L0_attn_Wv, L0_attn_bv, L0_attn_Wo, L0_attn_bo) + _L0_ffn_ref(xn, L0_ffn_router_w, L0_ffn_w_gate, L0_ffn_w_up, L0_ffn_w_down, L0_ffn_ws_gate_up, L0_ffn_ws_down)
    return x

_drawn_inputs = setup_inputs


def setup_inputs(seed=0):
    import zlib

    import numpy as np

    out = dict(_drawn_inputs(seed))
    spreads = {'L0_attn_bq': (0.0, 2.0),
     'L0_attn_bk': (0.0, 2.0),
     'L0_attn_bv': (0.0, 0.8),
     'L0_attn_bo': (0.0, 0.1)}
    factors = {'L0_attn_Wq': 200.0,
     'L0_attn_Wk': 64.0,
     'L0_attn_Wv': 64.0,
     'L0_attn_Wo': 8.0,
     'L0_ffn_router_w': 8.0,
     'L0_ffn_w_gate': 8.0,
     'L0_ffn_w_up': 8.0,
     'L0_ffn_w_down': 8.0,
     'L0_ffn_ws_gate_up': 3.865,
     'L0_ffn_ws_down': 3.873}
    for name, (base, spread) in spreads.items():
        noise = np.random.default_rng([zlib.crc32(name.encode()), seed]).standard_normal(out[name].shape)
        drawn = base * np.exp(spread * noise) if base else spread * noise
        out[name] = jnp.asarray(drawn.astype(out[name].dtype))
    for name, factor in factors.items():
        out[name] = (out[name] * factor).astype(out[name].dtype)
    return out
```

```python
from contextlib import ExitStack

import concourse.bass as bass
from concourse import mybir

F32 = mybir.dt.float32
F32R = mybir.dt.float32r
BF16 = mybir.dt.bfloat16
U32 = mybir.dt.uint32
ALU = mybir.AluOpType
ACT = mybir.ActivationFunctionType
AX = mybir.AxisListType.X

P = 128
B, N, D = 8, 1024, 256
T = B * N
H, DK = 16, 64
HD = H * DK
PAIRS = H // 2
NP = B * PAIRS
E, TOPK, F, C = 64, 8, 192, 128
F2 = F - P
KD = D // P
TILES = T // P
KT = N // P
ROW = D + E
EPS = 1e-5
SCALE = float(DK) ** -0.5
HALF = 512

UNIT = 4
UNITS = TILES // UNIT

HIGH, LOW = 0, 1
DMA = 16


def alone(engine, met, *waits):
    waits = [(sem, v if isinstance(v, int) else engine.to_reg(v)) for sem, v in waits]
    engine.wait_ge(*met)
    for sem, value in waits:
        engine.wait_ge(sem, value)


def known(v, least):
    return isinstance(v, int) and v < least


def f32(ap):
    return ap.bitcast(F32)


def norm_stage(nc, ctx, io, keep):
    def sb(name, shape, dt=F32):
        return ctx.enter_context(nc.sbuf_tensor(name, shape, dt))

    def sem(name):
        return ctx.enter_context(nc.semaphore(name))

    psum, ident, masks = keep["psum"], keep["ident"], keep["masks"]
    transposed_ps = psum[:, 0:2, :]
    router_ps = psum[:, 2, 0:UNIT * E]
    gate_ps, up_ps, down_ps = psum[:, 3, :], psum[:, 4, :], psum[:, 5, :]

    x_in = sb("x_in", [P, 2, UNIT, D])
    normed = sb("normed", [P, 2, UNIT, D])
    xt32 = sb("xt32", [P, 2, KD, HALF])
    xt_high = sb("xt_high", [P, 2, KD, HALF], F32R)
    xt_low = sb("xt_low", [P, 2, KD, HALF], F32R)
    values = sb("values", [P, 2, UNIT, HD])
    wv32 = sb("wv32", [P, KD, HD])
    wv = sb("wv", [P, 2, KD, HD], F32R)
    wqk = sb("wqk", [P, 2, KD, HD], F32R)
    router = sb("router", [P, KD, E])
    ws_gu = sb("ws_gu", [P, KD, 2 * F])
    ws_d0 = sb("ws_d0", [P, D])
    ws_d1 = sb("ws_d1", [F2, D])
    stats = sb("stats", [P, UNIT, 6])
    meanvar = sb("meanvar", [P, UNIT, 2])
    var_eps = sb("var_eps", [P, UNIT])
    minus_half = sb("minus_half", [P, UNIT])
    rstd0 = sb("rstd0", [P, UNIT])
    newton = sb("newton", [P, UNIT])
    rstd = sb("rstd", [P, UNIT])
    row4 = sb("row4", [P, UNIT])
    logit = sb("logit", [P, UNIT, E])
    prob_e = sb("prob_e", [P, UNIT, E])
    prob = sb("prob", [P, UNIT, E])
    top = sb("top", [P, UNIT, TOPK])
    replaced = sb("replaced", [P, UNIT, E])
    chosen = sb("chosen", [P, UNIT, E])
    weight = sb("weight", [P, 2, UNIT, E])
    exp_g = sb("exp_g", [P, HALF])
    silu = sb("silu", [P, HALF])
    hidden0 = sb("hidden0", [P, HALF])
    hidden1 = sb("hidden1", [F2, HALF])
    shared = sb("shared", [P, 2, UNIT, D])
    zeros = sb("zeros", [P, ROW])

    weights_in = sem("weights_in")
    wv_in = sem("wv_in")
    w_high = sem("w_high")
    w_low = sem("w_low")
    w_stored = sem("w_stored")
    ready = sem("ready")
    zeros_set = sem("zeros_set")
    x_loaded = sem("x_loaded")
    normed_ready = sem("normed_ready")
    var_ready = sem("var_ready")
    pow_ready = sem("pow_ready")
    vec = sem("vec")
    xt_filled = sem("xt_filled")
    xt_highs = sem("xt_highs")
    xt_lows = sem("xt_lows")
    router_filled = sem("router_filled")
    logits_ready = sem("logits_ready")
    exp_ready = sem("exp_ready")
    weight_ready = sem("weight_ready")
    gu_filled = sem("gu_filled")
    exp_g_ready = sem("exp_g_ready")
    hidden_ready = sem("hidden_ready")
    down_filled = sem("down_filled")
    shared_ready = sem("shared_ready")
    v_filled = sem("v_filled")
    v_copied = sem("v_copied")
    normed_stored = sem("normed_stored")
    xt_stored = sem("xt_stored")
    weight_stored = sem("weight_stored")
    v_stored = sem("v_stored")
    shared_stored = sem("shared_stored")
    pads_stored = sem("pads_stored")

    x_v = io["x"].rearrange("(u t p) d -> u p t d", p=P, t=UNIT)
    rows_v = io["rows"][0:T, :].rearrange("(u t p) d -> u p t d", p=P, t=UNIT)
    moe_v = io["moe"][0:T, :].rearrange("(u t p) d -> u p t d", p=P, t=UNIT)

    block = ctx.enter_context(nc.Block())

    @block.sync
    def _(sp):
        for n, w in enumerate(("wv", "wq", "wk")):
            if n:
                sp.wait_ge(w_low, n)
            sp.dma_start(wv32[:], io[w].rearrange("(k p) e -> p k e", p=P)).then_inc(wv_in, DMA)
            if n == 0:
                sp.dma_start(x_in[:, 0], x_v[0]).then_inc(x_loaded, DMA)
                sp.dma_start(router[:], io["router"].rearrange("(k p) e -> p k e", p=P)).then_inc(weights_in, DMA)
                sp.dma_start(ws_gu[:], io["ws_gu"].rearrange("(k p) e -> p k e", p=P)).then_inc(weights_in, DMA)
                sp.dma_start(ws_d0[:], io["ws_d"][0:P, :]).then_inc(weights_in, DMA)
                sp.dma_start(ws_d1[:], io["ws_d"][P:F, :]).then_inc(weights_in, DMA)
            else:
                sp.wait_ge(w_high, n + 1)
                sp.wait_ge(w_low, n + 1)
                for part in range(2):
                    for k in range(KD):
                        sp.dma_start(io["wqk"][:, :, n - 1, part, k, :].rearrange("h p c -> p h c"),
                                     f32(wqk[:, part, k, :]).rearrange("p (h c) -> p h c", c=P)
                                     ).then_inc(w_stored, DMA)
        sp.wait_ge(zeros_set, 1)
        sp.dma_start(io["rows"][T:T + C, :], zeros[:]).then_inc(pads_stored, DMA)
        sp.dma_start(io["moe"][T:T + C, :], zeros[:, 0:D]).then_inc(pads_stored, DMA)

        def unit(i, par, more):
            u = i * 2 + par
            if more:
                if not (isinstance(u, int) and u == 0):
                    sp.wait_ge(normed_ready, u)
                sp.dma_start(x_in[:, 1 - par], x_v[bass.ds(u + 1, 1)].rearrange("o p t d -> (o p) t d")
                             ).then_inc(x_loaded, DMA)
            one = bass.ds(u, 1)
            sp.wait_ge(normed_ready, u + 1)
            sp.dma_start(rows_v[one, :, :, 0:D].rearrange("o p t d -> (o p) t d"), normed[:, par]
                         ).then_inc(normed_stored, DMA)
            sp.wait_ge(xt_lows, u + 1)
            for part, tile in ((HIGH, xt_high), (LOW, xt_low)):
                for k in range(KD):
                    sp.dma_start(io["xt"][bass.ds(i, 1), :, part, k, par * HALF:(par + 1) * HALF]
                                 .rearrange("o p c -> (o p) c"), f32(tile[:, par, k, :])).then_inc(xt_stored, DMA)
            sp.wait_ge(weight_ready, u + 1)
            sp.dma_start(rows_v[one, :, :, D:ROW].rearrange("o p t d -> (o p) t d"), weight[:, par]
                         ).then_inc(weight_stored, DMA)
            for t in range(UNIT):
                sp.wait_ge(v_copied, (u * UNIT + t) * 2 + 2)
                sp.dma_start(io["v"][bass.ds(i * PAIRS, PAIRS), :, par * UNIT + t, :].rearrange("h p c -> p h c"),
                             values[:, par, t, :].rearrange("p (h c) -> p h c", c=P)).then_inc(v_stored, DMA)
            sp.wait_ge(shared_ready, 2 * u + 2)
            sp.dma_start(moe_v[one].rearrange("o p t d -> (o p) t d"), shared[:, par]).then_inc(shared_stored, DMA)

        unit(0, 0, True)
        unit(0, 1, True)
        with sp.Fori(1, UNITS // 2 - 1) as i:
            unit(i, 0, True)
            unit(i, 1, True)
        unit(UNITS // 2 - 1, 0, True)
        unit(UNITS // 2 - 1, 1, False)
        sp.wait_ge(w_stored, DMA * 8)
        sp.wait_ge(pads_stored, DMA * 2)
        sp.wait_ge(normed_stored, DMA * UNITS)
        sp.wait_ge(xt_stored, DMA * 4 * UNITS)
        sp.wait_ge(weight_stored, DMA * UNITS)
        sp.wait_ge(v_stored, DMA * UNIT * UNITS)
        sp.wait_ge(shared_stored, DMA * UNITS)

    @block.gpsimd
    def _(pool):
        nc.gpsimd.memset(zeros[:], 0.0).then_inc(zeros_set, 1)
        nc.gpsimd.memset(minus_half[:], -0.5).then_inc(ready, 1)
        nc.gpsimd.memset(ident[:], 0.0).then_inc(ready, 1)
        pool.wait_ge(ready, 2)
        nc.gpsimd.affine_select(out=ident[:], in_=ident[:], compare_op=ALU.not_equal, fill=1.0, base=0,
                                pattern=[[-1, P]], channel_multiplier=1).then_inc(ready, 1)
        with pool.Fori(0, UNITS) as u:
            pool.wait_ge(var_ready, u + 1)
            nc.gpsimd.tensor_tensor(rstd0[:], var_eps[:], minus_half[:], ALU.pow).then_inc(pow_ready, 1)

    @block.scalar
    def _(act):
        for n in range(3):
            act.wait_ge(wv_in, DMA * (n + 1))
            if n == 2:
                act.wait_ge(w_stored, DMA * 4)
            nc.scalar.copy((wv if n == 0 else wqk)[:, HIGH], wv32[:]).then_inc(w_high, 1)

        def unit(i, par):
            u = i * 2 + par
            first = isinstance(u, int) and u < 2

            def values_out(lo, hi):
                for n in range(lo, hi):
                    act.wait_ge(v_filled, 8 * u + n + 1)
                    if n == 0 and not first:
                        act.wait_ge(v_stored, DMA * UNIT * (u - 1))
                    nc.scalar.copy(values[:, par, n // 2, (n % 2) * HALF:(n % 2 + 1) * HALF],
                                   psum[:, 6 + n % 2, :]).then_inc(v_copied, 1)

            act.wait_ge(xt_filled, u + 1)
            if not first:
                act.wait_ge(xt_stored, DMA * 4 * (u - 1))
                act.wait_ge(down_filled, 2 * (u - 1))
            nc.scalar.copy(xt_high[:, par], transposed_ps)
            nc.scalar.copy(xt32[:, par], transposed_ps).then_inc(xt_highs, 1)
            act.wait_ge(logits_ready, u + 1)
            nc.scalar.activation(prob_e[:], logit[:], ACT.Exp).then_inc(exp_ready, 1)
            for c, rows in ((0, P), (1, F2)):
                act.wait_ge(gu_filled, 2 * u + c + 1)
                if c or not (isinstance(u, int) and u == 0):
                    act.wait_ge(hidden_ready, 2 * u + c)
                nc.scalar.activation(exp_g[0:rows, :], gate_ps[0:rows, :], ACT.Exp, scale=-1.0
                                     ).then_inc(exp_g_ready, 1)
                values_out(4 * c, 4 * c + 4)

        unit(0, 0)
        unit(0, 1)
        with act.Fori(1, UNITS // 2) as i:
            unit(i, 0)
            unit(i, 1)

    @block.vector
    def _(dve):
        NORM_LINKS, VEC = 7, 23
        for n in range(3):
            part = wv if n == 0 else wqk
            dve.wait_ge(w_high, n + 1)
            nc.vector.tensor_tensor(part[:, LOW], wv32[:], f32(part[:, HIGH]), ALU.subtract).then_inc(w_low, 1)

        def linked(start, count):
            def link(ins, standing=False):
                count[0] += 1
                ins.then_inc(vec, 1)
                if standing:
                    alone(dve, (x_loaded, DMA), (vec, start + count[0]))
                else:
                    dve.wait_ge(vec, start + count[0])
            return link

        def norm(v, par, link):
            first = isinstance(v, int) and v < 2
            dve.wait_ge(x_loaded, DMA * (v + 1))
            for t in range(UNIT):
                last = nc.vector.bn_stats(out=stats[:, t, :], in_=x_in[:, par, t, :])
            link(last, True)
            for t in range(UNIT):
                last = nc.vector.bn_aggr(out=meanvar[:, t, :], in_=stats[:, t, :])
            link(last)
            link(nc.vector.tensor_scalar(var_eps[:], meanvar[:, :, 1], EPS, None, ALU.add))
            nc.vector.tensor_copy(row4[:], var_eps[:]).then_inc(var_ready, 1)
            dve.wait_ge(pow_ready, v + 1)
            link(nc.vector.tensor_tensor(newton[:], rstd0[:], rstd0[:], ALU.mult))
            link(nc.vector.tensor_tensor(newton[:], newton[:], var_eps[:], ALU.mult))
            link(nc.vector.tensor_scalar(newton[:], newton[:], -0.5, 1.5, ALU.mult, ALU.add))
            link(nc.vector.tensor_tensor(rstd[:], newton[:], rstd0[:], ALU.mult))
            if not first:
                dve.wait_ge(normed_stored, DMA * (v - 1))
                dve.wait_ge(xt_filled, v - 1)
            for t in range(UNIT):
                last = nc.vector.tensor_scalar(normed[:, par, t, :], x_in[:, par, t, :], meanvar[:, t, 0:1],
                                               rstd[:, t:t + 1], ALU.subtract, ALU.mult)
            last.then_inc(normed_ready, 1)

        def unit(i, par, more):
            u = i * 2 + par
            first = isinstance(u, int) and u < 2
            count = [0]
            link = linked(u * VEC + NORM_LINKS, count)
            dve.wait_ge(xt_highs, u + 1)
            if not first:
                dve.wait_ge(xt_stored, DMA * 4 * (u - 1))
            nc.vector.tensor_tensor(xt_low[:, par], transposed_ps, f32(xt_high[:, par]), ALU.subtract
                                    ).then_inc(xt_lows, 1)
            dve.wait_ge(router_filled, u + 1)
            scores = router_ps.rearrange("p (t e) -> p t e", e=E)
            wide = [P, UNIT, E]
            link(nc.vector.tensor_reduce(out=row4[:], in_=scores, axis=AX, op=ALU.max))
            nc.vector.tensor_tensor(logit[:], scores, row4[:].rearrange("p (t o) -> p t o", o=1).to_broadcast(wide),
                                    ALU.subtract).then_inc(logits_ready, 1)
            dve.wait_ge(exp_ready, u + 1)
            link(nc.vector.tensor_reduce(out=row4[:], in_=prob_e[:], axis=AX, op=ALU.add))
            link(nc.vector.reciprocal(row4[:], row4[:]))
            link(nc.vector.tensor_tensor(prob[:], prob_e[:],
                                         row4[:].rearrange("p (t o) -> p t o", o=1).to_broadcast(wide), ALU.mult), True)
            for t in range(UNIT):
                last = nc.vector.max(out=top[:, t, :], in_=prob[:, t, :])
            link(last, True)
            for t in range(UNIT):
                last = nc.vector.match_replace(out=replaced[:, t, :], in_to_replace=top[:, t, :],
                                               in_values=prob[:, t, :], imm_value=-1.0)
            link(last)
            link(nc.vector.tensor_tensor(chosen[:], prob[:], replaced[:], ALU.not_equal))
            nc.vector.tensor_copy(masks[:, bass.ds(u * UNIT, UNIT), :], chosen[:])
            link(nc.vector.tensor_tensor(prob[:], prob[:], chosen[:], ALU.mult))
            link(nc.vector.tensor_reduce(out=row4[:], in_=prob[:], axis=AX, op=ALU.add))
            link(nc.vector.reciprocal(row4[:], row4[:]))
            if not first:
                dve.wait_ge(weight_stored, DMA * (u - 1))
            nc.vector.tensor_tensor(weight[:, par], prob[:], row4[:].rearrange("p (t o) -> p t o", o=1)
                                    .to_broadcast(wide), ALU.mult).then_inc(weight_ready, 1)
            if more:
                norm(u + 1, 1 - par, link)
            for c, (rows, hidden) in enumerate(((P, hidden0), (F2, hidden1))):
                dve.wait_ge(exp_g_ready, 2 * u + c + 1)
                link(nc.vector.tensor_scalar(silu[0:rows, :], exp_g[0:rows, :], 1.0, None, ALU.add))
                link(nc.vector.reciprocal(silu[0:rows, :], silu[0:rows, :]))
                link(nc.vector.tensor_tensor(silu[0:rows, :], gate_ps[0:rows, :], silu[0:rows, :], ALU.mult))
                if not (isinstance(u, int) and u == 0):
                    dve.wait_ge(down_filled, 2 * u)
                nc.vector.tensor_tensor(hidden[:], up_ps[0:rows, :], silu[0:rows, :], ALU.mult
                                        ).then_inc(hidden_ready, 1)
            if not first:
                dve.wait_ge(shared_stored, DMA * (u - 1))
            for n in range(2):
                dve.wait_ge(down_filled, 2 * u + n + 1)
                nc.vector.tensor_copy(shared[:, par, 2 * n:2 * n + 2, :],
                                      down_ps.rearrange("p (t d) -> p t d", d=D)).then_inc(shared_ready, 1)
            assert count[0] == VEC or not more, count[0]

        norm(0, 0, linked(0, [0]))
        unit(0, 0, True)
        unit(0, 1, True)
        with dve.Fori(1, UNITS // 2 - 1) as i:
            unit(i, 0, True)
            unit(i, 1, True)
        unit(UNITS // 2 - 1, 0, True)
        unit(UNITS // 2 - 1, 1, False)

    @block.tensor
    def _(pe):
        def transposes(u, par):
            pe.wait_ge(normed_ready, u + 1)
            if not (isinstance(u, int) and u == 0):
                pe.wait_ge(xt_lows, u)
            for k in range(KD):
                for t in range(UNIT):
                    last = nc.tensor.transpose(transposed_ps[:, k, t * P:(t + 1) * P],
                                               normed[:, par, t, k * P:(k + 1) * P], ident[:])
            last.then_inc(xt_filled, 1)

        def values_in(u, par, lo, hi):
            for n in range(lo, hi):
                t, half = n // 2, n % 2
                if not (isinstance(u, int) and u == 0 and n < 2):
                    pe.wait_ge(v_copied, 8 * u + n - 1)
                terms = [(xt_high, HIGH), (xt_high, LOW), (xt_low, HIGH)]
                for j, (tile, part) in enumerate(terms):
                    for k in range(KD):
                        last = nc.tensor.matmul(psum[:, 6 + n % 2, :], tile[:, par, k, t * P:(t + 1) * P],
                                                wv[:, part, k, half * HALF:(half + 1) * HALF],
                                                start=(j == 0 and k == 0), stop=(j == 2 and k == KD - 1))
                last.then_inc(v_filled, 1)

        def gate_up(u, par, c, rows):
            if c or not (isinstance(u, int) and u == 0):
                pe.wait_ge(hidden_ready, 2 * u + c)
            for out, col in ((gate_ps, c * P), (up_ps, F + c * P)):
                for k in range(KD):
                    last = nc.tensor.matmul(out[0:rows, :], ws_gu[:, k, col:col + rows], xt32[:, par, k, :],
                                            start=(k == 0), stop=(k == KD - 1))
            last.then_inc(gu_filled, 1)

        def unit(i, par, more):
            u = i * 2 + par
            pe.wait_ge(xt_highs, u + 1)
            pe.wait_ge(xt_lows, u + 1)
            if not (isinstance(u, int) and u == 0):
                pe.wait_ge(logits_ready, u)
            for t in range(UNIT):
                for k in range(KD):
                    last = nc.tensor.matmul(router_ps[:, t * E:(t + 1) * E], xt32[:, par, k, t * P:(t + 1) * P],
                                            router[:, k, :], start=(k == 0), stop=(k == KD - 1))
            last.then_inc(router_filled, 1)
            gate_up(u, par, 0, P)
            values_in(u, par, 0, 4)
            gate_up(u, par, 1, F2)
            if more:
                transposes(u + 1, 1 - par)
            values_in(u, par, 4, 8)
            pe.wait_ge(hidden_ready, 2 * u + 2)
            for n in range(2):
                if n or not (isinstance(u, int) and u == 0):
                    pe.wait_ge(shared_ready, 2 * u + n)
                for t in range(2):
                    cols = slice((2 * n + t) * P, (2 * n + t + 1) * P)
                    nc.tensor.matmul(down_ps[:, t * D:(t + 1) * D], hidden0[:, cols], ws_d0[:],
                                     start=True, stop=False)
                    last = nc.tensor.matmul(down_ps[:, t * D:(t + 1) * D], hidden1[:, cols], ws_d1[:],
                                            start=False, stop=True)
                last.then_inc(down_filled, 1)

        pe.wait_ge(ready, 3)
        pe.wait_ge(weights_in, DMA * 4)
        transposes(0, 0)
        pe.wait_ge(w_high, 1)
        pe.wait_ge(w_low, 1)
        unit(0, 0, True)
        unit(0, 1, True)
        with pe.Fori(1, UNITS // 2 - 1) as i:
            unit(i, 0, True)
            unit(i, 1, True)
        unit(UNITS // 2 - 1, 0, True)
        unit(UNITS // 2 - 1, 1, False)


def table_stage(nc, ctx, io, keep):
    def sb(name, shape, dt=F32):
        return ctx.enter_context(nc.sbuf_tensor(name, shape, dt))

    def sem(name):
        return ctx.enter_context(nc.semaphore(name))

    psum, masks = keep["psum"], keep["masks"]
    ones = sb("ones_bf", [P, P], BF16)
    upto = sb("upto", [P, P], BF16)
    slot_f = sb("slot_f", [P, 1])
    pad_row = sb("pad_row", [P, 1])
    expert_i = sb("expert_i", [P, E])
    counts = sb("counts", [P, E, TILES])
    carry = sb("carry", [P, E, TILES])
    running = sb("running", [P, E, TILES])
    before = sb("before", [P, E, TILES])
    tile_of = sb("tile_of", [P, E])
    base = sb("base", [P, E])
    rows = sb("rows_sb", [P, TILES // 2, P])
    scratch = sb("scratch_t", [P, E])

    consts = sem("t_consts")
    counted = sem("counted")
    counts_out = sem("counts_out")
    row_filled = sem("row_filled")
    rows_out = sem("rows_out")
    rows_stored = sem("rows_stored")
    tvec = sem("tvec")
    block = ctx.enter_context(nc.Block())

    @block.gpsimd
    def _(pool):
        nc.gpsimd.memset(ones[:], 1.0).then_inc(consts, 1)
        nc.gpsimd.memset(upto[:], 1.0).then_inc(consts, 1)
        nc.gpsimd.memset(carry[:], 1.0).then_inc(consts, 1)
        nc.gpsimd.iota(slot_f[:], pattern=[[1, 1]], base=0, channel_multiplier=1,
                       allow_small_or_imprecise_dtypes=True).then_inc(consts, 1)
        nc.gpsimd.iota(pad_row[:], pattern=[[1, 1]], base=T, channel_multiplier=1,
                       allow_small_or_imprecise_dtypes=True).then_inc(consts, 1)
        nc.gpsimd.iota(expert_i[:], pattern=[[1, E]], base=0, channel_multiplier=0,
                       allow_small_or_imprecise_dtypes=True).then_inc(consts, 1)
        pool.wait_ge(consts, 6)
        nc.gpsimd.affine_select(out=upto[:], in_=upto[:], compare_op=ALU.is_ge, fill=0.0, base=0,
                                pattern=[[1, P]], channel_multiplier=-1).then_inc(consts, 1)
        nc.gpsimd.memset(carry[:, :, 0:1], 0.0).then_inc(consts, 1)

    @block.tensor
    def _(pe):
        pe.wait_ge(consts, 8)
        flat = masks[:].rearrange("p j e -> p (j e)")
        for n in range(8):
            nc.tensor.matmul(psum[:, n, :], ones[:], flat[:, n * HALF:(n + 1) * HALF], start=True, stop=True
                             ).then_inc(counted, 1)
        for n in range(8):
            pe.wait_ge(counts_out, n + 1)
            for g in range(4):
                j = 4 * n + g
                last = nc.tensor.matmul(psum[:, n, g * P:(g + 1) * P], flat[:, j * P:(j + 1) * P], upto[:],
                                        start=True, stop=True)
            last.then_inc(row_filled, 1)

    @block.scalar
    def _(act):
        for n in range(8):
            act.wait_ge(counted, n + 1)
            nc.scalar.copy(counts[:, :, 8 * n:8 * n + 8].rearrange("p e j -> p j e"),
                           psum[:, n, :].rearrange("p (j e) -> p j e", e=E)).then_inc(counts_out, 1)
        for n in range(8):
            act.wait_ge(row_filled, n + 1)
            nc.scalar.copy(rows[:, 4 * n:4 * n + 4, :], psum[:, n, :].rearrange("p (g q) -> p g q", q=P)
                           ).then_inc(rows_out, 1)

    @block.sync
    def _(sp):
        sp.wait_ge(rows_out, 8)
        sp.dma_start(io["counts"].rearrange("(g r) q -> r g q", r=P), rows[:]).then_inc(rows_stored, DMA)
        sp.wait_ge(rows_stored, DMA)

    @block.vector
    def _(dve):
        count = [0]

        def link(ins):
            count[0] += 1
            ins.then_inc(tvec, 1)
            dve.wait_ge(tvec, count[0])

        dve.wait_ge(consts, 8)
        dve.wait_ge(counts_out, 8)
        link(nc.vector.tensor_tensor_scan(running[:].rearrange("p e j -> p (e j)"),
                                          carry[:].rearrange("p e j -> p (e j)"),
                                          counts[:].rearrange("p e j -> p (e j)"), 0.0, ALU.mult, ALU.add))
        link(nc.vector.tensor_scalar(before[:], running[:], slot_f[:, 0:1], None, ALU.is_le))
        link(nc.vector.tensor_reduce(out=tile_of[:], in_=before[:], axis=AX, op=ALU.add))
        link(nc.vector.tensor_tensor(before[:], before[:], counts[:], ALU.mult))
        link(nc.vector.tensor_reduce(out=base[:], in_=before[:], axis=AX, op=ALU.add))
        nc.vector.tensor_scalar(keep["rank"][:], base[:], -1.0, slot_f[:, 0:1], ALU.mult, ALU.add)
        link(nc.vector.tensor_scalar(keep["valid"][:], tile_of[:], float(TILES), None, ALU.is_lt))
        link(nc.vector.tensor_scalar(base[:], tile_of[:], float(P), pad_row[:, 0:1], ALU.mult, ALU.subtract))
        link(nc.vector.tensor_tensor(base[:], base[:], keep["valid"][:], ALU.mult))
        link(nc.vector.tensor_scalar(keep["first"][:], base[:], pad_row[:, 0:1], None, ALU.add))
        link(nc.vector.tensor_scalar(scratch[:], tile_of[:], float(TILES - 1), float(E), ALU.min, ALU.mult))
        link(nc.vector.tensor_tensor(keep["count_row"][:], scratch[:], expert_i[:], ALU.add))


def step_items(fin, att, nxt, prj):
    slots = [[] for _ in range(KT)]
    if att:
        slots[0].append(("XT",))
    if prj:
        slots[1].append(("PJ", 0))
    units = iter([(h, qt) for h in range(2) for qt in range(KT)])
    for slot, n in ((1, 2), (2, 3), (3, 3), (4, 3), (5, 3), (6, 2)):
        if slot == 2 and fin:
            slots[2] += [("SUM", 0), ("SUM", 1)]
        if nxt:
            for _ in range(n):
                h, qt = next(units)
                slots[slot] += [("MAX", h, qt, 0), ("MAX", h, qt, 1)]
        if att and slot in (3, 4, 6):
            slots[slot].append(({3: "GU", 4: "HT", 6: "DN"}[slot],))
        if prj and slot in (3, 5, 6):
            slots[slot].append(("PJ", {3: 1, 5: 2, 6: 3}[slot]))
    if nxt:
        slots[7] += [("MT", 0), ("MT", 1)]
    return slots


def n_items(flags):
    return sum(len(s) for s in step_items(*flags))


FULL = (True, True, True, True)
HEAD = [(-2, (False, False, False, True)), (-1, (False, False, True, True)), (0, (False, True, True, True))]
LOOP0, LOOP1 = 1, NP - 3
TAIL = [(NP - 3, FULL), (NP - 2, (True, True, True, False)), (NP - 1, (True, True, False, False)),
        (NP, (True, False, False, False))]
ITEMS = n_items(FULL)
assert ITEMS % 2 == 0 and (LOOP1 - LOOP0) % 2 == 0


def schedule():
    base, at = {}, 0
    for s, flags in HEAD:
        base[s] = at
        at += n_items(flags)
    loop = at
    at += ITEMS * (LOOP1 - LOOP0)
    for s, flags in TAIL:
        base[s] = at
        at += n_items(flags)
    assert loop % 2 == 0
    return base, loop


BASE, LOOP_BASE = schedule()


def run_steps(engine, step):
    for s, flags in HEAD:
        step(s, s % 2, flags, BASE[s])
    with engine.Fori(0, (LOOP1 - LOOP0) // 2) as i:
        for k in range(2):
            step(i * 2 + LOOP0 + k, (LOOP0 + k) % 2, FULL, i * (2 * ITEMS) + LOOP_BASE + k * ITEMS)
    for s, flags in TAIL:
        step(s, s % 2, flags, BASE[s])


def item_at(flags, item):
    flat = [it for slot in step_items(*flags) for it in slot]
    return flat.index(item)


def attention_stage(nc, ctx, io, keep):
    def sb(name, shape, dt=F32):
        return ctx.enter_context(nc.sbuf_tensor(name, shape, dt))

    def sem(name):
        return ctx.enter_context(nc.semaphore(name))

    psum, ident = keep["psum"], keep["ident"]
    scores_ps = psum[:, 0:4, :].rearrange("p (h b) c -> p h (b c)", h=2)
    out_ps = psum[:, 4:6, :].rearrange("p b c -> p (b c)")
    work = [psum[:, 6, :], psum[:, 7, :]]

    q_full = sb("q_full", [P, 2, 2, N], F32R)
    q_rest = sb("q_rest", [DK + 1, 2, 2, N], F32R)
    k_full = sb("k_full", [P, 2, 2, N], F32R)
    k_rest = sb("k_rest", [DK + 1, 2, 2, N], F32R)
    high = sb("high", [P, 2, 2, N], F32R)
    low = sb("low", [P, 2, 2, N], F32R)
    x_t = sb("x_t", [P, 2, KD, N], F32R)
    w_qk = sb("w_qk", [P, 2, 2, 2, KD, P], F32R)
    bias = sb("bias", [P, 2, 2])
    v_sb = sb("v_sb", [P, 2, KT, P])
    probs = sb("probs", [P, 2, 2, N])
    sums = sb("sums", [P, 2, 2, N])
    out_raw = sb("out_raw", [P, N])
    recip = sb("recip", [P, N])
    out_t = sb("out_t", [P, N])
    ones = sb("ones", [P, DK])
    maxima = sb("maxima", [P, 2 * KT, 2])
    merged = sb("merged", [P, 2 * KT])
    minus_max = sb("minus_max", [KT, 2, P], F32R)
    w_gu = sb("w_gu", [P, 2, KD, 2 * F])
    w_d0 = sb("w_d0", [P, 2, D])
    w_d1 = sb("w_d1", [F2, 2, D])
    count_slot = sb("count_slot", [P, 1], U32)
    count_rows = sb("count_rows", [P, P])
    is_before = sb("is_before", [P, P])
    n_before = sb("n_before", [P, 1])
    token = sb("token", [P, 2], U32)
    x_e = sb("x_e", [P, 2, ROW])
    x_et = sb("x_et", [P, KD, P])
    exp_g = sb("exp_ge", [P, F])
    silu = sb("silu_e", [P, F])
    hidden = sb("hidden_e", [P, F])
    hidden_t0 = sb("hidden_t0", [P, P])
    hidden_t1 = sb("hidden_t1", [F2, P])
    y_e = sb("y_e", [P, 2, D])

    set_up = sem("set_up")
    standing = sem("standing")
    x_loaded = sem("xt_loaded")
    w_loaded = sem("w_loaded")
    v_loaded = sem("v_loaded")
    highs_ready = sem("highs_ready")
    placed = sem("placed")
    shift_placed = sem("shift_placed")
    scores_ready = sem("scores_ready")
    probs_ready = sem("probs_ready")
    pv_done = sem("pv_done")
    out_copied = sem("out_copied")
    sums_added = sem("sums_added")
    out_ready = sem("out_ready")
    out_stored = sem("out_stored")
    work_filled = sem("work_filled")
    work_emptied = sem("work_emptied")
    maxima_merged = sem("maxima_merged")
    experts_loaded = sem("experts_loaded")
    slot_copied = sem("slot_copied")
    counts_loaded = sem("counts_loaded")
    tokens_vec = sem("tokens_vec")
    tokens_ready = sem("tokens_ready")
    tokens_loaded = sem("tokens_loaded")
    exp_g_ready = sem("exp_ge_ready")
    silu_vec = sem("silu_vec")
    scattered = sem("scattered")

    block = ctx.enter_context(nc.Block())
    SHUFFLES = 12

    @block.tensor
    def _(pe):
        pe.wait_ge(set_up, 3)

        def score(s, par, kt, h):
            n = 16 * s + 2 * kt + h
            if kt == 0 and h == 0:
                pe.wait_ge(placed, DMA * SHUFFLES * (s + 1))
                pe.wait_ge(shift_placed, DMA * 2 * (s + 1))
            if not known(n, 2):
                pe.wait_ge(probs_ready, n - 1)
            keys = slice(kt * P, (kt + 1) * P)
            for k, q, rows in ((k_full, q_full, P), (k_rest, q_rest, DK + 1)):
                for half in range(2):
                    cols = slice(half * HALF, (half + 1) * HALF)
                    last = nc.tensor.matmul(scores_ps[:, h, cols], k[0:rows, par, h, keys], q[0:rows, par, h, cols],
                                            start=(rows == P), stop=(rows != P))
            last.then_inc(scores_ready, 1)

        def pv(p, par, kt):
            pe.wait_ge(probs_ready, 16 * p + 2 * kt + 2)
            if kt == 0:
                pe.wait_ge(v_loaded, DMA * (p + 1))
                if not known(p, 1):
                    pe.wait_ge(out_copied, p)
            for half in range(2):
                cols = slice(half * HALF, (half + 1) * HALF)
                for h in range(2):
                    rows = slice(DK * h, DK * (h + 1))
                    last = nc.tensor.matmul(out_ps[rows, cols], v_sb[:, par, kt, rows], probs[:, h, kt % 2, cols],
                                            start=(kt == 0), stop=(kt == KT - 1))
            last.then_inc(pv_done, 1)

        def item(s, par, flags, base, k, what):
            out = work[k % 2]
            kind = what[0]
            if not known(base + k, 2):
                pe.wait_ge(work_emptied, base + k - 1)
            if kind == "PJ":
                which, half = what[1] // 2, what[1] % 2
                cols = slice(half * HALF, (half + 1) * HALF)
                if what[1] == 0:
                    pe.wait_ge(x_loaded, DMA * (s + 3))
                    pe.wait_ge(w_loaded, 2 * DMA * (s + 3))
                terms = [(HIGH, HIGH), (LOW, HIGH), (HIGH, LOW)]
                for j, (wp, xp) in enumerate(terms):
                    for kd in range(KD):
                        last = nc.tensor.matmul(out, w_qk[:, par, which, wp, kd, :], x_t[:, xp, kd, cols],
                                                start=(j == 0 and kd == 0), stop=(j == 2 and kd == KD - 1))
            elif kind == "MAX":
                _, h, qt, half = what
                rows = slice(DK * h, DK * (h + 1))
                if (h, qt, half) == (0, 0, 0):
                    pe.wait_ge(highs_ready, 4 * (s + 2))
                last = nc.tensor.matmul(out, high[rows, 1 - par, 0, qt * P:(qt + 1) * P],
                                        high[rows, 1 - par, 1, half * HALF:(half + 1) * HALF], start=True, stop=True)
            elif kind == "MT":
                pe.wait_ge(maxima_merged, s + 2)
                h = what[1]
                last = nc.tensor.matmul(out[0:KT, 0:P], merged[:, h * KT:(h + 1) * KT], ident[:],
                                        start=True, stop=True)
            elif kind == "SUM":
                cols = slice(what[1] * HALF, (what[1] + 1) * HALF)
                if what[1] == 0:
                    pe.wait_ge(sums_added, 14 * s)
                for h in range(2):
                    last = nc.tensor.matmul(out[DK * h:DK * (h + 1), :], ones[:], sums[:, 1 - par, h, cols],
                                            start=True, stop=True)
            elif kind == "XT":
                pe.wait_ge(tokens_loaded, DMA * (s + 1))
                for kd in range(KD):
                    last = nc.tensor.transpose(out[:, kd * P:(kd + 1) * P], x_e[:, par, kd * P:(kd + 1) * P], ident[:])
            elif kind == "GU":
                pe.wait_ge(experts_loaded, 4 * DMA * (s + 1))
                pe.wait_ge(work_emptied, base + item_at(flags, ("XT",)) + 1)
                for kd in range(KD):
                    last = nc.tensor.matmul(out[:, 0:2 * F], x_et[:, kd, :], w_gu[:, par, kd, :],
                                            start=(kd == 0), stop=(kd == KD - 1))
            elif kind == "HT":
                pe.wait_ge(work_emptied, base + item_at(flags, ("GU",)) + 1)
                nc.tensor.matmul(out[:, 0:P], hidden[:, 0:P], ident[:], start=True, stop=True)
                last = nc.tensor.matmul(out[0:F2, P:2 * P], hidden[:, P:F], ident[:], start=True, stop=True)
            elif kind == "DN":
                pe.wait_ge(work_emptied, base + item_at(flags, ("HT",)) + 1)
                nc.tensor.matmul(out[:, 0:D], hidden_t0[:], w_d0[:, par, :], start=True, stop=False)
                last = nc.tensor.matmul(out[:, 0:D], hidden_t1[:], w_d1[:, par, :], start=False, stop=True)
            last.then_inc(work_filled, 1)

        def step(s, par, flags, base):
            fin, att, nxt, prj = flags
            k = 0
            for kt, items in enumerate(step_items(*flags)):
                if att:
                    score(s, par, kt, 0)
                    score(s, par, kt, 1)
                for what in items:
                    item(s, par, flags, base, k, what)
                    k += 1
                if kt == 0 and fin:
                    pv(s - 1, 1 - par, KT - 1)
                if kt > 0 and att:
                    pv(s, par, kt - 1)

        run_steps(pe, step)

    @block.scalar
    def _(act):
        def step(s, par, flags, base):
            fin, att, nxt, prj = flags
            k = 0
            for kt, items in enumerate(step_items(*flags)):
                for h in range(2) if att else ():
                    n = 16 * s + 2 * kt + h
                    act.wait_ge(scores_ready, n + 1)
                    if not (isinstance(s, int) and s == 0 and kt < 2):
                        act.wait_ge(pv_done, 8 * s + kt - 1)
                        added = 14 * s + (2 * (kt - 3) + h if kt >= 3 else h if kt == 2 else
                                          2 * (kt + 5) + h - 14)
                        act.wait_ge(sums_added, added + 1)
                    nc.scalar.activation(probs[:, h, kt % 2, :], scores_ps[:, h, :], ACT.Exp, scale=SCALE
                                         ).then_inc(probs_ready, 1)
                for what in items:
                    if what[0] == "PJ":
                        which, half = what[1] // 2, what[1] % 2
                        act.wait_ge(work_filled, base + k + 1)
                        if what[1] == 0 and not known(s, 0):
                            act.wait_ge(placed, DMA * SHUFFLES * (s + 1))
                        nc.scalar.activation(high[:, par, which, half * HALF:(half + 1) * HALF], work[k % 2],
                                             ACT.Identity, bias=bias[:, par, which:which + 1]
                                             ).then_inc(highs_ready, 1)
                    if what[0] == "GU":
                        act.wait_ge(work_filled, base + k + 1)
                        nc.scalar.activation(exp_g[:], work[k % 2][:, 0:F], ACT.Exp, scale=-1.0
                                             ).then_inc(exp_g_ready, 1)
                    k += 1
                if kt == 0 and fin:
                    act.wait_ge(pv_done, 8 * s)
                    if not known(s, 2):
                        act.wait_ge(out_ready, s - 1)
                    nc.scalar.copy(out_raw[:], out_ps).then_inc(out_copied, 1)

        run_steps(act, step)

    @block.vector
    def _(dve):
        nc.vector.memset(ones[:], 1.0).then_inc(set_up, 1)
        nc.vector.memset(f32(k_rest[DK:DK + 1, :, :, :]), 1.0).then_inc(set_up, 1)
        dve.wait_ge(set_up, 2)
        nc.vector.memset(maxima[:], 0.0).then_inc(set_up, 1)

        def step(s, par, flags, base):
            fin, att, nxt, prj = flags
            k = 0
            for kt, items in enumerate(step_items(*flags)):
                for what in items:
                    bank, kind = work[k % 2], what[0]
                    if kind == "MT" and what[1] == 0:
                        dve.wait_ge(work_emptied, base + k)
                        nc.vector.tensor_reduce(out=merged[:], in_=maxima[:], axis=AX, op=ALU.max
                                                ).then_inc(maxima_merged, 1)
                    dve.wait_ge(work_filled, base + k + 1)
                    if kind == "PJ":
                        which, half = what[1] // 2, what[1] % 2
                        cols = slice(half * HALF, (half + 1) * HALF)
                        dve.wait_ge(highs_ready, 4 * (s + 2) + what[1] + 1)
                        last = nc.vector.scalar_tensor_tensor(
                            out=low[:, par, which, cols], in0=bank, scalar=bias[:, par, which:which + 1],
                            in1=f32(high[:, par, which, cols]), op0=ALU.add, op1=ALU.subtract)
                    elif kind == "MAX":
                        _, h, qt, half = what
                        last = nc.vector.tensor_reduce(out=maxima[:, h * KT + qt, half:half + 1], in_=bank, axis=AX,
                                                       op=ALU.max)
                    elif kind == "MT":
                        if what[1] == 0 and not known(s, 0):
                            dve.wait_ge(shift_placed, 2 * DMA * (s + 1))
                        last = nc.vector.tensor_scalar(minus_max[:, what[1], :], bank[0:KT, 0:P], -1.0, None, ALU.mult)
                    elif kind == "SUM":
                        last = nc.vector.reciprocal(recip[:, what[1] * HALF:(what[1] + 1) * HALF], bank)
                    elif kind == "XT":
                        last = nc.vector.tensor_copy(x_et[:].rearrange("p k c -> p (k c)"), bank[:, 0:D])
                    elif kind == "GU":
                        dve.wait_ge(exp_g_ready, s + 1)
                        nc.vector.tensor_scalar(silu[:], exp_g[:], 1.0, None, ALU.add).then_inc(silu_vec, 1)
                        dve.wait_ge(silu_vec, 3 * s + 1)
                        nc.vector.reciprocal(silu[:], silu[:]).then_inc(silu_vec, 1)
                        dve.wait_ge(silu_vec, 3 * s + 2)
                        nc.vector.tensor_tensor(silu[:], bank[:, 0:F], silu[:], ALU.mult).then_inc(silu_vec, 1)
                        dve.wait_ge(silu_vec, 3 * s + 3)
                        last = nc.vector.tensor_tensor(hidden[:], bank[:, F:2 * F], silu[:], ALU.mult)
                    elif kind == "HT":
                        nc.vector.tensor_copy(hidden_t0[:], bank[:, 0:P])
                        last = nc.vector.tensor_copy(hidden_t1[:], bank[0:F2, P:2 * P])
                    elif kind == "DN":
                        if not known(s, 2):
                            dve.wait_ge(scattered, DMA * (s - 1))
                        last = nc.vector.tensor_scalar(y_e[:, par, :], bank[:, 0:D],
                                                       x_e[:, par, bass.ds(s + D, 1)], None, ALU.mult)
                    last.then_inc(work_emptied, 1)
                    k += 1
                    if kind == "SUM" and what[1] == 1:
                        dve.wait_ge(work_emptied, base + k)
                        dve.wait_ge(out_copied, s)
                        if not known(s, 2):
                            dve.wait_ge(out_stored, DMA * (s - 1))
                        nc.vector.tensor_tensor(out_t[:], out_raw[:], recip[:], ALU.mult).then_inc(out_ready, 1)
                if kt == 2 and nxt:
                    e = s + 1
                    dve.wait_ge(counts_loaded, DMA * (s + 2))
                    nc.vector.tensor_scalar(is_before[:], count_rows[:], keep["rank"][:, bass.ds(e, 1)], None,
                                            ALU.is_le).then_inc(tokens_vec, 1)
                    dve.wait_ge(tokens_vec, 2 * s + 3)
                    nc.vector.tensor_reduce(out=n_before[:], in_=is_before[:], axis=AX, op=ALU.add
                                            ).then_inc(tokens_vec, 1)
                    dve.wait_ge(tokens_vec, 2 * s + 4)
                    if not known(s, 1):
                        dve.wait_ge(scattered, DMA * s)
                    nc.vector.tensor_scalar(token[:, 1 - par:2 - par], n_before[:], keep["valid"][:, bass.ds(e, 1)],
                                            keep["first"][:, bass.ds(e, 1)], ALU.mult, ALU.add
                                            ).then_inc(tokens_ready, 1)

        run_steps(dve, step)

    @block.gpsimd
    def _(pool):
        nc.gpsimd.memset(is_before[:], 0.0).then_inc(standing, 1)

        def step(s, par, flags, base):
            fin, att, nxt, prj = flags
            if nxt:
                if not known(s, 0):
                    pool.wait_ge(tokens_ready, s + 1)
                nc.gpsimd.tensor_copy(count_slot[:], keep["count_row"][:, bass.ds(s + 1, 1)]).then_inc(slot_copied, 1)
                alone(pool, (standing, 1), (slot_copied, s + 2))
                nc.gpsimd.indirect_dma_start(
                    out=count_rows[:], out_offset=None, in_=io["counts"],
                    in_offset=bass.IndirectOffsetOnAxis(ap=count_slot[:, 0:1], axis=0)).then_inc(counts_loaded, DMA)
            for kt in range(1, KT) if att else ():
                for h in range(2):
                    pool.wait_ge(probs_ready, 16 * s + 2 * kt + h + 1)
                    if kt == 1:
                        if not known(s, 2):
                            pool.wait_ge(out_ready, s - 1)
                        first = probs[:, h, 0, :]
                    else:
                        first = sums[:, par, h, :]
                        pool.wait_ge(sums_added, 14 * s + 2 * (kt - 2) + h + 1)
                    nc.gpsimd.tensor_tensor(sums[:, par, h, :], first, probs[:, h, kt % 2, :], ALU.add
                                            ).then_inc(sums_added, 1)
                if kt == 4 and nxt:
                    fetch(s, par)
            if nxt and not att:
                fetch(s, par)
            if att:
                waits = [(work_emptied, base + item_at(flags, ("DN",)) + 1)]
                if not known(s, 1):
                    waits.append((scattered, DMA * s))
                alone(pool, (standing, 1), *waits)
                nc.gpsimd.indirect_dma_start(
                    out=io["moe"], out_offset=bass.IndirectOffsetOnAxis(ap=token[:, par:par + 1], axis=0),
                    in_=y_e[:, par, :], in_offset=None, compute_op=ALU.add).then_inc(scattered, DMA)

        def fetch(s, par):
            alone(pool, (standing, 1), (tokens_ready, s + 2))
            nc.gpsimd.indirect_dma_start(
                out=x_e[:, 1 - par, :], out_offset=None, in_=io["rows"],
                in_offset=bass.IndirectOffsetOnAxis(ap=token[:, 1 - par:2 - par], axis=0)
            ).then_inc(tokens_loaded, DMA)

        run_steps(pool, step)
        pool.wait_ge(scattered, DMA * NP)

    @block.sync
    def _(sp):
        def one(ap, i, pattern, out):
            return ap[bass.ds(i, 1)].rearrange(f"o {pattern} -> {out}", p=P)

        def load_projection(p, par):
            sp.dma_start(f32(x_t[:]), one(io["xt"], p // PAIRS, "p a k c", "(o p) a k c")).then_inc(x_loaded, DMA)
            hp = p % PAIRS
            sp.dma_start(f32(w_qk[:, par]), one(io["wqk"], hp, "p w a k c", "(o p) w a k c")).then_inc(w_loaded, DMA)
            sp.dma_start(bias[:, par, :], one(io["bqk"], hp, "p w", "(o p) w")).then_inc(w_loaded, DMA)

        load_projection(0, 0)

        def step(s, par, flags, base):
            fin, att, nxt, prj = flags
            if nxt:
                p, pp = s + 1, 1 - par
                e = p
                if att:
                    waits = [(placed, DMA * SHUFFLES * (s + 1)), (v_loaded, DMA * (s + 1)),
                             (experts_loaded, 4 * DMA * (s + 1)), (shift_placed, 2 * DMA * (s + 1))]
                    if fin:
                        waits.append((pv_done, 8 * s))
                    alone(sp, (standing, 1), *waits)
                sp.dma_start(v_sb[:, pp], one(io["v"], p, "p t c", "(o p) t c")).then_inc(v_loaded, DMA)
                sp.wait_ge(work_emptied, base)
                for h in range(2):
                    rows = slice(DK * h, DK * (h + 1))
                    top, bottom = slice(0, DK), slice(DK, P)
                    for dst, to, src, which in ((k_full, top, high, 1), (k_full, bottom, high, 1),
                                                (q_full, top, high, 0), (q_full, bottom, low, 0),
                                                (k_rest, top, low, 1), (q_rest, top, high, 0)):
                        sp.dma_start(f32(dst[to, pp, h, :]), f32(src[rows, pp, which, :])).then_inc(placed, DMA)
                sp.dma_start(w_gu[:, pp, :, 0:F], one(io["w_gate"], e, "(k p) f", "p (o k) f")
                             ).then_inc(experts_loaded, DMA)
                sp.dma_start(w_gu[:, pp, :, F:2 * F], one(io["w_up"], e, "(k p) f", "p (o k) f")
                             ).then_inc(experts_loaded, DMA)
                sp.dma_start(w_d0[:, pp, :], io["w_down"][bass.ds(e, 1), 0:P, :].rearrange("o p d -> (o p) d")
                             ).then_inc(experts_loaded, DMA)
                sp.dma_start(w_d1[:, pp, :], io["w_down"][bass.ds(e, 1), P:F, :].rearrange("o p d -> (o p) d")
                             ).then_inc(experts_loaded, DMA)
            if fin:
                if known(s, 2):
                    sp.wait_ge(out_ready, s)
                else:
                    alone(sp, (standing, 1), (out_stored, DMA * (s - 1)), (out_ready, s))
                sp.dma_start(one(io["ot"], s - 1, "p c", "(o p) c"), out_t[:]).then_inc(out_stored, DMA)
            if prj and not (isinstance(s, int) and s == NP - 3):
                alone(sp, (standing, 1), (x_loaded, DMA * (s + 3)), (w_loaded, 2 * DMA * (s + 3)),
                      (work_emptied, base + item_at(flags, ("PJ", 3)) + 1))
                load_projection(s + 3, 1 - par)
            if nxt:
                for h in range(2):
                    sp.wait_ge(work_emptied, base + item_at(flags, ("MT", h)) + 1)
                    sp.dma_start(f32(q_rest[DK:DK + 1, 1 - par, h, :]), f32(minus_max[:, h, :])
                                 ).then_inc(shift_placed, DMA)

        run_steps(sp, step)
        sp.wait_ge(out_stored, DMA * NP)


def output_stage(nc, ctx, io, keep):
    def sb(name, shape, dt=F32):
        return ctx.enter_context(nc.sbuf_tensor(name, shape, dt))

    def sem(name):
        return ctx.enter_context(nc.semaphore(name))

    psum = keep["psum"]
    wo = sb("wo", [P, PAIRS, D])
    bv = sb("bv", [P, PAIRS])
    bv_wide = sb("bv_wide", [P, PAIRS, P])
    bo = sb("bo", [1, D])
    ones_o = sb("ones_o", [P, P])
    const = sb("const", [P, UNIT, D])
    ot = sb("ot_sb", [P, 2, PAIRS, HALF])
    x_in = sb("x_out", [P, 2, UNIT, D])
    moe = sb("moe_sb", [P, 2, UNIT, D])
    rest = sb("rest", [P, 2, UNIT, D])
    y = sb("y", [P, 2, UNIT, D])

    loaded_w = sem("loaded_w")
    ones_set = sem("ones_set")
    bv_ready = sem("bv_ready")
    const_filled = sem("const_filled")
    const_ready = sem("const_ready")
    ot_loaded = sem("ot_loaded")
    xm_loaded = sem("xm_loaded")
    part_ready = sem("part_ready")
    rest_ready = sem("rest_ready")
    y_filled = sem("y_filled")
    y_ready = sem("y_ready")
    y_stored = sem("y_stored")
    block = ctx.enter_context(nc.Block())

    x_v = io["x"].rearrange("(u t p) d -> u p t d", p=P, t=UNIT)
    moe_v = io["moe"][0:T, :].rearrange("(u t p) d -> u p t d", p=P, t=UNIT)
    out_v = io["out"].rearrange("(u t p) d -> u p t d", p=P, t=UNIT)
    parts = "o p t d -> (o p) t d"

    def rounds(engine, unit):
        unit(0, 0)
        unit(0, 1)
        with engine.Fori(1, UNITS // 2) as i:
            unit(i, 0)
            unit(i, 1)

    def early(u):
        return isinstance(u, int) and u < 2

    @block.sync
    def _(sp):
        sp.dma_start(wo[:], io["wo"].rearrange("(h p) d -> p h d", p=P)).then_inc(loaded_w, DMA)
        sp.dma_start(bv[:], io["bv"]).then_inc(loaded_w, DMA)
        sp.dma_start(bo[:], io["bo"]).then_inc(loaded_w, DMA)

        def unit(i, par):
            u = i * 2 + par
            waits = [(ot_loaded, DMA * u), (xm_loaded, 2 * DMA * u)] if not known(u, 1) else []
            if not early(u):
                waits += [(y_filled, 2 * (u - 1)), (rest_ready, u - 1)]
            if waits:
                alone(sp, (loaded_w, 3 * DMA), *waits)
            sp.dma_start(ot[:, par], io["ot"][bass.ds(i * PAIRS, PAIRS), :, par * HALF:(par + 1) * HALF]
                         .rearrange("h p c -> p h c")).then_inc(ot_loaded, DMA)
            sp.dma_start(x_in[:, par], x_v[bass.ds(u, 1)].rearrange(parts)).then_inc(xm_loaded, DMA)
            sp.dma_start(moe[:, par], moe_v[bass.ds(u, 1)].rearrange(parts)).then_inc(xm_loaded, DMA)

        rounds(sp, unit)

    @block.gpsimd
    def _(pool):
        nc.gpsimd.memset(ones_o[:], 1.0).then_inc(ones_set, 1)
        pool.wait_ge(const_ready, 2)

        def unit(i, par):
            u = i * 2 + par
            pool.wait_ge(xm_loaded, 2 * DMA * (u + 1))
            if not early(u):
                pool.wait_ge(y_ready, 2 * (u - 1))
            nc.gpsimd.tensor_tensor(rest[:, par], x_in[:, par], moe[:, par], ALU.add).then_inc(part_ready, 1)
            pool.wait_ge(part_ready, u + 1)
            nc.gpsimd.tensor_tensor(rest[:, par], rest[:, par], const[:], ALU.add).then_inc(rest_ready, 1)

        rounds(pool, unit)

    @block.vector
    def _(dve):
        dve.wait_ge(loaded_w, 3 * DMA)
        dve.wait_ge(ones_set, 1)
        for h in range(PAIRS):
            last = nc.vector.tensor_scalar(bv_wide[:, h, :], ones_o[:], bv[:, h:h + 1], None, ALU.mult)
        last.then_inc(bv_ready, 1)
        dve.wait_ge(const_filled, 1)
        for half in range(2):
            nc.vector.tensor_copy(const[:, 2 * half:2 * half + 2, :],
                                  psum[:, 0, :].rearrange("p (t d) -> p t d", d=D)).then_inc(const_ready, 1)

        def unit(i, par):
            u = i * 2 + par
            dve.wait_ge(rest_ready, u + 1)
            if not early(u):
                dve.wait_ge(y_stored, DMA * (u - 1))
            for n in range(2):
                dve.wait_ge(y_filled, 2 * u + n + 1)
                nc.vector.tensor_tensor(y[:, par, 2 * n:2 * n + 2, :],
                                        psum[:, 2 + 2 * par + n, :].rearrange("p (t d) -> p t d", d=D),
                                        rest[:, par, 2 * n:2 * n + 2, :], ALU.add).then_inc(y_ready, 1)

        rounds(dve, unit)

    @block.tensor
    def _(pe):
        pe.wait_ge(bv_ready, 1)
        for t in range(2):
            cols = slice(t * D, (t + 1) * D)
            for h in range(PAIRS):
                nc.tensor.matmul(psum[:, 0, cols], bv_wide[:, h, :], wo[:, h, :], start=(h == 0), stop=False)
            last = nc.tensor.matmul(psum[:, 0, cols], ones_o[0:1, :], bo[:], start=False, stop=True)
        last.then_inc(const_filled, 1)

        def unit(i, par):
            u = i * 2 + par
            pe.wait_ge(ot_loaded, DMA * (u + 1))
            if not early(u):
                pe.wait_ge(y_ready, 2 * (u - 1))
            for n in range(2):
                for t in range(2):
                    tok = slice((2 * n + t) * P, (2 * n + t + 1) * P)
                    for h in range(PAIRS):
                        last = nc.tensor.matmul(psum[:, 2 + 2 * par + n, t * D:(t + 1) * D], ot[:, par, h, tok],
                                                wo[:, h, :], start=(h == 0), stop=(h == PAIRS - 1))
                last.then_inc(y_filled, 1)

        rounds(pe, unit)

    @block.scalar
    def _(act):
        def unit(i, par):
            u = i * 2 + par
            if not known(u, 1):
                act.wait_ge(y_stored, DMA * u)
            act.wait_ge(y_ready, 2 * (u + 1))
            act.dma_start(out_v[bass.ds(u, 1)].rearrange(parts), y[:, par]).then_inc(y_stored, DMA)

        rounds(act, unit)
        act.wait_ge(y_stored, DMA * UNITS)


def build(nc, io):
    def dram(name, shape):
        return nc.dram_tensor(name, shape, F32, kind="Internal").ap()

    io["rows"] = dram("rows", [T + C, ROW])
    io["moe"] = dram("moe", [T + C, D])
    io["xt"] = dram("xt", [B, P, 2, KD, N])
    io["v"] = dram("v", [NP, P, KT, P])
    io["wqk"] = dram("wqk_parts", [PAIRS, P, 2, 2, KD, P])
    io["counts"] = dram("counts_rows", [TILES * E, P])
    io["ot"] = dram("ot", [NP, P, N])
    with ExitStack() as ctx:
        keep = {
            "psum": ctx.enter_context(nc.psum_tensor("psum", [P, 8, HALF], F32)),
            "ident": ctx.enter_context(nc.sbuf_tensor("ident", [P, P], F32)),
        }
        for name in ("rank", "valid", "first"):
            keep[name] = ctx.enter_context(nc.sbuf_tensor(name, [P, E], F32))
        keep["count_row"] = ctx.enter_context(nc.sbuf_tensor("count_row", [P, E], U32))
        with ExitStack() as mctx:
            keep["masks"] = mctx.enter_context(nc.sbuf_tensor("masks", [P, TILES, E], BF16))
            with ExitStack() as sub:
                norm_stage(nc, sub, io, keep)
            with ExitStack() as sub:
                table_stage(nc, sub, io, keep)
        with ExitStack() as sub:
            attention_stage(nc, sub, io, keep)
        with ExitStack() as sub:
            output_stage(nc, sub, io, keep)


def kernel(**inputs):
    import numpy as np
    import concourse.bacc as bacc
    from concourse.bass_utils import run_bass_kernel_spmd

    a = {k.replace("L0_", ""): np.asarray(v) for k, v in inputs.items()}
    arrays = {
        "x": a["attn_y"].reshape(T, D),
        "wq": a["attn_Wq"].T, "wk": a["attn_Wk"].T, "wv": a["attn_Wv"].T, "wo": a["attn_Wo"].T,
        "bqk": np.stack([a["attn_bq"].reshape(PAIRS, P), a["attn_bk"].reshape(PAIRS, P)], axis=-1),
        "bv": a["attn_bv"].reshape(PAIRS, P).T, "bo": a["attn_bo"].reshape(1, D),
        "router": a["ffn_router_w"].T, "w_gate": a["ffn_w_gate"], "w_up": a["ffn_w_up"],
        "w_down": a["ffn_w_down"], "ws_gu": a["ffn_ws_gate_up"], "ws_d": a["ffn_ws_down"],
    }
    nc = bacc.Bacc("TRN2", target_bir_lowering=False, num_devices=1)
    io, feed = {}, {}
    for name, v in arrays.items():
        v = np.ascontiguousarray(v)
        feed[f"in_{name}"] = v
        io[name] = nc.dram_tensor(f"in_{name}", v.shape, F32, kind="ExternalInput").ap()
    io["out"] = nc.dram_tensor("out_y", (T, D), F32, kind="ExternalOutput").ap()
    build(nc, io)
    got = run_bass_kernel_spmd(nc, [feed], core_ids=[0])
    return got.results[0]["out_y"].reshape(B, N, D)
```

```python
from contextlib import ExitStack

import concourse.bass as bass
from concourse import mybir

F32 = mybir.dt.float32
F32R = mybir.dt.float32r
BF16 = mybir.dt.bfloat16
U32 = mybir.dt.uint32
ALU = mybir.AluOpType
ACT = mybir.ActivationFunctionType
AX = mybir.AxisListType.X

P = 128
B, N, D = 8, 1024, 256
T = B * N
H, DK = 16, 64
HD = H * DK
PAIRS = H // 2
NP = B * PAIRS
E, TOPK, F, C = 64, 8, 192, 128
F2 = F - P
KD = D // P
TILES = T // P
KT = N // P
ROW = D + E
EPS = 1e-5
SCALE = float(DK) ** -0.5
HALF = 512

UNIT = 4
UNITS = TILES // UNIT

HIGH, LOW = 0, 1
DMA = 16


def alone(engine, met, *waits):
    waits = [(sem, v if isinstance(v, int) else engine.to_reg(v)) for sem, v in waits]
    engine.wait_ge(*met)
    for sem, value in waits:
        engine.wait_ge(sem, value)


def known(v, least):
    return isinstance(v, int) and v < least


def f32(ap):
    return ap.bitcast(F32)


def norm_stage(nc, ctx, io, keep):
    def sb(name, shape, dt=F32):
        return ctx.enter_context(nc.sbuf_tensor(name, shape, dt))

    def sem(name):
        return ctx.enter_context(nc.semaphore(name))

    psum, ident, masks = keep["psum"], keep["ident"], keep["masks"]
    transposed_ps = psum[:, 0:2, :]
    router_ps = psum[:, 2, 0:UNIT * E]
    gate_ps, up_ps, down_ps = psum[:, 3, :], psum[:, 4, :], psum[:, 5, :]

    x_in = sb("x_in", [P, 2, UNIT, D])
    normed = sb("normed", [P, 2, UNIT, D])
    xt32 = sb("xt32", [P, 2, KD, HALF])
    xt_high = sb("xt_high", [P, 2, KD, HALF], F32R)
    xt_low = sb("xt_low", [P, 2, KD, HALF], F32R)
    values = sb("values", [P, 2, UNIT, HD])
    wv32 = sb("wv32", [P, KD, HD])
    wv = sb("wv", [P, 2, KD, HD], F32R)
    wqk = sb("wqk", [P, 2, KD, HD], F32R)
    router = sb("router", [P, KD, E])
    ws_gu = sb("ws_gu", [P, KD, 2 * F])
    ws_d0 = sb("ws_d0", [P, D])
    ws_d1 = sb("ws_d1", [F2, D])
    stats = sb("stats", [P, UNIT, 6])
    meanvar = sb("meanvar", [P, UNIT, 2])
    var_eps = sb("var_eps", [P, UNIT])
    minus_half = sb("minus_half", [P, UNIT])
    rstd0 = sb("rstd0", [P, UNIT])
    newton = sb("newton", [P, UNIT])
    rstd = sb("rstd", [P, UNIT])
    row4 = sb("row4", [P, UNIT])
    logit = sb("logit", [P, UNIT, E])
    prob_e = sb("prob_e", [P, UNIT, E])
    prob = sb("prob", [P, UNIT, E])
    top = sb("top", [P, UNIT, TOPK])
    replaced = sb("replaced", [P, UNIT, E])
    chosen = sb("chosen", [P, UNIT, E])
    weight = sb("weight", [P, 2, UNIT, E])
    exp_g = sb("exp_g", [P, HALF])
    silu = sb("silu", [P, HALF])
    hidden0 = sb("hidden0", [P, HALF])
    hidden1 = sb("hidden1", [F2, HALF])
    shared = sb("shared", [P, 2, UNIT, D])
    zeros = sb("zeros", [P, ROW])

    weights_in = sem("weights_in")
    wv_in = sem("wv_in")
    w_high = sem("w_high")
    w_low = sem("w_low")
    w_stored = sem("w_stored")
    ready = sem("ready")
    zeros_set = sem("zeros_set")
    x_loaded = sem("x_loaded")
    normed_ready = sem("normed_ready")
    var_ready = sem("var_ready")
    pow_ready = sem("pow_ready")
    vec = sem("vec")
    xt_filled = sem("xt_filled")
    xt_highs = sem("xt_highs")
    xt_lows = sem("xt_lows")
    router_filled = sem("router_filled")
    logits_ready = sem("logits_ready")
    exp_ready = sem("exp_ready")
    weight_ready = sem("weight_ready")
    gu_filled = sem("gu_filled")
    exp_g_ready = sem("exp_g_ready")
    hidden_ready = sem("hidden_ready")
    down_filled = sem("down_filled")
    shared_ready = sem("shared_ready")
    v_filled = sem("v_filled")
    v_copied = sem("v_copied")
    normed_stored = sem("normed_stored")
    xt_stored = sem("xt_stored")
    weight_stored = sem("weight_stored")
    v_stored = sem("v_stored")
    shared_stored = sem("shared_stored")
    pads_stored = sem("pads_stored")

    x_v = io["x"].rearrange("(u t p) d -> u p t d", p=P, t=UNIT)
    rows_v = io["rows"][0:T, :].rearrange("(u t p) d -> u p t d", p=P, t=UNIT)
    moe_v = io["moe"][0:T, :].rearrange("(u t p) d -> u p t d", p=P, t=UNIT)

    block = ctx.enter_context(nc.Block())

    @block.sync
    def _(sp):
        for n, w in enumerate(("wv", "wq", "wk")):
            if n:
                sp.wait_ge(w_low, n)
            sp.dma_start(wv32[:], io[w].rearrange("(k p) e -> p k e", p=P)).then_inc(wv_in, DMA)
            if n == 0:
                sp.dma_start(x_in[:, 0], x_v[0]).then_inc(x_loaded, DMA)
                sp.dma_start(router[:], io["router"].rearrange("(k p) e -> p k e", p=P)).then_inc(weights_in, DMA)
                sp.dma_start(ws_gu[:], io["ws_gu"].rearrange("(k p) e -> p k e", p=P)).then_inc(weights_in, DMA)
                sp.dma_start(ws_d0[:], io["ws_d"][0:P, :]).then_inc(weights_in, DMA)
                sp.dma_start(ws_d1[:], io["ws_d"][P:F, :]).then_inc(weights_in, DMA)
            else:
                sp.wait_ge(w_high, n + 1)
                sp.wait_ge(w_low, n + 1)
                for part in range(2):
                    for k in range(KD):
                        sp.dma_start(io["wqk"][:, :, n - 1, part, k, :].rearrange("h p c -> p h c"),
                                     f32(wqk[:, part, k, :]).rearrange("p (h c) -> p h c", c=P)
                                     ).then_inc(w_stored, DMA)
        sp.wait_ge(zeros_set, 1)
        sp.dma_start(io["rows"][T:T + C, :], zeros[:]).then_inc(pads_stored, DMA)
        sp.dma_start(io["moe"][T:T + C, :], zeros[:, 0:D]).then_inc(pads_stored, DMA)

        def unit(i, par, more):
            u = i * 2 + par
            if more:
                if not (isinstance(u, int) and u == 0):
                    sp.wait_ge(normed_ready, u)
                sp.dma_start(x_in[:, 1 - par], x_v[bass.ds(u + 1, 1)].rearrange("o p t d -> (o p) t d")
                             ).then_inc(x_loaded, DMA)
            one = bass.ds(u, 1)
            sp.wait_ge(normed_ready, u + 1)
            sp.dma_start(rows_v[one, :, :, 0:D].rearrange("o p t d -> (o p) t d"), normed[:, par]
                         ).then_inc(normed_stored, DMA)
            sp.wait_ge(xt_lows, u + 1)
            for part, tile in ((HIGH, xt_high), (LOW, xt_low)):
                for k in range(KD):
                    sp.dma_start(io["xt"][bass.ds(i, 1), :, part, k, par * HALF:(par + 1) * HALF]
                                 .rearrange("o p c -> (o p) c"), f32(tile[:, par, k, :])).then_inc(xt_stored, DMA)
            sp.wait_ge(weight_ready, u + 1)
            sp.dma_start(rows_v[one, :, :, D:ROW].rearrange("o p t d -> (o p) t d"), weight[:, par]
                         ).then_inc(weight_stored, DMA)
            for t in range(UNIT):
                sp.wait_ge(v_copied, (u * UNIT + t) * 2 + 2)
                sp.dma_start(io["v"][bass.ds(i * PAIRS, PAIRS), :, par * UNIT + t, :].rearrange("h p c -> p h c"),
                             values[:, par, t, :].rearrange("p (h c) -> p h c", c=P)).then_inc(v_stored, DMA)
            sp.wait_ge(shared_ready, 2 * u + 2)
            sp.dma_start(moe_v[one].rearrange("o p t d -> (o p) t d"), shared[:, par]).then_inc(shared_stored, DMA)

        unit(0, 0, True)
        unit(0, 1, True)
        with sp.Fori(1, UNITS // 2 - 1) as i:
            unit(i, 0, True)
            unit(i, 1, True)
        unit(UNITS // 2 - 1, 0, True)
        unit(UNITS // 2 - 1, 1, False)
        sp.wait_ge(w_stored, DMA * 8)
        sp.wait_ge(pads_stored, DMA * 2)
        sp.wait_ge(normed_stored, DMA * UNITS)
        sp.wait_ge(xt_stored, DMA * 4 * UNITS)
        sp.wait_ge(weight_stored, DMA * UNITS)
        sp.wait_ge(v_stored, DMA * UNIT * UNITS)
        sp.wait_ge(shared_stored, DMA * UNITS)

    @block.gpsimd
    def _(pool):
        nc.gpsimd.memset(zeros[:], 0.0).then_inc(zeros_set, 1)
        nc.gpsimd.memset(minus_half[:], -0.5).then_inc(ready, 1)
        nc.gpsimd.memset(ident[:], 0.0).then_inc(ready, 1)
        pool.wait_ge(ready, 2)
        nc.gpsimd.affine_select(out=ident[:], in_=ident[:], compare_op=ALU.not_equal, fill=1.0, base=0,
                                pattern=[[-1, P]], channel_multiplier=1).then_inc(ready, 1)
        with pool.Fori(0, UNITS) as u:
            pool.wait_ge(var_ready, u + 1)
            nc.gpsimd.tensor_tensor(rstd0[:], var_eps[:], minus_half[:], ALU.pow).then_inc(pow_ready, 1)

    @block.scalar
    def _(act):
        for n in range(3):
            act.wait_ge(wv_in, DMA * (n + 1))
            if n == 2:
                act.wait_ge(w_stored, DMA * 4)
            nc.scalar.copy((wv if n == 0 else wqk)[:, HIGH], wv32[:]).then_inc(w_high, 1)

        def unit(i, par):
            u = i * 2 + par
            first = isinstance(u, int) and u < 2

            def values_out(lo, hi):
                for n in range(lo, hi):
                    act.wait_ge(v_filled, 8 * u + n + 1)
                    if n == 0 and not first:
                        act.wait_ge(v_stored, DMA * UNIT * (u - 1))
                    nc.scalar.copy(values[:, par, n // 2, (n % 2) * HALF:(n % 2 + 1) * HALF],
                                   psum[:, 6 + n % 2, :]).then_inc(v_copied, 1)

            act.wait_ge(xt_filled, u + 1)
            if not first:
                act.wait_ge(xt_stored, DMA * 4 * (u - 1))
                act.wait_ge(down_filled, 2 * (u - 1))
            nc.scalar.copy(xt_high[:, par], transposed_ps)
            nc.scalar.copy(xt32[:, par], transposed_ps).then_inc(xt_highs, 1)
            act.wait_ge(logits_ready, u + 1)
            nc.scalar.activation(prob_e[:], logit[:], ACT.Exp).then_inc(exp_ready, 1)
            for c, rows in ((0, P), (1, F2)):
                act.wait_ge(gu_filled, 2 * u + c + 1)
                if c or not (isinstance(u, int) and u == 0):
                    act.wait_ge(hidden_ready, 2 * u + c)
                nc.scalar.activation(exp_g[0:rows, :], gate_ps[0:rows, :], ACT.Exp, scale=-1.0
                                     ).then_inc(exp_g_ready, 1)
                values_out(4 * c, 4 * c + 4)

        unit(0, 0)
        unit(0, 1)
        with act.Fori(1, UNITS // 2) as i:
            unit(i, 0)
            unit(i, 1)

    @block.vector
    def _(dve):
        NORM_LINKS, VEC = 7, 23
        for n in range(3):
            part = wv if n == 0 else wqk
            dve.wait_ge(w_high, n + 1)
            nc.vector.tensor_tensor(part[:, LOW], wv32[:], f32(part[:, HIGH]), ALU.subtract).then_inc(w_low, 1)

        def linked(start, count):
            def link(ins, standing=False):
                count[0] += 1
                ins.then_inc(vec, 1)
                if standing:
                    alone(dve, (x_loaded, DMA), (vec, start + count[0]))
                else:
                    dve.wait_ge(vec, start + count[0])
            return link

        def norm(v, par, link):
            first = isinstance(v, int) and v < 2
            dve.wait_ge(x_loaded, DMA * (v + 1))
            for t in range(UNIT):
                last = nc.vector.bn_stats(out=stats[:, t, :], in_=x_in[:, par, t, :])
            link(last, True)
            for t in range(UNIT):
                last = nc.vector.bn_aggr(out=meanvar[:, t, :], in_=stats[:, t, :])
            link(last)
            link(nc.vector.tensor_scalar(var_eps[:], meanvar[:, :, 1], EPS, None, ALU.add))
            nc.vector.tensor_copy(row4[:], var_eps[:]).then_inc(var_ready, 1)
            dve.wait_ge(pow_ready, v + 1)
            link(nc.vector.tensor_tensor(newton[:], rstd0[:], rstd0[:], ALU.mult))
            link(nc.vector.tensor_tensor(newton[:], newton[:], var_eps[:], ALU.mult))
            link(nc.vector.tensor_scalar(newton[:], newton[:], -0.5, 1.5, ALU.mult, ALU.add))
            link(nc.vector.tensor_tensor(rstd[:], newton[:], rstd0[:], ALU.mult))
            if not first:
                dve.wait_ge(normed_stored, DMA * (v - 1))
                dve.wait_ge(xt_filled, v - 1)
            for t in range(UNIT):
                last = nc.vector.tensor_scalar(normed[:, par, t, :], x_in[:, par, t, :], meanvar[:, t, 0:1],
                                               rstd[:, t:t + 1], ALU.subtract, ALU.mult)
            last.then_inc(normed_ready, 1)

        def unit(i, par, more):
            u = i * 2 + par
            first = isinstance(u, int) and u < 2
            count = [0]
            link = linked(u * VEC + NORM_LINKS, count)
            dve.wait_ge(xt_highs, u + 1)
            if not first:
                dve.wait_ge(xt_stored, DMA * 4 * (u - 1))
            nc.vector.tensor_tensor(xt_low[:, par], transposed_ps, f32(xt_high[:, par]), ALU.subtract
                                    ).then_inc(xt_lows, 1)
            dve.wait_ge(router_filled, u + 1)
            scores = router_ps.rearrange("p (t e) -> p t e", e=E)
            wide = [P, UNIT, E]
            link(nc.vector.tensor_reduce(out=row4[:], in_=scores, axis=AX, op=ALU.max))
            nc.vector.tensor_tensor(logit[:], scores, row4[:].rearrange("p (t o) -> p t o", o=1).to_broadcast(wide),
                                    ALU.subtract).then_inc(logits_ready, 1)
            dve.wait_ge(exp_ready, u + 1)
            link(nc.vector.tensor_reduce(out=row4[:], in_=prob_e[:], axis=AX, op=ALU.add))
            link(nc.vector.reciprocal(row4[:], row4[:]))
            link(nc.vector.tensor_tensor(prob[:], prob_e[:],
                                         row4[:].rearrange("p (t o) -> p t o", o=1).to_broadcast(wide), ALU.mult), True)
            for t in range(UNIT):
                last = nc.vector.max(out=top[:, t, :], in_=prob[:, t, :])
            link(last, True)
            for t in range(UNIT):
                last = nc.vector.match_replace(out=replaced[:, t, :], in_to_replace=top[:, t, :],
                                               in_values=prob[:, t, :], imm_value=-1.0)
            link(last)
            link(nc.vector.tensor_tensor(chosen[:], prob[:], replaced[:], ALU.not_equal))
            nc.vector.tensor_copy(masks[:, bass.ds(u * UNIT, UNIT), :], chosen[:])
            link(nc.vector.tensor_tensor(prob[:], prob[:], chosen[:], ALU.mult))
            link(nc.vector.tensor_reduce(out=row4[:], in_=prob[:], axis=AX, op=ALU.add))
            link(nc.vector.reciprocal(row4[:], row4[:]))
            if not first:
                dve.wait_ge(weight_stored, DMA * (u - 1))
            nc.vector.tensor_tensor(weight[:, par], prob[:], row4[:].rearrange("p (t o) -> p t o", o=1)
                                    .to_broadcast(wide), ALU.mult).then_inc(weight_ready, 1)
            if more:
                norm(u + 1, 1 - par, link)
            for c, (rows, hidden) in enumerate(((P, hidden0), (F2, hidden1))):
                dve.wait_ge(exp_g_ready, 2 * u + c + 1)
                link(nc.vector.tensor_scalar(silu[0:rows, :], exp_g[0:rows, :], 1.0, None, ALU.add))
                link(nc.vector.reciprocal(silu[0:rows, :], silu[0:rows, :]))
                link(nc.vector.tensor_tensor(silu[0:rows, :], gate_ps[0:rows, :], silu[0:rows, :], ALU.mult))
                if not (isinstance(u, int) and u == 0):
                    dve.wait_ge(down_filled, 2 * u)
                nc.vector.tensor_tensor(hidden[:], up_ps[0:rows, :], silu[0:rows, :], ALU.mult
                                        ).then_inc(hidden_ready, 1)
            if not first:
                dve.wait_ge(shared_stored, DMA * (u - 1))
            for n in range(2):
                dve.wait_ge(down_filled, 2 * u + n + 1)
                nc.vector.tensor_copy(shared[:, par, 2 * n:2 * n + 2, :],
                                      down_ps.rearrange("p (t d) -> p t d", d=D)).then_inc(shared_ready, 1)
            assert count[0] == VEC or not more, count[0]

        norm(0, 0, linked(0, [0]))
        unit(0, 0, True)
        unit(0, 1, True)
        with dve.Fori(1, UNITS // 2 - 1) as i:
            unit(i, 0, True)
            unit(i, 1, True)
        unit(UNITS // 2 - 1, 0, True)
        unit(UNITS // 2 - 1, 1, False)

    @block.tensor
    def _(pe):
        def transposes(u, par):
            pe.wait_ge(normed_ready, u + 1)
            if not (isinstance(u, int) and u == 0):
                pe.wait_ge(xt_lows, u)
            for k in range(KD):
                for t in range(UNIT):
                    last = nc.tensor.transpose(transposed_ps[:, k, t * P:(t + 1) * P],
                                               normed[:, par, t, k * P:(k + 1) * P], ident[:])
            last.then_inc(xt_filled, 1)

        def values_in(u, par, lo, hi):
            for n in range(lo, hi):
                t, half = n // 2, n % 2
                if not (isinstance(u, int) and u == 0 and n < 2):
                    pe.wait_ge(v_copied, 8 * u + n - 1)
                terms = [(xt_high, HIGH), (xt_high, LOW), (xt_low, HIGH)]
                for j, (tile, part) in enumerate(terms):
                    for k in range(KD):
                        last = nc.tensor.matmul(psum[:, 6 + n % 2, :], tile[:, par, k, t * P:(t + 1) * P],
                                                wv[:, part, k, half * HALF:(half + 1) * HALF],
                                                start=(j == 0 and k == 0), stop=(j == 2 and k == KD - 1))
                last.then_inc(v_filled, 1)

        def gate_up(u, par, c, rows):
            if c or not (isinstance(u, int) and u == 0):
                pe.wait_ge(hidden_ready, 2 * u + c)
            for out, col in ((gate_ps, c * P), (up_ps, F + c * P)):
                for k in range(KD):
                    last = nc.tensor.matmul(out[0:rows, :], ws_gu[:, k, col:col + rows], xt32[:, par, k, :],
                                            start=(k == 0), stop=(k == KD - 1))
            last.then_inc(gu_filled, 1)

        def unit(i, par, more):
            u = i * 2 + par
            pe.wait_ge(xt_highs, u + 1)
            pe.wait_ge(xt_lows, u + 1)
            if not (isinstance(u, int) and u == 0):
                pe.wait_ge(logits_ready, u)
            for t in range(UNIT):
                for k in range(KD):
                    last = nc.tensor.matmul(router_ps[:, t * E:(t + 1) * E], xt32[:, par, k, t * P:(t + 1) * P],
                                            router[:, k, :], start=(k == 0), stop=(k == KD - 1))
            last.then_inc(router_filled, 1)
            gate_up(u, par, 0, P)
            values_in(u, par, 0, 4)
            gate_up(u, par, 1, F2)
            if more:
                transposes(u + 1, 1 - par)
            values_in(u, par, 4, 8)
            pe.wait_ge(hidden_ready, 2 * u + 2)
            for n in range(2):
                if n or not (isinstance(u, int) and u == 0):
                    pe.wait_ge(shared_ready, 2 * u + n)
                for t in range(2):
                    cols = slice((2 * n + t) * P, (2 * n + t + 1) * P)
                    nc.tensor.matmul(down_ps[:, t * D:(t + 1) * D], hidden0[:, cols], ws_d0[:],
                                     start=True, stop=False)
                    last = nc.tensor.matmul(down_ps[:, t * D:(t + 1) * D], hidden1[:, cols], ws_d1[:],
                                            start=False, stop=True)
                last.then_inc(down_filled, 1)

        pe.wait_ge(ready, 3)
        pe.wait_ge(weights_in, DMA * 4)
        transposes(0, 0)
        pe.wait_ge(w_high, 1)
        pe.wait_ge(w_low, 1)
        unit(0, 0, True)
        unit(0, 1, True)
        with pe.Fori(1, UNITS // 2 - 1) as i:
            unit(i, 0, True)
            unit(i, 1, True)
        unit(UNITS // 2 - 1, 0, True)
        unit(UNITS // 2 - 1, 1, False)


def table_stage(nc, ctx, io, keep):
    def sb(name, shape, dt=F32):
        return ctx.enter_context(nc.sbuf_tensor(name, shape, dt))

    def sem(name):
        return ctx.enter_context(nc.semaphore(name))

    psum, masks = keep["psum"], keep["masks"]
    ones = sb("ones_bf", [P, P], BF16)
    upto = sb("upto", [P, P], BF16)
    slot_f = sb("slot_f", [P, 1])
    pad_row = sb("pad_row", [P, 1])
    expert_i = sb("expert_i", [P, E])
    counts = sb("counts", [P, E, TILES])
    carry = sb("carry", [P, E, TILES])
    running = sb("running", [P, E, TILES])
    before = sb("before", [P, E, TILES])
    tile_of = sb("tile_of", [P, E])
    base = sb("base", [P, E])
    rows = sb("rows_sb", [P, TILES // 2, P])
    scratch = sb("scratch_t", [P, E])

    consts = sem("t_consts")
    counted = sem("counted")
    counts_out = sem("counts_out")
    row_filled = sem("row_filled")
    rows_out = sem("rows_out")
    rows_stored = sem("rows_stored")
    tvec = sem("tvec")
    block = ctx.enter_context(nc.Block())

    @block.gpsimd
    def _(pool):
        nc.gpsimd.memset(ones[:], 1.0).then_inc(consts, 1)
        nc.gpsimd.memset(upto[:], 1.0).then_inc(consts, 1)
        nc.gpsimd.memset(carry[:], 1.0).then_inc(consts, 1)
        nc.gpsimd.iota(slot_f[:], pattern=[[1, 1]], base=0, channel_multiplier=1,
                       allow_small_or_imprecise_dtypes=True).then_inc(consts, 1)
        nc.gpsimd.iota(pad_row[:], pattern=[[1, 1]], base=T, channel_multiplier=1,
                       allow_small_or_imprecise_dtypes=True).then_inc(consts, 1)
        nc.gpsimd.iota(expert_i[:], pattern=[[1, E]], base=0, channel_multiplier=0,
                       allow_small_or_imprecise_dtypes=True).then_inc(consts, 1)
        pool.wait_ge(consts, 6)
        nc.gpsimd.affine_select(out=upto[:], in_=upto[:], compare_op=ALU.is_ge, fill=0.0, base=0,
                                pattern=[[1, P]], channel_multiplier=-1).then_inc(consts, 1)
        nc.gpsimd.memset(carry[:, :, 0:1], 0.0).then_inc(consts, 1)

    @block.tensor
    def _(pe):
        pe.wait_ge(consts, 8)
        flat = masks[:].rearrange("p j e -> p (j e)")
        for n in range(8):
            nc.tensor.matmul(psum[:, n, :], ones[:], flat[:, n * HALF:(n + 1) * HALF], start=True, stop=True
                             ).then_inc(counted, 1)
        for n in range(8):
            pe.wait_ge(counts_out, n + 1)
            for g in range(4):
                j = 4 * n + g
                last = nc.tensor.matmul(psum[:, n, g * P:(g + 1) * P], flat[:, j * P:(j + 1) * P], upto[:],
                                        start=True, stop=True)
            last.then_inc(row_filled, 1)

    @block.scalar
    def _(act):
        for n in range(8):
            act.wait_ge(counted, n + 1)
            nc.scalar.copy(counts[:, :, 8 * n:8 * n + 8].rearrange("p e j -> p j e"),
                           psum[:, n, :].rearrange("p (j e) -> p j e", e=E)).then_inc(counts_out, 1)
        for n in range(8):
            act.wait_ge(row_filled, n + 1)
            nc.scalar.copy(rows[:, 4 * n:4 * n + 4, :], psum[:, n, :].rearrange("p (g q) -> p g q", q=P)
                           ).then_inc(rows_out, 1)

    @block.sync
    def _(sp):
        sp.wait_ge(rows_out, 8)
        sp.dma_start(io["counts"].rearrange("(g r) q -> r g q", r=P), rows[:]).then_inc(rows_stored, DMA)
        sp.wait_ge(rows_stored, DMA)

    @block.vector
    def _(dve):
        count = [0]

        def link(ins):
            count[0] += 1
            ins.then_inc(tvec, 1)
            dve.wait_ge(tvec, count[0])

        dve.wait_ge(consts, 8)
        dve.wait_ge(counts_out, 8)
        link(nc.vector.tensor_tensor_scan(running[:].rearrange("p e j -> p (e j)"),
                                          carry[:].rearrange("p e j -> p (e j)"),
                                          counts[:].rearrange("p e j -> p (e j)"), 0.0, ALU.mult, ALU.add))
        link(nc.vector.tensor_scalar(before[:], running[:], slot_f[:, 0:1], None, ALU.is_le))
        link(nc.vector.tensor_reduce(out=tile_of[:], in_=before[:], axis=AX, op=ALU.add))
        link(nc.vector.tensor_tensor(before[:], before[:], counts[:], ALU.mult))
        link(nc.vector.tensor_reduce(out=base[:], in_=before[:], axis=AX, op=ALU.add))
        nc.vector.tensor_scalar(keep["rank"][:], base[:], -1.0, slot_f[:, 0:1], ALU.mult, ALU.add)
        link(nc.vector.tensor_scalar(keep["valid"][:], tile_of[:], float(TILES), None, ALU.is_lt))
        link(nc.vector.tensor_scalar(base[:], tile_of[:], float(P), pad_row[:, 0:1], ALU.mult, ALU.subtract))
        link(nc.vector.tensor_tensor(base[:], base[:], keep["valid"][:], ALU.mult))
        link(nc.vector.tensor_scalar(keep["first"][:], base[:], pad_row[:, 0:1], None, ALU.add))
        link(nc.vector.tensor_scalar(scratch[:], tile_of[:], float(TILES - 1), float(E), ALU.min, ALU.mult))
        link(nc.vector.tensor_tensor(keep["count_row"][:], scratch[:], expert_i[:], ALU.add))


DVE, ACTE = 0, 1
EMPTIED_BY = {"MAX": DVE, "MT": DVE, "PJ": DVE, "XT": ACTE, "GU": ACTE, "HT": ACTE, "DN": ACTE, "SUM": ACTE}
PARTS = 6
PLACES = {(0, 5): ("XT",), (1, 0): ("PJ", 0), (1, 3): ("SUM", 0), (2, 0): ("PJ", 1), (2, 1): ("GU",),
          (2, 4): ("SUM", 1), (3, 0): ("PJ", 2), (4, 0): ("PJ", 3), (5, 0): ("MT", 0), (5, 3): ("HT",),
          (6, 1): ("DN",), (7, 3): ("MT", 1)}
SIDE = {"XT": 1, "GU": 1, "HT": 1, "DN": 1, "SUM": 0, "MAX": 2, "MT": 2, "PJ": 3}


def step_items(flags):
    units = iter([("MAX", h, qt, half) for h in range(2) for qt in range(KT) for half in range(2)])
    out = []
    for slot in range(KT):
        for part in range(PARTS):
            item = PLACES.get((slot, part)) or next(units, None)
            if item and flags[SIDE[item[0]]]:
                out.append((slot, part, item))
    assert next(units, None) is None
    return out


def n_items(flags, who=None):
    return sum(who is None or EMPTIED_BY[it[0]] == who for _, _, it in step_items(flags))


FULL = (True, True, True, True)
HEAD = [(-2, (False, False, False, True)), (-1, (False, False, True, True)), (0, (False, True, True, True)),
        (1, FULL), (2, FULL)]
LOOP0, LOOP1 = 3, NP - 3
TAIL = [(NP - 3, FULL), (NP - 2, (True, True, True, False)), (NP - 1, (True, True, False, False)),
        (NP, (True, False, False, False))]
assert (LOOP1 - LOOP0) % 2 == 0


class Step:

    def __init__(self, s, flags, last, base, counts):
        self.s, self.flags, self.last, self.base, self.counts = s, flags, last, base, counts
        self.items = step_items(flags)

    def emptied(self, sems, k):
        if k >= 0:
            who = EMPTIED_BY[self.items[k][2][0]]
            return sems[who], self.counts[who] + sum(EMPTIED_BY[it[2][0]] == who for it in self.items[:k + 1])
        before = step_items(self.last)
        who = EMPTIED_BY[before[k][2][0]]
        left = sum(EMPTIED_BY[it[2][0]] == who for it in before[len(before) + k + 1:])
        return sems[who], self.counts[who] - left

    def at(self, item):
        return [it for _, _, it in self.items].index(item)


def run_steps(engine, step):
    base, counts, last = 0, [0, 0], None

    def written(steps):
        nonlocal base, counts, last
        for s, flags in steps:
            step(Step(s, flags, last, base, tuple(counts)), s % 2)
            base += n_items(flags)
            counts = [counts[w] + n_items(flags, w) for w in (DVE, ACTE)]
            last = flags

    written(HEAD)
    n, each = n_items(FULL), [n_items(FULL, w) for w in (DVE, ACTE)]
    assert base % 2 == 0 and n % 2 == 0
    with engine.Fori(0, (LOOP1 - LOOP0) // 2) as i:
        for k in range(2):
            step(Step(i * 2 + LOOP0 + k, FULL, FULL, i * (2 * n) + base + k * n,
                      tuple(i * (2 * each[w]) + counts[w] + k * each[w] for w in (DVE, ACTE))), (LOOP0 + k) % 2)
    base += n * (LOOP1 - LOOP0)
    counts = [counts[w] + each[w] * (LOOP1 - LOOP0) for w in (DVE, ACTE)]
    written(TAIL)


DVE_JOBS = {(2, 0): [("RECIP", 0)], (2, 1): [("RECIP", 1)], (2, 2): [("RECIP", 2)], (2, 3): [("RECIP", 3)],
            (3, 1): [("SILU", 0)], (3, 2): [("SILU", 1)], (3, 4): [("SILU", 2)], (3, 5): [("SILU", 3)],
            (4, 0): [("RECIP", 4)], (4, 1): [("RECIP", 5)], (4, 2): [("RECIP", 6)], (4, 3): [("RECIP", 7)],
            (4, 4): [("TOKEN", 0)], (4, 5): [("TOKEN", 1)], (5, 1): [("TOKEN", 2)],
            (5, 2): [("OUT", 0)], (5, 5): [("OUT", 1)]}


def attention_stage(nc, ctx, io, keep):
    def sb(name, shape, dt=F32):
        return ctx.enter_context(nc.sbuf_tensor(name, shape, dt))

    def sem(name):
        return ctx.enter_context(nc.semaphore(name))

    psum, ident = keep["psum"], keep["ident"]
    scores_ps = psum[:, 0:4, :].rearrange("p (h b) c -> p h (b c)", h=2)
    out_ps = psum[:, 4:6, :].rearrange("p b c -> p (b c)")
    work = [psum[:, 6, :], psum[:, 7, :]]

    q_full = sb("q_full", [P, 2, 2, N], F32R)
    q_rest = sb("q_rest", [DK + 1, 2, 2, N], F32R)
    k_full = sb("k_full", [P, 2, 2, N], F32R)
    k_rest = sb("k_rest", [DK + 1, 2, 2, N], F32R)
    high = sb("high", [P, 2, 2, N], F32R)
    low = sb("low", [P, 2, 2, N], F32R)
    x_t = sb("x_t", [P, 2, KD, N], F32R)
    w_qk = sb("w_qk", [P, 2, 2, 2, KD, P], F32R)
    bias = sb("bias", [P, 2, 2])
    v_sb = sb("v_sb", [P, 2, KT, P])
    probs = sb("probs", [P, 2, 2, N])
    sums = sb("sums", [P, 2, 2, N])
    out_raw = sb("out_raw", [P, N])
    sum_all = sb("sum_all", [P, N])
    recip = sb("recip", [P, N])
    out_t = sb("out_t", [P, N])
    ones = sb("ones", [P, DK])
    maxima = sb("maxima", [P, 2 * KT, 2])
    merged = sb("merged", [P, 2 * KT])
    minus_max = sb("minus_max", [KT, 2, P], F32R)
    w_gu = sb("w_gu", [P, 2, KD, 2 * F])
    w_d0 = sb("w_d0", [P, 2, D])
    w_d1 = sb("w_d1", [F2, 2, D])
    count_slot = sb("count_slot", [P, 1], U32)
    count_rows = sb("count_rows", [P, P])
    is_before = sb("is_before", [P, P])
    n_before = sb("n_before", [P, 1])
    token = sb("token", [P, 2], U32)
    x_e = sb("x_e", [P, 2, ROW])
    x_et = sb("x_et", [P, KD, P])
    gate_up = sb("gate_up", [P, 2 * F])
    exp_g = sb("exp_ge", [P, F])
    silu = sb("silu_e", [P, F])
    hidden = sb("hidden_e", [P, F])
    hidden_t0 = sb("hidden_t0", [P, P])
    hidden_t1 = sb("hidden_t1", [F2, P])
    y_e = sb("y_e", [P, 2, D])

    set_up = sem("set_up")
    standing = sem("standing")
    x_loaded = sem("xt_loaded")
    w_loaded = sem("w_loaded")
    v_loaded = sem("v_loaded")
    highs_ready = sem("highs_ready")
    placed = sem("placed")
    shift_placed = sem("shift_placed")
    scores_ready = sem("scores_ready")
    probs_ready = sem("probs_ready")
    pv_done = sem("pv_done")
    out_copied = sem("out_copied")
    sums_added = sem("sums_added")
    out_ready = sem("out_ready")
    out_stored = sem("out_stored")
    work_filled = sem("work_filled")
    emptied = (sem("emptied_by_dve"), sem("emptied_by_act"))
    maxima_merged = sem("maxima_merged")
    experts_loaded = sem("experts_loaded")
    slot_copied = sem("slot_copied")
    counts_loaded = sem("counts_loaded")
    tokens_vec = sem("tokens_vec")
    tokens_ready = sem("tokens_ready")
    tokens_loaded = sem("tokens_loaded")
    gate_ready = sem("gate_ready")
    silu_vec = sem("silu_vec")
    hidden_ready = sem("hidden_e_ready")
    recip_ready = sem("recip_ready")
    scattered = sem("scattered")

    block = ctx.enter_context(nc.Block())
    SHUFFLES = 12

    @block.tensor
    def _(pe):
        pe.wait_ge(set_up, 3)

        def score(s, par, kt, h, part):
            n = 16 * s + 2 * kt + h
            if kt == 0 and h == 0:
                if part == 0:
                    pe.wait_ge(placed, DMA * SHUFFLES * (s + 1))
                else:
                    pe.wait_ge(shift_placed, DMA * 2 * (s + 1))
            if part == 0 and not known(n, 2):
                pe.wait_ge(probs_ready, n - 1)
            keys = slice(kt * P, (kt + 1) * P)
            k, q, rows = ((k_full, q_full, P), (k_rest, q_rest, DK + 1))[part]
            for half in range(2):
                cols = slice(half * HALF, (half + 1) * HALF)
                last = nc.tensor.matmul(scores_ps[:, h, cols], k[0:rows, par, h, keys], q[0:rows, par, h, cols],
                                        start=(part == 0), stop=(part == 1))
            if part == 1:
                last.then_inc(scores_ready, 1)

        def pv(p, par, kt, half):
            if half == 0:
                pe.wait_ge(probs_ready, 16 * p + 2 * kt + 2)
                if kt == 0:
                    pe.wait_ge(v_loaded, DMA * (p + 1))
                    if not known(p, 1):
                        pe.wait_ge(out_copied, p)
            cols = slice(half * HALF, (half + 1) * HALF)
            for h in range(2):
                rows = slice(DK * h, DK * (h + 1))
                last = nc.tensor.matmul(out_ps[rows, cols], v_sb[:, par, kt, rows], probs[:, h, kt % 2, cols],
                                        start=(kt == 0), stop=(kt == KT - 1))
            if half == 1:
                last.then_inc(pv_done, 1)

        def item(st, par, k, what):
            s = st.s
            out = work[k % 2]
            kind = what[0]
            if k >= 2 or st.last:
                pe.wait_ge(*st.emptied(emptied, k - 2))
            if kind == "PJ":
                which, half = what[1] // 2, what[1] % 2
                cols = slice(half * HALF, (half + 1) * HALF)
                if what[1] == 0:
                    pe.wait_ge(x_loaded, DMA * (s + 3))
                    pe.wait_ge(w_loaded, 2 * DMA * (s + 3))
                terms = [(HIGH, HIGH), (LOW, HIGH), (HIGH, LOW)]
                for j, (wp, xp) in enumerate(terms):
                    for kd in range(KD):
                        last = nc.tensor.matmul(out, w_qk[:, par, which, wp, kd, :], x_t[:, xp, kd, cols],
                                                start=(j == 0 and kd == 0), stop=(j == 2 and kd == KD - 1))
            elif kind == "MAX":
                _, h, qt, half = what
                rows = slice(DK * h, DK * (h + 1))
                if (h, qt, half) == (0, 0, 0):
                    pe.wait_ge(highs_ready, 4 * (s + 2))
                last = nc.tensor.matmul(out, high[rows, 1 - par, 0, qt * P:(qt + 1) * P],
                                        high[rows, 1 - par, 1, half * HALF:(half + 1) * HALF], start=True, stop=True)
            elif kind == "MT":
                h = what[1]
                pe.wait_ge(maxima_merged, 2 * (s + 1) + h + 1)
                last = nc.tensor.matmul(out[0:KT, 0:P], merged[:, h * KT:(h + 1) * KT], ident[:],
                                        start=True, stop=True)
            elif kind == "SUM":
                cols = slice(what[1] * HALF, (what[1] + 1) * HALF)
                if what[1] == 0:
                    pe.wait_ge(sums_added, 14 * s)
                for h in range(2):
                    last = nc.tensor.matmul(out[DK * h:DK * (h + 1), :], ones[:], sums[:, 1 - par, h, cols],
                                            start=True, stop=True)
            elif kind == "XT":
                pe.wait_ge(tokens_loaded, DMA * (s + 1))
                for kd in range(KD):
                    last = nc.tensor.transpose(out[:, kd * P:(kd + 1) * P], x_e[:, par, kd * P:(kd + 1) * P], ident[:])
            elif kind == "GU":
                pe.wait_ge(experts_loaded, 4 * DMA * (s + 1))
                pe.wait_ge(*st.emptied(emptied, st.at(("XT",))))
                for kd in range(KD):
                    last = nc.tensor.matmul(out[:, 0:2 * F], x_et[:, kd, :], w_gu[:, par, kd, :],
                                            start=(kd == 0), stop=(kd == KD - 1))
            elif kind == "HT":
                pe.wait_ge(hidden_ready, s + 1)
                nc.tensor.matmul(out[:, 0:P], hidden[:, 0:P], ident[:], start=True, stop=True)
                last = nc.tensor.matmul(out[0:F2, P:2 * P], hidden[:, P:F], ident[:], start=True, stop=True)
            elif kind == "DN":
                pe.wait_ge(*st.emptied(emptied, st.at(("HT",))))
                nc.tensor.matmul(out[:, 0:D], hidden_t0[:], w_d0[:, par, :], start=True, stop=False)
                last = nc.tensor.matmul(out[:, 0:D], hidden_t1[:], w_d1[:, par, :], start=False, stop=True)
            last.then_inc(work_filled, 1)

        def step(st, par):
            s, (fin, att, nxt, prj) = st.s, st.flags
            k = 0
            for kt in range(KT):
                for part in range(PARTS):
                    if part < 4 and att:
                        score(s, par, kt, part // 2, part % 2)
                    elif part >= 4 and kt == 0 and fin:
                        pv(s - 1, 1 - par, KT - 1, part - 4)
                    elif part >= 4 and kt > 0 and att:
                        pv(s, par, kt - 1, part - 4)
                    while k < len(st.items) and st.items[k][:2] == (kt, part):
                        item(st, par, k, st.items[k][2])
                        k += 1

        run_steps(pe, step)

    @block.scalar
    def _(act):
        def read(st, par, k, what):
            s, bank, kind = st.s, work[k % 2], what[0]
            if EMPTIED_BY[kind] == ACTE or kind == "PJ":
                act.wait_ge(work_filled, st.base + k + 1)
            if kind == "PJ":
                which, half = what[1] // 2, what[1] % 2
                if what[1] == 0 and not known(s, 0):
                    act.wait_ge(placed, DMA * SHUFFLES * (s + 1))
                nc.scalar.activation(high[:, par, which, half * HALF:(half + 1) * HALF], bank,
                                     ACT.Identity, bias=bias[:, par, which:which + 1]
                                     ).then_inc(highs_ready, 1)
            elif kind == "SUM":
                nc.scalar.copy(sum_all[:, what[1] * HALF:(what[1] + 1) * HALF], bank).then_inc(emptied[ACTE], 1)
            elif kind == "XT":
                nc.scalar.copy(x_et[:].rearrange("p k c -> p (k c)"), bank[:, 0:D]).then_inc(emptied[ACTE], 1)
            elif kind == "GU":
                nc.scalar.activation(exp_g[:], bank[:, 0:F], ACT.Exp, scale=-1.0).then_inc(gate_ready, 1)
                nc.scalar.copy(gate_up[:], bank[:, 0:2 * F]).then_inc(emptied[ACTE], 1)
            elif kind == "HT":
                nc.scalar.copy(hidden_t0[:], bank[:, 0:P])
                nc.scalar.copy(hidden_t1[:], bank[0:F2, P:2 * P]).then_inc(emptied[ACTE], 1)
            elif kind == "DN":
                if not known(s, 2):
                    act.wait_ge(scattered, DMA * (s - 1))
                nc.scalar.activation(y_e[:, par, :], bank[:, 0:D], ACT.Copy, scale=x_e[:, par, bass.ds(s + D, 1)]
                                     ).then_inc(emptied[ACTE], 1)

        def step(st, par):
            s, (fin, att, nxt, prj) = st.s, st.flags
            k = 0
            for kt in range(KT):
                for part in range(PARTS):
                    if part in (1, 3) and att:
                        h = part // 2
                        act.wait_ge(scores_ready, 16 * s + 2 * kt + h + 1)
                        if not (isinstance(s, int) and s == 0 and kt < 2):
                            act.wait_ge(pv_done, 8 * s + kt - 1)
                            added = 14 * s + (2 * (kt - 3) + h if kt >= 3 else h if kt == 2 else
                                              2 * (kt + 5) + h - 14)
                            act.wait_ge(sums_added, added + 1)
                        nc.scalar.activation(probs[:, h, kt % 2, :], scores_ps[:, h, :], ACT.Exp, scale=SCALE
                                             ).then_inc(probs_ready, 1)
                    while k < len(st.items) and st.items[k][:2] == (kt, part):
                        read(st, par, k, st.items[k][2])
                        k += 1
                if kt == 0 and fin:
                    act.wait_ge(pv_done, 8 * s)
                    if not known(s, 2):
                        act.wait_ge(out_ready, s - 1)
                    nc.scalar.copy(out_raw[:], out_ps).then_inc(out_copied, 1)

        run_steps(act, step)

    @block.vector
    def _(dve):
        nc.vector.memset(ones[:], 1.0).then_inc(set_up, 1)
        nc.vector.memset(f32(k_rest[DK:DK + 1, :, :, :]), 1.0).then_inc(set_up, 1)
        dve.wait_ge(set_up, 2)
        nc.vector.memset(maxima[:], 0.0).then_inc(set_up, 1)

        def read(st, par, k, what):
            s, bank, kind = st.s, work[k % 2], what[0]
            if EMPTIED_BY[kind] != DVE:
                return
            if kind == "MT":
                h = what[1]
                tiles = slice(h * KT, (h + 1) * KT)
                dve.wait_ge(*st.emptied(emptied, st.at(("MAX", h, KT - 1, 1))))
                nc.vector.tensor_reduce(out=merged[:, tiles], in_=maxima[:, tiles, :], axis=AX, op=ALU.max
                                        ).then_inc(maxima_merged, 1)
            dve.wait_ge(work_filled, st.base + k + 1)
            if kind == "PJ":
                which, half = what[1] // 2, what[1] % 2
                cols = slice(half * HALF, (half + 1) * HALF)
                dve.wait_ge(highs_ready, 4 * (s + 2) + what[1] + 1)
                last = nc.vector.scalar_tensor_tensor(
                    out=low[:, par, which, cols], in0=bank, scalar=bias[:, par, which:which + 1],
                    in1=f32(high[:, par, which, cols]), op0=ALU.add, op1=ALU.subtract)
            elif kind == "MAX":
                _, h, qt, half = what
                last = nc.vector.tensor_reduce(out=maxima[:, h * KT + qt, half:half + 1], in_=bank, axis=AX,
                                               op=ALU.max)
            elif kind == "MT":
                if h == 0 and not known(s, 0):
                    dve.wait_ge(shift_placed, 2 * DMA * (s + 1))
                last = nc.vector.tensor_scalar(minus_max[:, h, :], bank[0:KT, 0:P], -1.0, None, ALU.mult)
            last.then_inc(emptied[DVE], 1)

        def job(st, par, what):
            s, (kind, n) = st.s, what
            if kind == "RECIP":
                if n % 4 == 0:
                    dve.wait_ge(*st.emptied(emptied, st.at(("SUM", n // 4))))
                cols = slice(n * P, (n + 1) * P)
                last = nc.vector.reciprocal(recip[:, cols], sum_all[:, cols]).then_inc(recip_ready, 1)
            elif kind == "OUT":
                cols = slice(n * HALF, (n + 1) * HALF)
                if n == 0:
                    dve.wait_ge(recip_ready, 8 * s)
                    dve.wait_ge(out_copied, s)
                    if not known(s, 2):
                        dve.wait_ge(out_stored, DMA * (s - 1))
                last = nc.vector.tensor_tensor(out_t[:, cols], out_raw[:, cols], recip[:, cols], ALU.mult)
                if n == 1:
                    last.then_inc(out_ready, 1)
            elif kind == "SILU":
                if n == 0:
                    dve.wait_ge(*st.emptied(emptied, st.at(("GU",))))
                    nc.vector.tensor_scalar(silu[:], exp_g[:], 1.0, None, ALU.add).then_inc(silu_vec, 1)
                    return
                dve.wait_ge(silu_vec, 3 * s + n)
                if n == 1:
                    nc.vector.reciprocal(silu[:], silu[:]).then_inc(silu_vec, 1)
                elif n == 2:
                    nc.vector.tensor_tensor(silu[:], gate_up[:, 0:F], silu[:], ALU.mult).then_inc(silu_vec, 1)
                else:
                    nc.vector.tensor_tensor(hidden[:], gate_up[:, F:2 * F], silu[:], ALU.mult
                                            ).then_inc(hidden_ready, 1)
            elif kind == "TOKEN":
                e = s + 1
                if n == 0:
                    dve.wait_ge(counts_loaded, DMA * (s + 2))
                    nc.vector.tensor_scalar(is_before[:], count_rows[:], keep["rank"][:, bass.ds(e, 1)], None,
                                            ALU.is_le).then_inc(tokens_vec, 1)
                    return
                dve.wait_ge(tokens_vec, 2 * s + 2 + n)
                if n == 1:
                    nc.vector.tensor_reduce(out=n_before[:], in_=is_before[:], axis=AX, op=ALU.add
                                            ).then_inc(tokens_vec, 1)
                else:
                    if not known(s, 1):
                        dve.wait_ge(scattered, DMA * s)
                    nc.vector.tensor_scalar(token[:, 1 - par:2 - par], n_before[:], keep["valid"][:, bass.ds(e, 1)],
                                            keep["first"][:, bass.ds(e, 1)], ALU.mult, ALU.add
                                            ).then_inc(tokens_ready, 1)

        needs = {"RECIP": 0, "OUT": 0, "SILU": 1, "TOKEN": 2}

        def step(st, par):
            k = 0
            for kt in range(KT):
                for part in range(PARTS):
                    for what in DVE_JOBS.get((kt, part), ()):
                        if st.flags[needs[what[0]]]:
                            job(st, par, what)
                    while k < len(st.items) and st.items[k][:2] == (kt, part):
                        read(st, par, k, st.items[k][2])
                        k += 1

        run_steps(dve, step)

    @block.gpsimd
    def _(pool):
        nc.gpsimd.memset(is_before[:], 0.0).then_inc(standing, 1)

        def step(st, par):
            s, (fin, att, nxt, prj) = st.s, st.flags
            if nxt:
                if not known(s, 0):
                    pool.wait_ge(tokens_ready, s + 1)
                nc.gpsimd.tensor_copy(count_slot[:], keep["count_row"][:, bass.ds(s + 1, 1)]).then_inc(slot_copied, 1)
                alone(pool, (standing, 1), (slot_copied, s + 2))
                nc.gpsimd.indirect_dma_start(
                    out=count_rows[:], out_offset=None, in_=io["counts"],
                    in_offset=bass.IndirectOffsetOnAxis(ap=count_slot[:, 0:1], axis=0)).then_inc(counts_loaded, DMA)
            for kt in range(1, KT) if att else ():
                for h in range(2):
                    pool.wait_ge(probs_ready, 16 * s + 2 * kt + h + 1)
                    if kt == 1:
                        if not known(s, 2):
                            pool.wait_ge(out_ready, s - 1)
                        first = probs[:, h, 0, :]
                    else:
                        first = sums[:, par, h, :]
                        pool.wait_ge(sums_added, 14 * s + 2 * (kt - 2) + h + 1)
                    nc.gpsimd.tensor_tensor(sums[:, par, h, :], first, probs[:, h, kt % 2, :], ALU.add
                                            ).then_inc(sums_added, 1)
                if kt == 5 and nxt:
                    fetch(s, par)
            if nxt and not att:
                fetch(s, par)
            if att:
                waits = [st.emptied(emptied, st.at(("DN",)))]
                if not known(s, 1):
                    waits.append((scattered, DMA * s))
                alone(pool, (standing, 1), *waits)
                nc.gpsimd.indirect_dma_start(
                    out=io["moe"], out_offset=bass.IndirectOffsetOnAxis(ap=token[:, par:par + 1], axis=0),
                    in_=y_e[:, par, :], in_offset=None, compute_op=ALU.add).then_inc(scattered, DMA)

        def fetch(s, par):
            alone(pool, (standing, 1), (tokens_ready, s + 2))
            nc.gpsimd.indirect_dma_start(
                out=x_e[:, 1 - par, :], out_offset=None, in_=io["rows"],
                in_offset=bass.IndirectOffsetOnAxis(ap=token[:, 1 - par:2 - par], axis=0)
            ).then_inc(tokens_loaded, DMA)

        run_steps(pool, step)
        pool.wait_ge(scattered, DMA * NP)

    @block.sync
    def _(sp):
        def one(ap, i, pattern, out):
            return ap[bass.ds(i, 1)].rearrange(f"o {pattern} -> {out}", p=P)

        def load_projection(p, par):
            sp.dma_start(f32(x_t[:]), one(io["xt"], p // PAIRS, "p a k c", "(o p) a k c")).then_inc(x_loaded, DMA)
            hp = p % PAIRS
            sp.dma_start(f32(w_qk[:, par]), one(io["wqk"], hp, "p w a k c", "(o p) w a k c")).then_inc(w_loaded, DMA)
            sp.dma_start(bias[:, par, :], one(io["bqk"], hp, "p w", "(o p) w")).then_inc(w_loaded, DMA)

        load_projection(0, 0)

        def step(st, par):
            s, (fin, att, nxt, prj) = st.s, st.flags
            if nxt:
                p, pp = s + 1, 1 - par
                e = p
                if att:
                    waits = [(placed, DMA * SHUFFLES * (s + 1)), (v_loaded, DMA * (s + 1)),
                             (experts_loaded, 4 * DMA * (s + 1)), (shift_placed, 2 * DMA * (s + 1))]
                    if fin:
                        waits.append((pv_done, 8 * s))
                    alone(sp, (standing, 1), *waits)
                sp.dma_start(v_sb[:, pp], one(io["v"], p, "p t c", "(o p) t c")).then_inc(v_loaded, DMA)
                if known(st.counts[ACTE], 1):
                    sp.wait_ge(emptied[DVE], st.counts[DVE])
                else:
                    alone(sp, (standing, 1), (emptied[DVE], st.counts[DVE]), (emptied[ACTE], st.counts[ACTE]))
                for h in range(2):
                    rows = slice(DK * h, DK * (h + 1))
                    top, bottom = slice(0, DK), slice(DK, P)
                    for dst, to, src, which in ((k_full, top, high, 1), (k_full, bottom, high, 1),
                                                (q_full, top, high, 0), (q_full, bottom, low, 0),
                                                (k_rest, top, low, 1), (q_rest, top, high, 0)):
                        sp.dma_start(f32(dst[to, pp, h, :]), f32(src[rows, pp, which, :])).then_inc(placed, DMA)
                sp.dma_start(w_gu[:, pp, :, 0:F], one(io["w_gate"], e, "(k p) f", "p (o k) f")
                             ).then_inc(experts_loaded, DMA)
                sp.dma_start(w_gu[:, pp, :, F:2 * F], one(io["w_up"], e, "(k p) f", "p (o k) f")
                             ).then_inc(experts_loaded, DMA)
                sp.dma_start(w_d0[:, pp, :], io["w_down"][bass.ds(e, 1), 0:P, :].rearrange("o p d -> (o p) d")
                             ).then_inc(experts_loaded, DMA)
                sp.dma_start(w_d1[:, pp, :], io["w_down"][bass.ds(e, 1), P:F, :].rearrange("o p d -> (o p) d")
                             ).then_inc(experts_loaded, DMA)
            if fin:
                if known(s, 2):
                    sp.wait_ge(out_ready, s)
                else:
                    alone(sp, (standing, 1), (out_stored, DMA * (s - 1)), (out_ready, s))
                sp.dma_start(one(io["ot"], s - 1, "p c", "(o p) c"), out_t[:]).then_inc(out_stored, DMA)
            if prj and not (isinstance(s, int) and s == NP - 3):
                alone(sp, (standing, 1), (x_loaded, DMA * (s + 3)), (w_loaded, 2 * DMA * (s + 3)),
                      st.emptied(emptied, st.at(("PJ", 3))))
                load_projection(s + 3, 1 - par)
            if nxt:
                for h in range(2):
                    sp.wait_ge(*st.emptied(emptied, st.at(("MT", h))))
                    sp.dma_start(f32(q_rest[DK:DK + 1, 1 - par, h, :]), f32(minus_max[:, h, :])
                                 ).then_inc(shift_placed, DMA)

        run_steps(sp, step)
        sp.wait_ge(out_stored, DMA * NP)


def output_stage(nc, ctx, io, keep):
    def sb(name, shape, dt=F32):
        return ctx.enter_context(nc.sbuf_tensor(name, shape, dt))

    def sem(name):
        return ctx.enter_context(nc.semaphore(name))

    psum = keep["psum"]
    wo = sb("wo", [P, PAIRS, D])
    bv = sb("bv", [P, PAIRS])
    bv_wide = sb("bv_wide", [P, PAIRS, P])
    bo = sb("bo", [1, D])
    ones_o = sb("ones_o", [P, P])
    const = sb("const", [P, UNIT, D])
    ot = sb("ot_sb", [P, 2, PAIRS, HALF])
    x_in = sb("x_out", [P, 2, UNIT, D])
    moe = sb("moe_sb", [P, 2, UNIT, D])
    rest = sb("rest", [P, 2, UNIT, D])
    y = sb("y", [P, 2, UNIT, D])

    loaded_w = sem("loaded_w")
    ones_set = sem("ones_set")
    bv_ready = sem("bv_ready")
    const_filled = sem("const_filled")
    const_ready = sem("const_ready")
    ot_loaded = sem("ot_loaded")
    xm_loaded = sem("xm_loaded")
    part_ready = sem("part_ready")
    rest_ready = sem("rest_ready")
    y_filled = sem("y_filled")
    y_ready = sem("y_ready")
    y_stored = sem("y_stored")
    block = ctx.enter_context(nc.Block())

    x_v = io["x"].rearrange("(u t p) d -> u p t d", p=P, t=UNIT)
    moe_v = io["moe"][0:T, :].rearrange("(u t p) d -> u p t d", p=P, t=UNIT)
    out_v = io["out"].rearrange("(u t p) d -> u p t d", p=P, t=UNIT)
    parts = "o p t d -> (o p) t d"

    def rounds(engine, unit):
        unit(0, 0)
        unit(0, 1)
        with engine.Fori(1, UNITS // 2) as i:
            unit(i, 0)
            unit(i, 1)

    def early(u):
        return isinstance(u, int) and u < 2

    @block.sync
    def _(sp):
        sp.dma_start(wo[:], io["wo"].rearrange("(h p) d -> p h d", p=P)).then_inc(loaded_w, DMA)
        sp.dma_start(bv[:], io["bv"]).then_inc(loaded_w, DMA)
        sp.dma_start(bo[:], io["bo"]).then_inc(loaded_w, DMA)

        def unit(i, par):
            u = i * 2 + par
            waits = [(ot_loaded, DMA * u), (xm_loaded, 2 * DMA * u)] if not known(u, 1) else []
            if not early(u):
                waits += [(y_filled, 2 * (u - 1)), (rest_ready, u - 1)]
            if waits:
                alone(sp, (loaded_w, 3 * DMA), *waits)
            sp.dma_start(ot[:, par], io["ot"][bass.ds(i * PAIRS, PAIRS), :, par * HALF:(par + 1) * HALF]
                         .rearrange("h p c -> p h c")).then_inc(ot_loaded, DMA)
            sp.dma_start(x_in[:, par], x_v[bass.ds(u, 1)].rearrange(parts)).then_inc(xm_loaded, DMA)
            sp.dma_start(moe[:, par], moe_v[bass.ds(u, 1)].rearrange(parts)).then_inc(xm_loaded, DMA)

        rounds(sp, unit)

    @block.gpsimd
    def _(pool):
        nc.gpsimd.memset(ones_o[:], 1.0).then_inc(ones_set, 1)
        pool.wait_ge(const_ready, 2)

        def unit(i, par):
            u = i * 2 + par
            pool.wait_ge(xm_loaded, 2 * DMA * (u + 1))
            if not early(u):
                pool.wait_ge(y_ready, 2 * (u - 1))
            nc.gpsimd.tensor_tensor(rest[:, par], x_in[:, par], moe[:, par], ALU.add).then_inc(part_ready, 1)
            pool.wait_ge(part_ready, u + 1)
            nc.gpsimd.tensor_tensor(rest[:, par], rest[:, par], const[:], ALU.add).then_inc(rest_ready, 1)

        rounds(pool, unit)

    @block.vector
    def _(dve):
        dve.wait_ge(loaded_w, 3 * DMA)
        dve.wait_ge(ones_set, 1)
        for h in range(PAIRS):
            last = nc.vector.tensor_scalar(bv_wide[:, h, :], ones_o[:], bv[:, h:h + 1], None, ALU.mult)
        last.then_inc(bv_ready, 1)
        dve.wait_ge(const_filled, 1)
        for half in range(2):
            nc.vector.tensor_copy(const[:, 2 * half:2 * half + 2, :],
                                  psum[:, 0, :].rearrange("p (t d) -> p t d", d=D)).then_inc(const_ready, 1)

        def unit(i, par):
            u = i * 2 + par
            dve.wait_ge(rest_ready, u + 1)
            if not early(u):
                dve.wait_ge(y_stored, DMA * (u - 1))
            for n in range(2):
                dve.wait_ge(y_filled, 2 * u + n + 1)
                nc.vector.tensor_tensor(y[:, par, 2 * n:2 * n + 2, :],
                                        psum[:, 2 + 2 * par + n, :].rearrange("p (t d) -> p t d", d=D),
                                        rest[:, par, 2 * n:2 * n + 2, :], ALU.add).then_inc(y_ready, 1)

        rounds(dve, unit)

    @block.tensor
    def _(pe):
        pe.wait_ge(bv_ready, 1)
        for t in range(2):
            cols = slice(t * D, (t + 1) * D)
            for h in range(PAIRS):
                nc.tensor.matmul(psum[:, 0, cols], bv_wide[:, h, :], wo[:, h, :], start=(h == 0), stop=False)
            last = nc.tensor.matmul(psum[:, 0, cols], ones_o[0:1, :], bo[:], start=False, stop=True)
        last.then_inc(const_filled, 1)

        def unit(i, par):
            u = i * 2 + par
            pe.wait_ge(ot_loaded, DMA * (u + 1))
            if not early(u):
                pe.wait_ge(y_ready, 2 * (u - 1))
            for n in range(2):
                for t in range(2):
                    tok = slice((2 * n + t) * P, (2 * n + t + 1) * P)
                    for h in range(PAIRS):
                        last = nc.tensor.matmul(psum[:, 2 + 2 * par + n, t * D:(t + 1) * D], ot[:, par, h, tok],
                                                wo[:, h, :], start=(h == 0), stop=(h == PAIRS - 1))
                last.then_inc(y_filled, 1)

        rounds(pe, unit)

    @block.scalar
    def _(act):
        def unit(i, par):
            u = i * 2 + par
            if not known(u, 1):
                act.wait_ge(y_stored, DMA * u)
            act.wait_ge(y_ready, 2 * (u + 1))
            act.dma_start(out_v[bass.ds(u, 1)].rearrange(parts), y[:, par]).then_inc(y_stored, DMA)

        rounds(act, unit)
        act.wait_ge(y_stored, DMA * UNITS)


def build(nc, io):
    def dram(name, shape):
        return nc.dram_tensor(name, shape, F32, kind="Internal").ap()

    io["rows"] = dram("rows", [T + C, ROW])
    io["moe"] = dram("moe", [T + C, D])
    io["xt"] = dram("xt", [B, P, 2, KD, N])
    io["v"] = dram("v", [NP, P, KT, P])
    io["wqk"] = dram("wqk_parts", [PAIRS, P, 2, 2, KD, P])
    io["counts"] = dram("counts_rows", [TILES * E, P])
    io["ot"] = dram("ot", [NP, P, N])
    with ExitStack() as ctx:
        keep = {
            "psum": ctx.enter_context(nc.psum_tensor("psum", [P, 8, HALF], F32)),
            "ident": ctx.enter_context(nc.sbuf_tensor("ident", [P, P], F32)),
        }
        for name in ("rank", "valid", "first"):
            keep[name] = ctx.enter_context(nc.sbuf_tensor(name, [P, E], F32))
        keep["count_row"] = ctx.enter_context(nc.sbuf_tensor("count_row", [P, E], U32))
        with ExitStack() as mctx:
            keep["masks"] = mctx.enter_context(nc.sbuf_tensor("masks", [P, TILES, E], BF16))
            with ExitStack() as sub:
                norm_stage(nc, sub, io, keep)
            with ExitStack() as sub:
                table_stage(nc, sub, io, keep)
        with ExitStack() as sub:
            attention_stage(nc, sub, io, keep)
        with ExitStack() as sub:
            output_stage(nc, sub, io, keep)


def kernel(**inputs):
    import numpy as np
    import concourse.bacc as bacc
    from concourse.bass_utils import run_bass_kernel_spmd

    a = {k.replace("L0_", ""): np.asarray(v) for k, v in inputs.items()}
    arrays = {
        "x": a["attn_y"].reshape(T, D),
        "wq": a["attn_Wq"].T, "wk": a["attn_Wk"].T, "wv": a["attn_Wv"].T, "wo": a["attn_Wo"].T,
        "bqk": np.stack([a["attn_bq"].reshape(PAIRS, P), a["attn_bk"].reshape(PAIRS, P)], axis=-1),
        "bv": a["attn_bv"].reshape(PAIRS, P).T, "bo": a["attn_bo"].reshape(1, D),
        "router": a["ffn_router_w"].T, "w_gate": a["ffn_w_gate"], "w_up": a["ffn_w_up"],
        "w_down": a["ffn_w_down"], "ws_gu": a["ffn_ws_gate_up"], "ws_d": a["ffn_ws_down"],
    }
    nc = bacc.Bacc("TRN2", target_bir_lowering=False, num_devices=1)
    io, feed = {}, {}
    for name, v in arrays.items():
        v = np.ascontiguousarray(v)
        feed[f"in_{name}"] = v
        io[name] = nc.dram_tensor(f"in_{name}", v.shape, F32, kind="ExternalInput").ap()
    io["out"] = nc.dram_tensor("out_y", (T, D), F32, kind="ExternalOutput").ap()
    build(nc, io)
    got = run_bass_kernel_spmd(nc, [feed], core_ids=[0])
    return got.results[0]["out_y"].reshape(B, N, D)
```

```python
from contextlib import ExitStack

import concourse.bass as bass
from concourse import mybir

F32 = mybir.dt.float32
F32R = mybir.dt.float32r
BF16 = mybir.dt.bfloat16
U32 = mybir.dt.uint32
ALU = mybir.AluOpType
ACT = mybir.ActivationFunctionType
AX = mybir.AxisListType.X

P = 128
B, N, D = 8, 1024, 256
T = B * N
H, DK = 16, 64
HD = H * DK
PAIRS = H // 2
NP = B * PAIRS
E, TOPK, F, C = 64, 8, 192, 128
F2 = F - P
KD = D // P
TILES = T // P
KT = N // P
ROW = D + E
EPS = 1e-5
SCALE = float(DK) ** -0.5
HALF = 512

UNIT = 4
UNITS = TILES // UNIT

HIGH, LOW = 0, 1
DMA = 16


def alone(engine, met, *waits):
    waits = [(sem, v if isinstance(v, int) else engine.to_reg(v)) for sem, v in waits]
    engine.wait_ge(*met)
    for sem, value in waits:
        engine.wait_ge(sem, value)


def known(v, least):
    return isinstance(v, int) and v < least


def f32(ap):
    return ap.bitcast(F32)


def norm_stage(nc, ctx, io, keep):
    def sb(name, shape, dt=F32):
        return ctx.enter_context(nc.sbuf_tensor(name, shape, dt))

    def sem(name):
        return ctx.enter_context(nc.semaphore(name))

    psum, ident, masks = keep["psum"], keep["ident"], keep["masks"]
    transposed_ps = psum[:, 0:2, :]
    router_ps = psum[:, 2, 0:UNIT * E]
    gate_ps, up_ps, down_ps = psum[:, 3, :], psum[:, 4, :], psum[:, 5, :]

    x_in = sb("x_in", [P, 2, UNIT, D])
    normed = sb("normed", [P, 2, UNIT, D])
    xt32 = sb("xt32", [P, 2, KD, HALF])
    xt_high = sb("xt_high", [P, 2, KD, HALF], F32R)
    xt_low = sb("xt_low", [P, 2, KD, HALF], F32R)
    values = sb("values", [P, 2, UNIT, HD])
    wv32 = sb("wv32", [P, KD, HD])
    wv = sb("wv", [P, 2, KD, HD], F32R)
    wqk = sb("wqk", [P, 2, KD, HD], F32R)
    router = sb("router", [P, KD, E])
    ws_gu32 = sb("ws_gu32", [P, KD, 2 * F])
    ws_gu = sb("ws_gu", [P, 2, KD, 2 * F], F32R)
    ws_d0 = sb("ws_d0", [P, D])
    ws_d1 = sb("ws_d1", [F2, D])
    stats = sb("stats", [P, UNIT, 6])
    meanvar = sb("meanvar", [P, UNIT, 2])
    var_eps = sb("var_eps", [P, UNIT])
    minus_half = sb("minus_half", [P, UNIT])
    rstd0 = sb("rstd0", [P, UNIT])
    newton = sb("newton", [P, UNIT])
    rstd = sb("rstd", [P, UNIT])
    row4 = sb("row4", [P, UNIT])
    logit = sb("logit", [P, UNIT, E])
    prob_e = sb("prob_e", [P, UNIT, E])
    prob = sb("prob", [P, UNIT, E])
    top = sb("top", [P, UNIT, TOPK])
    replaced = sb("replaced", [P, UNIT, E])
    chosen = sb("chosen", [P, UNIT, E])
    weight = sb("weight", [P, 2, UNIT, E])
    exp_g = sb("exp_g", [P, 2, HALF])
    silu = sb("silu", [P, 2, HALF])
    hidden0 = sb("hidden0", [P, HALF])
    hidden1 = sb("hidden1", [F2, HALF])
    up_rest = sb("up_rest", [F2, HALF])
    shared = sb("shared", [P, 2, UNIT, D])
    zeros = sb("zeros", [P, ROW])

    weights_in = sem("weights_in")
    wv_in = sem("wv_in")
    w_high = sem("w_high")
    w_low = sem("w_low")
    w_stored = sem("w_stored")
    ws_high = sem("ws_high")
    ws_low = sem("ws_low")
    ready = sem("ready")
    zeros_set = sem("zeros_set")
    x_loaded = sem("x_loaded")
    normed_ready = sem("normed_ready")
    var_ready = sem("var_ready")
    pow_ready = sem("pow_ready")
    vec = sem("vec")
    xt_filled = sem("xt_filled")
    xt_highs = sem("xt_highs")
    xt_lows = sem("xt_lows")
    router_filled = sem("router_filled")
    logits_ready = sem("logits_ready")
    exp_ready = sem("exp_ready")
    weight_ready = sem("weight_ready")
    gu_filled = sem("gu_filled")
    act_own = sem("act_own")
    exp_g_ready = sem("exp_g_ready")
    chosen_ready = sem("chosen_ready")
    mask_kept = sem("mask_kept")
    hidden_ready = sem("hidden_ready")
    down_filled = sem("down_filled")
    shared_ready = sem("shared_ready")
    v_filled = sem("v_filled")
    v_copied = sem("v_copied")
    normed_stored = sem("normed_stored")
    xt_stored = sem("xt_stored")
    weight_stored = sem("weight_stored")
    v_stored = sem("v_stored")
    shared_stored = sem("shared_stored")
    pads_stored = sem("pads_stored")

    x_v = io["x"].rearrange("(u t p) d -> u p t d", p=P, t=UNIT)
    rows_v = io["rows"][0:T, :].rearrange("(u t p) d -> u p t d", p=P, t=UNIT)
    moe_v = io["moe"][0:T, :].rearrange("(u t p) d -> u p t d", p=P, t=UNIT)

    block = ctx.enter_context(nc.Block())

    @block.sync
    def _(sp):
        def load_weights(n):
            if n:
                sp.wait_ge(w_low, n)
            sp.dma_start(wv32[:], io[("wv", "wq", "wk")[n]].rearrange("(k p) e -> p k e", p=P)).then_inc(wv_in, DMA)

        def store_weights(n):
            sp.wait_ge(w_high, n + 1)
            sp.wait_ge(w_low, n + 1)
            for part in range(2):
                for k in range(KD):
                    sp.dma_start(io["wqk"][:, :, n - 1, part, k, :].rearrange("h p c -> p h c"),
                                 f32(wqk[:, part, k, :]).rearrange("p (h c) -> p h c", c=P)
                                 ).then_inc(w_stored, DMA)

        sp.dma_start(x_in[:, 0], x_v[0]).then_inc(x_loaded, DMA)
        sp.dma_start(router[:], io["router"].rearrange("(k p) e -> p k e", p=P)).then_inc(weights_in, DMA)
        sp.dma_start(ws_gu32[:], io["ws_gu"].rearrange("(k p) e -> p k e", p=P)).then_inc(weights_in, DMA)
        sp.dma_start(ws_d0[:], io["ws_d"][0:P, :]).then_inc(weights_in, DMA)
        sp.dma_start(ws_d1[:], io["ws_d"][P:F, :]).then_inc(weights_in, DMA)
        load_weights(0)
        sp.wait_ge(x_loaded, DMA)
        sp.dma_start(x_in[:, 1], x_v[1]).then_inc(x_loaded, DMA)

        def unit(i, par, ahead):
            u = i * 2 + par
            if ahead:
                alone(sp, (x_loaded, DMA), (x_loaded, DMA * (u + 2)), (normed_ready, u + 1))
                sp.dma_start(x_in[:, par], x_v[bass.ds(u + 2, 1)].rearrange("o p t d -> (o p) t d")
                             ).then_inc(x_loaded, DMA)
            one = bass.ds(u, 1)

            def after(sem, per_unit, *wait):
                if known(u, 1):
                    sp.wait_ge(*wait)
                else:
                    alone(sp, (x_loaded, DMA), (sem, DMA * per_unit * u), wait)

            after(normed_stored, 1, normed_ready, u + 1)
            sp.dma_start(rows_v[one, :, :, 0:D].rearrange("o p t d -> (o p) t d"), normed[:, par]
                         ).then_inc(normed_stored, DMA)
            after(xt_stored, 4, xt_lows, u + 1)
            for part, tile in ((HIGH, xt_high), (LOW, xt_low)):
                for k in range(KD):
                    sp.dma_start(io["xt"][bass.ds(i, 1), :, part, k, par * HALF:(par + 1) * HALF]
                                 .rearrange("o p c -> (o p) c"), f32(tile[:, par, k, :])).then_inc(xt_stored, DMA)
            after(weight_stored, 1, weight_ready, u + 1)
            sp.dma_start(rows_v[one, :, :, D:ROW].rearrange("o p t d -> (o p) t d"), weight[:, par]
                         ).then_inc(weight_stored, DMA)
            for t in range(UNIT):
                if t == 0:
                    after(v_stored, UNIT, v_copied, (u * UNIT + t) * 2 + 2)
                else:
                    sp.wait_ge(v_copied, (u * UNIT + t) * 2 + 2)
                sp.dma_start(io["v"][bass.ds(i * PAIRS, PAIRS), :, par * UNIT + t, :].rearrange("h p c -> p h c"),
                             values[:, par, t, :].rearrange("p (h c) -> p h c", c=P)).then_inc(v_stored, DMA)
            after(shared_stored, 1, shared_ready, 2 * u + 2)
            sp.dma_start(moe_v[one].rearrange("o p t d -> (o p) t d"), shared[:, par]).then_inc(shared_stored, DMA)

        load_weights(1)
        unit(0, 0, True)
        store_weights(1)
        load_weights(2)
        sp.wait_ge(zeros_set, 1)
        sp.dma_start(io["rows"][T:T + C, :], zeros[:]).then_inc(pads_stored, DMA)
        sp.dma_start(io["moe"][T:T + C, :], zeros[:, 0:D]).then_inc(pads_stored, DMA)
        unit(0, 1, True)
        store_weights(2)
        with sp.Fori(1, UNITS // 2 - 1) as i:
            unit(i, 0, True)
            unit(i, 1, True)
        unit(UNITS // 2 - 1, 0, False)
        unit(UNITS // 2 - 1, 1, False)
        sp.wait_ge(w_stored, DMA * 8)
        sp.wait_ge(pads_stored, DMA * 2)
        sp.wait_ge(normed_stored, DMA * UNITS)
        sp.wait_ge(xt_stored, DMA * 4 * UNITS)
        sp.wait_ge(weight_stored, DMA * UNITS)
        sp.wait_ge(v_stored, DMA * UNIT * UNITS)
        sp.wait_ge(shared_stored, DMA * UNITS)

    @block.gpsimd
    def _(pool):
        nc.gpsimd.memset(zeros[:], 0.0).then_inc(zeros_set, 1)
        nc.gpsimd.memset(minus_half[:], -0.5).then_inc(ready, 1)
        nc.gpsimd.memset(ident[:], 0.0).then_inc(ready, 1)
        pool.wait_ge(ready, 2)
        nc.gpsimd.affine_select(out=ident[:], in_=ident[:], compare_op=ALU.not_equal, fill=1.0, base=0,
                                pattern=[[-1, P]], channel_multiplier=1).then_inc(ready, 1)

        def power(v):
            pool.wait_ge(var_ready, v + 1)
            nc.gpsimd.tensor_tensor(rstd0[:], var_eps[:], minus_half[:], ALU.pow).then_inc(pow_ready, 1)

        def low_part(v, par):
            pool.wait_ge(xt_highs, v + 1)
            if not known(v, 2):
                pool.wait_ge(xt_stored, DMA * 4 * (v - 1))
            nc.gpsimd.tensor_tensor(xt_low[:, par], xt32[:, par], f32(xt_high[:, par]), ALU.subtract
                                    ).then_inc(xt_lows, 1)

        def unit(i, par, more):
            u = i * 2 + par
            pool.wait_ge(chosen_ready, u + 1)
            nc.gpsimd.tensor_copy(masks[:, bass.ds(u * UNIT, UNIT), :], chosen[:]).then_inc(mask_kept, 1)
            if more:
                power(u + 1)
                low_part(u + 1, 1 - par)

        power(0)
        low_part(0, 0)
        unit(0, 0, True)
        unit(0, 1, True)
        with pool.Fori(1, UNITS // 2 - 1) as i:
            unit(i, 0, True)
            unit(i, 1, True)
        unit(UNITS // 2 - 1, 0, True)
        unit(UNITS // 2 - 1, 1, False)

    @block.scalar
    def _(act):
        def weight_high(n):
            act.wait_ge(wv_in, DMA * (n + 1))
            if n == 2:
                act.wait_ge(w_stored, DMA * 4)
            nc.scalar.copy((wv if n == 0 else wqk)[:, HIGH], wv32[:]).then_inc(w_high, 1)

        def shared_high():
            act.wait_ge(weights_in, DMA * 4)
            nc.scalar.copy(ws_gu[:, HIGH], ws_gu32[:]).then_inc(ws_high, 1)

        def copy_xt(v, par):
            act.wait_ge(xt_filled, v + 1)
            if not known(v, 2):
                act.wait_ge(xt_stored, DMA * 4 * (v - 1))
                act.wait_ge(down_filled, 2 * (v - 1))
            nc.scalar.copy(xt_high[:, par], transposed_ps)
            nc.scalar.copy(xt32[:, par], transposed_ps).then_inc(xt_highs, 1)

        def router_exp(u):
            act.wait_ge(logits_ready, u + 1)
            nc.scalar.activation(prob_e[:], logit[:], ACT.Exp).then_inc(exp_ready, 1)

        def unit(i, par, more, weights=None):
            u = i * 2 + par

            def values_out(lo, hi):
                for n in range(lo, hi):
                    act.wait_ge(v_filled, 8 * u + n + 1)
                    if n == 0 and not known(u, 2):
                        act.wait_ge(v_stored, DMA * UNIT * (u - 1))
                    nc.scalar.copy(values[:, par, n // 2, (n % 2) * HALF:(n % 2 + 1) * HALF],
                                   psum[:, 6 + n % 2, :]).then_inc(v_copied, 1)

            def one_plus_exp(c, rows):
                bank = down_ps if c else gate_ps
                act.wait_ge(gu_filled, 2 * u + c + 1)
                if not known(u, 1):
                    act.wait_ge(hidden_ready, 2 * (u - 1) + c + 1)
                nc.scalar.activation(exp_g[0:rows, c, :], bank[0:rows, :], ACT.Exp, scale=-1.0).then_inc(act_own, 1)
                act.wait_ge(act_own, 2 * u + c + 1)
                if c:
                    nc.scalar.copy(up_rest[:], bank[F2:P, :])
                nc.scalar.activation(exp_g[0:rows, c, :], exp_g[0:rows, c, :], ACT.Copy, bias=1.0
                                     ).then_inc(exp_g_ready, 1)

            one_plus_exp(0, P)
            values_out(0, 2)
            one_plus_exp(1, F2)
            values_out(2, 5)
            if more:
                copy_xt(u + 1, 1 - par)
            values_out(5, 8)
            if weights:
                weight_high(weights)
            if more:
                router_exp(u + 1)
            if not known(u, 2):
                act.wait_ge(shared_stored, DMA * (u - 1))
            for n in range(2):
                act.wait_ge(down_filled, 2 * u + n + 1)
                nc.scalar.copy(shared[:, par, 2 * n:2 * n + 2, :],
                               down_ps.rearrange("p (t d) -> p t d", d=D)).then_inc(shared_ready, 1)

        copy_xt(0, 0)
        shared_high()
        weight_high(0)
        router_exp(0)
        unit(0, 0, True, 1)
        unit(0, 1, True, 2)
        with act.Fori(1, UNITS // 2 - 1) as i:
            unit(i, 0, True)
            unit(i, 1, True)
        unit(UNITS // 2 - 1, 0, True)
        unit(UNITS // 2 - 1, 1, False)

    @block.vector
    def _(dve):
        NORM_LINKS, VEC = 7, 20

        def weight_low(n):
            part = wv if n == 0 else wqk
            dve.wait_ge(w_high, n + 1)
            nc.vector.tensor_tensor(part[:, LOW], wv32[:], f32(part[:, HIGH]), ALU.subtract).then_inc(w_low, 1)

        def linked(start, count):
            def link(ins, standing=False):
                count[0] += 1
                ins.then_inc(vec, 1)
                if standing:
                    alone(dve, (x_loaded, DMA), (vec, start + count[0]))
                else:
                    dve.wait_ge(vec, start + count[0])
            return link

        def norm(v, par, link):
            first = isinstance(v, int) and v < 2
            dve.wait_ge(x_loaded, DMA * (v + 1))
            for t in range(UNIT):
                last = nc.vector.bn_stats(out=stats[:, t, :], in_=x_in[:, par, t, :])
            link(last, True)
            for t in range(UNIT):
                last = nc.vector.bn_aggr(out=meanvar[:, t, :], in_=stats[:, t, :])
            link(last)
            link(nc.vector.tensor_scalar(var_eps[:], meanvar[:, :, 1], EPS, None, ALU.add))
            nc.vector.tensor_copy(row4[:], var_eps[:]).then_inc(var_ready, 1)
            dve.wait_ge(pow_ready, v + 1)
            link(nc.vector.tensor_tensor(newton[:], rstd0[:], rstd0[:], ALU.mult))
            link(nc.vector.tensor_tensor(newton[:], newton[:], var_eps[:], ALU.mult))
            link(nc.vector.tensor_scalar(newton[:], newton[:], -0.5, 1.5, ALU.mult, ALU.add))
            link(nc.vector.tensor_tensor(rstd[:], newton[:], rstd0[:], ALU.mult))
            if not first:
                dve.wait_ge(normed_stored, DMA * (v - 1))
                dve.wait_ge(xt_filled, v - 1)
            for t in range(UNIT):
                last = nc.vector.tensor_scalar(normed[:, par, t, :], x_in[:, par, t, :], meanvar[:, t, 0:1],
                                               rstd[:, t:t + 1], ALU.subtract, ALU.mult)
            last.then_inc(normed_ready, 1)

        def unit(i, par, more):
            u = i * 2 + par
            first = isinstance(u, int) and u < 2
            count = [0]
            link = linked(u * VEC + NORM_LINKS, count)
            dve.wait_ge(router_filled, u + 1)
            scores = router_ps.rearrange("p (t e) -> p t e", e=E)
            wide = [P, UNIT, E]
            link(nc.vector.tensor_reduce(out=row4[:], in_=scores, axis=AX, op=ALU.max))
            nc.vector.tensor_tensor(logit[:], scores, row4[:].rearrange("p (t o) -> p t o", o=1).to_broadcast(wide),
                                    ALU.subtract).then_inc(logits_ready, 1)
            dve.wait_ge(exp_ready, u + 1)
            link(nc.vector.tensor_reduce(out=row4[:], in_=prob_e[:], axis=AX, op=ALU.add))
            link(nc.vector.reciprocal(row4[:], row4[:]))
            link(nc.vector.tensor_tensor(prob[:], prob_e[:],
                                         row4[:].rearrange("p (t o) -> p t o", o=1).to_broadcast(wide), ALU.mult), True)
            for t in range(UNIT):
                last = nc.vector.max(out=top[:, t, :], in_=prob[:, t, :])
            link(last, True)
            for t in range(UNIT):
                last = nc.vector.match_replace(out=replaced[:, t, :], in_to_replace=top[:, t, :],
                                               in_values=prob[:, t, :], imm_value=-1.0)
            link(last)
            if not known(u, 1):
                dve.wait_ge(mask_kept, u)
            nc.vector.tensor_tensor(chosen[:], prob[:], replaced[:], ALU.not_equal).then_inc(chosen_ready, 1)
            dve.wait_ge(chosen_ready, u + 1)
            link(nc.vector.tensor_tensor(prob[:], prob[:], chosen[:], ALU.mult))
            link(nc.vector.tensor_reduce(out=row4[:], in_=prob[:], axis=AX, op=ALU.add))
            link(nc.vector.reciprocal(row4[:], row4[:]))
            if not first:
                dve.wait_ge(weight_stored, DMA * (u - 1))
            nc.vector.tensor_tensor(weight[:, par], prob[:], row4[:].rearrange("p (t o) -> p t o", o=1)
                                    .to_broadcast(wide), ALU.mult).then_inc(weight_ready, 1)
            if more:
                norm(u + 1, 1 - par, link)
            for c, (rows, hidden, gate) in enumerate(((P, hidden0, gate_ps), (F2, hidden1, down_ps))):
                dve.wait_ge(exp_g_ready, 2 * u + c + 1)
                link(nc.vector.reciprocal(silu[0:rows, c, :], exp_g[0:rows, c, :]))
                link(nc.vector.tensor_tensor(silu[0:rows, c, :], gate[0:rows, :], silu[0:rows, c, :], ALU.mult))
                if not known(u, 1):
                    dve.wait_ge(down_filled, 2 * u)
                nc.vector.tensor_tensor(hidden[:], up_rest[:] if c else up_ps, silu[0:rows, c, :], ALU.mult
                                        ).then_inc(hidden_ready, 1)
            assert count[0] == VEC or not more, count[0]

        norm(0, 0, linked(0, [0]))
        dve.wait_ge(ws_high, 1)
        nc.vector.tensor_tensor(ws_gu[:, LOW], ws_gu32[:], f32(ws_gu[:, HIGH]), ALU.subtract).then_inc(ws_low, 1)
        weight_low(0)
        unit(0, 0, True)
        weight_low(1)
        unit(0, 1, True)
        weight_low(2)
        with dve.Fori(1, UNITS // 2 - 1) as i:
            unit(i, 0, True)
            unit(i, 1, True)
        unit(UNITS // 2 - 1, 0, True)
        unit(UNITS // 2 - 1, 1, False)

    @block.tensor
    def _(pe):
        def transposes(u, par):
            pe.wait_ge(normed_ready, u + 1)
            if not known(u, 1):
                pe.wait_ge(xt_highs, u)
            for k in range(KD):
                for t in range(UNIT):
                    last = nc.tensor.transpose(transposed_ps[:, k, t * P:(t + 1) * P],
                                               normed[:, par, t, k * P:(k + 1) * P], ident[:])
            last.then_inc(xt_filled, 1)

        def values_in(u, par, lo, hi):
            for n in range(lo, hi):
                t, half = n // 2, n % 2
                if not (isinstance(u, int) and u == 0 and n < 2):
                    pe.wait_ge(v_copied, 8 * u + n - 1)
                terms = [(xt_high, HIGH), (xt_high, LOW), (xt_low, HIGH)]
                for j, (tile, part) in enumerate(terms):
                    for k in range(KD):
                        last = nc.tensor.matmul(psum[:, 6 + n % 2, :], tile[:, par, k, t * P:(t + 1) * P],
                                                wv[:, part, k, half * HALF:(half + 1) * HALF],
                                                start=(j == 0 and k == 0), stop=(j == 2 and k == KD - 1))
                last.then_inc(v_filled, 1)

        def gate_up(u, par, c):
            if not known(u, 1):
                pe.wait_ge(*((shared_ready, 2 * u) if c else (hidden_ready, 2 * (u - 1) + 1)))
            for out, col in ((down_ps, 2 * P),) if c else ((gate_ps, 0), (up_ps, P)):
                for j, (part, tile) in enumerate(((HIGH, xt_high), (LOW, xt_high), (HIGH, xt_low))):
                    for k in range(KD):
                        last = nc.tensor.matmul(out, ws_gu[:, part, k, col:col + P], tile[:, par, k, :],
                                                start=(j == 0 and k == 0), stop=(j == 2 and k == KD - 1))
            last.then_inc(gu_filled, 1)

        def route(u, par):
            pe.wait_ge(xt_highs, u + 1)
            if not known(u, 1):
                pe.wait_ge(logits_ready, u)
            for t in range(UNIT):
                for k in range(KD):
                    last = nc.tensor.matmul(router_ps[:, t * E:(t + 1) * E], xt32[:, par, k, t * P:(t + 1) * P],
                                            router[:, k, :], start=(k == 0), stop=(k == KD - 1))
            last.then_inc(router_filled, 1)

        def unit(i, par, more):
            u = i * 2 + par
            pe.wait_ge(xt_lows, u + 1)
            gate_up(u, par, 0)
            values_in(u, par, 0, 2)
            gate_up(u, par, 1)
            values_in(u, par, 2, 5)
            if more:
                transposes(u + 1, 1 - par)
            values_in(u, par, 5, 8)
            if more:
                route(u + 1, 1 - par)
            pe.wait_ge(hidden_ready, 2 * u + 2)
            for n in range(2):
                if n or not (isinstance(u, int) and u == 0):
                    pe.wait_ge(shared_ready, 2 * u + n)
                for t in range(2):
                    cols = slice((2 * n + t) * P, (2 * n + t + 1) * P)
                    nc.tensor.matmul(down_ps[:, t * D:(t + 1) * D], hidden0[:, cols], ws_d0[:],
                                     start=True, stop=False)
                    last = nc.tensor.matmul(down_ps[:, t * D:(t + 1) * D], hidden1[:, cols], ws_d1[:],
                                            start=False, stop=True)
                last.then_inc(down_filled, 1)

        pe.wait_ge(ready, 3)
        transposes(0, 0)
        pe.wait_ge(weights_in, DMA * 4)
        route(0, 0)
        pe.wait_ge(ws_low, 1)
        pe.wait_ge(w_high, 1)
        pe.wait_ge(w_low, 1)
        unit(0, 0, True)
        unit(0, 1, True)
        with pe.Fori(1, UNITS // 2 - 1) as i:
            unit(i, 0, True)
            unit(i, 1, True)
        unit(UNITS // 2 - 1, 0, True)
        unit(UNITS // 2 - 1, 1, False)


def table_stage(nc, ctx, io, keep):
    def sb(name, shape, dt=F32):
        return ctx.enter_context(nc.sbuf_tensor(name, shape, dt))

    def sem(name):
        return ctx.enter_context(nc.semaphore(name))

    psum, masks = keep["psum"], keep["masks"]
    ones = sb("ones_bf", [P, P], BF16)
    upto = sb("upto", [P, P], BF16)
    slot_f = sb("slot_f", [P, 1])
    pad_row = sb("pad_row", [P, 1])
    expert_i = sb("expert_i", [P, E])
    counts = sb("counts", [P, E, TILES])
    carry = sb("carry", [P, E, TILES])
    running = sb("running", [P, E, TILES])
    before = sb("before", [P, E, TILES])
    tile_of = sb("tile_of", [P, E])
    base = sb("base", [P, E])
    rows = sb("rows_sb", [P, TILES // 2, P])
    scratch = sb("scratch_t", [P, E])

    consts = sem("t_consts")
    counted = sem("counted")
    counts_out = sem("counts_out")
    row_filled = sem("row_filled")
    rows_out = sem("rows_out")
    rows_stored = sem("rows_stored")
    tvec = sem("tvec")
    block = ctx.enter_context(nc.Block())

    @block.gpsimd
    def _(pool):
        nc.gpsimd.memset(ones[:], 1.0).then_inc(consts, 1)
        nc.gpsimd.memset(upto[:], 1.0).then_inc(consts, 1)
        nc.gpsimd.memset(carry[:], 1.0).then_inc(consts, 1)
        nc.gpsimd.iota(slot_f[:], pattern=[[1, 1]], base=0, channel_multiplier=1,
                       allow_small_or_imprecise_dtypes=True).then_inc(consts, 1)
        nc.gpsimd.iota(pad_row[:], pattern=[[1, 1]], base=T, channel_multiplier=1,
                       allow_small_or_imprecise_dtypes=True).then_inc(consts, 1)
        nc.gpsimd.iota(expert_i[:], pattern=[[1, E]], base=0, channel_multiplier=0,
                       allow_small_or_imprecise_dtypes=True).then_inc(consts, 1)
        pool.wait_ge(consts, 6)
        nc.gpsimd.affine_select(out=upto[:], in_=upto[:], compare_op=ALU.is_ge, fill=0.0, base=0,
                                pattern=[[1, P]], channel_multiplier=-1).then_inc(consts, 1)
        nc.gpsimd.memset(carry[:, :, 0:1], 0.0).then_inc(consts, 1)

    @block.tensor
    def _(pe):
        pe.wait_ge(consts, 8)
        flat = masks[:].rearrange("p j e -> p (j e)")
        for n in range(8):
            nc.tensor.matmul(psum[:, n, :], ones[:], flat[:, n * HALF:(n + 1) * HALF], start=True, stop=True
                             ).then_inc(counted, 1)
        for n in range(8):
            pe.wait_ge(counts_out, n + 1)
            for g in range(4):
                j = 4 * n + g
                last = nc.tensor.matmul(psum[:, n, g * P:(g + 1) * P], flat[:, j * P:(j + 1) * P], upto[:],
                                        start=True, stop=True)
            last.then_inc(row_filled, 1)

    @block.scalar
    def _(act):
        for n in range(8):
            act.wait_ge(counted, n + 1)
            nc.scalar.copy(counts[:, :, 8 * n:8 * n + 8].rearrange("p e j -> p j e"),
                           psum[:, n, :].rearrange("p (j e) -> p j e", e=E)).then_inc(counts_out, 1)
        for n in range(8):
            act.wait_ge(row_filled, n + 1)
            nc.scalar.copy(rows[:, 4 * n:4 * n + 4, :], psum[:, n, :].rearrange("p (g q) -> p g q", q=P)
                           ).then_inc(rows_out, 1)

    @block.sync
    def _(sp):
        load_projection(sp, io, keep, 0, 0)
        sp.wait_ge(rows_out, 8)
        sp.dma_start(io["counts"].rearrange("(g r) q -> r g q", r=P), rows[:]).then_inc(rows_stored, DMA)
        sp.wait_ge(rows_stored, DMA)

    @block.vector
    def _(dve):
        count = [0]

        def link(ins):
            count[0] += 1
            ins.then_inc(tvec, 1)
            dve.wait_ge(tvec, count[0])

        dve.wait_ge(consts, 8)
        dve.wait_ge(counts_out, 8)
        link(nc.vector.tensor_tensor_scan(running[:].rearrange("p e j -> p (e j)"),
                                          carry[:].rearrange("p e j -> p (e j)"),
                                          counts[:].rearrange("p e j -> p (e j)"), 0.0, ALU.mult, ALU.add))
        link(nc.vector.tensor_scalar(before[:], running[:], slot_f[:, 0:1], None, ALU.is_le))
        link(nc.vector.tensor_reduce(out=tile_of[:], in_=before[:], axis=AX, op=ALU.add))
        link(nc.vector.tensor_tensor(before[:], before[:], counts[:], ALU.mult))
        link(nc.vector.tensor_reduce(out=base[:], in_=before[:], axis=AX, op=ALU.add))
        nc.vector.tensor_scalar(keep["rank"][:], base[:], -1.0, slot_f[:, 0:1], ALU.mult, ALU.add)
        link(nc.vector.tensor_scalar(keep["valid"][:], tile_of[:], float(TILES), None, ALU.is_lt))
        link(nc.vector.tensor_scalar(base[:], tile_of[:], float(P), pad_row[:, 0:1], ALU.mult, ALU.subtract))
        link(nc.vector.tensor_tensor(base[:], base[:], keep["valid"][:], ALU.mult))
        link(nc.vector.tensor_scalar(keep["first"][:], base[:], pad_row[:, 0:1], None, ALU.add))
        link(nc.vector.tensor_scalar(scratch[:], tile_of[:], float(TILES - 1), float(E), ALU.min, ALU.mult))
        link(nc.vector.tensor_tensor(keep["count_row"][:], scratch[:], expert_i[:], ALU.add))


DVE, ACTE = 0, 1
EMPTIED_BY = {"MAX": DVE, "MT": DVE, "PJ": DVE, "XT": ACTE, "GU": ACTE, "HT": ACTE, "DN": ACTE, "SUM": ACTE}
PARTS = (("score", (0, 0)), ("score", (0, 1)), ("out", 0), ("score", (1, 0)), ("score", (1, 1)), ("out", 1))
BANKS = 3
PLAN = ("M||XT|M M||M",
        "M|SUM0 M||M|M|M M PJ0",
        "PJ1||M GU|||PJ2",
        "M|SUM1 M|M M|PJ3||M M",
        "M||M|M|M|",
        "M|M M|M|HT|M|MT0 M",
        "M||DN M M||M|",
        "|M||MT1||")
DVE_PLAN = ("|||||",
            "|||||",
            "RECIP0|RECIP1||RECIP2|SILU0|SILU1 RECIP3",
            "SILU2||RECIP4 RECIP5|SILU3||",
            "||RECIP6|RECIP7|TOKEN0|",
            "|TOKEN1||OUT0|OUT1|",
            "||TOKEN2|||",
            "|||||")
SIDE = {"XT": 1, "GU": 1, "HT": 1, "DN": 1, "SUM": 0, "MAX": 2, "MT": 2, "PJ": 3}


def places(plan):
    return [(slot, part, name) for slot, line in enumerate(plan)
            for part, names in enumerate(line.split("|")) for name in names.split()]


def step_items(flags):
    units = iter([("MAX", h, qt, half) for h in range(2) for qt in range(KT) for half in range(2)])
    out = []
    for slot, part, name in places(PLAN):
        item = next(units) if name == "M" else (name,) if name.isalpha() else (name[:-1], int(name[-1]))
        if flags[SIDE[item[0]]]:
            out.append((slot, part, item))
    assert next(units, None) is None
    return out


def n_items(flags, who=None):
    return sum(who is None or EMPTIED_BY[it[0]] == who for _, _, it in step_items(flags))


FULL = (True, True, True, True)
HEAD = [(-2, (False, False, False, True)), (-1, (False, False, True, True)), (0, (False, True, True, True)),
        (1, FULL), (2, FULL)]
LOOP0, LOOP1 = 3, NP - 3
TAIL = [(NP - 3, FULL), (NP - 2, (True, True, True, False)), (NP - 1, (True, True, False, False)),
        (NP, (True, False, False, False))]
assert (LOOP1 - LOOP0) % 2 == 0


class Step:

    def __init__(self, s, flags, last, base, counts):
        self.s, self.flags, self.last, self.base, self.counts = s, flags, last, base, counts
        self.items = step_items(flags)

    def emptied(self, sems, k):
        if k >= 0:
            who = EMPTIED_BY[self.items[k][2][0]]
            return sems[who], self.counts[who] + sum(EMPTIED_BY[it[2][0]] == who for it in self.items[:k + 1])
        before = step_items(self.last)
        who = EMPTIED_BY[before[k][2][0]]
        left = sum(EMPTIED_BY[it[2][0]] == who for it in before[len(before) + k + 1:])
        return sems[who], self.counts[who] - left

    def reused(self, sems, k):
        if k >= BANKS:
            return self.emptied(sems, k - BANKS)
        if self.last is None:
            return None
        n = n_items(self.last)
        return self.emptied(sems, max(j for j in range(n) if j % BANKS == k % BANKS) - n)

    def at(self, item):
        return [it for _, _, it in self.items].index(item)


def run_steps(engine, step):
    base, counts, last = 0, [0, 0], None

    def written(steps):
        nonlocal base, counts, last
        for s, flags in steps:
            step(Step(s, flags, last, base, tuple(counts)), s % 2)
            base += n_items(flags)
            counts = [counts[w] + n_items(flags, w) for w in (DVE, ACTE)]
            last = flags

    written(HEAD)
    n, each = n_items(FULL), [n_items(FULL, w) for w in (DVE, ACTE)]
    with engine.Fori(0, (LOOP1 - LOOP0) // 2) as i:
        for k in range(2):
            step(Step(i * 2 + LOOP0 + k, FULL, FULL, i * (2 * n) + base + k * n,
                      tuple(i * (2 * each[w]) + counts[w] + k * each[w] for w in (DVE, ACTE))), (LOOP0 + k) % 2)
    base += n * (LOOP1 - LOOP0)
    counts = [counts[w] + each[w] * (LOOP1 - LOOP0) for w in (DVE, ACTE)]
    written(TAIL)


def one(ap, i, pattern, out):
    return ap[bass.ds(i, 1)].rearrange(f"o {pattern} -> {out}", p=P)


FIRST_RELOAD = LOOP0 + 3
assert FIRST_RELOAD <= PAIRS


def x_loads(pair):
    return 1 if known(pair, FIRST_RELOAD) else pair - (FIRST_RELOAD - 2)


def load_projection(sp, io, keep, p, par):
    if known(p, 1) or not known(p, FIRST_RELOAD):
        sp.dma_start(f32(keep["x_t"][:]), one(io["xt"], p // PAIRS, "p a k c", "(o p) a k c")
                     ).then_inc(keep["x_loaded"], DMA)
    hp = p % PAIRS
    sp.dma_start(f32(keep["w_qk"][:, par]), one(io["wqk"], hp, "p w a k c", "(o p) w a k c")
                 ).then_inc(keep["w_loaded"], DMA)
    sp.dma_start(keep["bias"][:, par, :], one(io["bqk"], hp, "p w", "(o p) w")).then_inc(keep["w_loaded"], DMA)


def attention_stage(nc, ctx, io, keep):
    def sb(name, shape, dt=F32):
        return ctx.enter_context(nc.sbuf_tensor(name, shape, dt))

    def sem(name):
        return ctx.enter_context(nc.semaphore(name))

    psum, ident = keep["psum"], keep["ident"]
    scores_ps = [psum[:, b, :] for b in range(BANKS)]
    out_ps = psum[:, 3:5, :].rearrange("p b c -> p (b c)")
    work = [psum[:, 5 + b, :] for b in range(BANKS)]
    SCORES = 4 * KT

    q_full = sb("q_full", [P, 2, 2, N], F32R)
    q_rest = sb("q_rest", [DK + 1, 2, 2, N], F32R)
    k_full = sb("k_full", [P, 2, 2, N], F32R)
    k_rest = sb("k_rest", [DK + 1, 2, 2, N], F32R)
    high = sb("high", [P, 2, 2, N], F32R)
    low = sb("low", [P, 2, 2, N], F32R)
    x_t, w_qk, bias = keep["x_t"], keep["w_qk"], keep["bias"]
    v_sb = sb("v_sb", [P, 2, KT, P])
    probs = sb("probs", [P, 2, 2, N])
    sums = sb("sums", [P, 2, 2, N])
    out_raw = sb("out_raw", [P, N])
    sum_all = sb("sum_all", [P, N])
    recip = sb("recip", [P, N])
    out_t = sb("out_t", [P, N])
    ones = sb("ones", [P, DK])
    maxima = sb("maxima", [P, 2 * KT, 2])
    merged = sb("merged", [P, 2 * KT])
    minus_max = sb("minus_max", [KT, 2, P], F32R)
    w_gu = sb("w_gu", [P, 2, KD, 2 * F])
    w_d0 = sb("w_d0", [P, 2, D])
    w_d1 = sb("w_d1", [F2, 2, D])
    count_slot = sb("count_slot", [P, 1], U32)
    count_rows = sb("count_rows", [P, P])
    is_before = sb("is_before", [P, P])
    n_before = sb("n_before", [P, 1])
    token = sb("token", [P, 2], U32)
    x_e = sb("x_e", [P, 2, ROW])
    x_et = sb("x_et", [P, KD, P])
    gate_up = sb("gate_up", [P, 2 * F])
    exp_g = sb("exp_ge", [P, F])
    silu = exp_g
    hidden = sb("hidden_e", [P, F])
    hidden_t0 = sb("hidden_t0", [P, P])
    hidden_t1 = sb("hidden_t1", [F2, P])
    y_e = sb("y_e", [P, 2, D])

    set_up = sem("set_up")
    ones_row = sem("ones_row")
    standing = sem("standing")
    x_loaded, w_loaded = keep["x_loaded"], keep["w_loaded"]
    v_loaded = sem("v_loaded")
    highs_ready = sem("highs_ready")
    placed = sem("placed")
    shift_placed = (sem("shift_placed0"), sem("shift_placed1"))
    scores_ready = sem("scores_ready")
    probs_ready = sem("probs_ready")
    pv_done = sem("pv_done")
    out_copied = sem("out_copied")
    sums_added = sem("sums_added")
    out_ready = sem("out_ready")
    out_stored = sem("out_stored")
    work_filled = sem("work_filled")
    emptied = (sem("emptied_by_dve"), sem("emptied_by_act"))
    maxima_merged = sem("maxima_merged")
    experts_loaded = sem("experts_loaded")
    slot_copied = sem("slot_copied")
    counts_loaded = sem("counts_loaded")
    tokens_vec = sem("tokens_vec")
    tokens_ready = sem("tokens_ready")
    tokens_loaded = sem("tokens_loaded")
    gate_ready = sem("gate_ready")
    silu_vec = sem("silu_vec")
    hidden_ready = sem("hidden_e_ready")
    recip_ready = sem("recip_ready")
    scattered = sem("scattered")

    block = ctx.enter_context(nc.Block())
    SHUFFLES = 12

    @block.tensor
    def _(pe):
        pe.wait_ge(set_up, 2)

        def score(s, par, kt, h, half):
            n = 4 * kt + 2 * h + half
            if n >= BANKS:
                pe.wait_ge(probs_ready, SCORES * s + n - BANKS + 1)
            elif not known(s, 1):
                before = max(m for m in range(SCORES) if m % BANKS == n)
                pe.wait_ge(probs_ready, SCORES * s - (SCORES - before - 1))
            if n == 0:
                if known(s, 1):
                    pe.wait_ge(ones_row, 1)
                pe.wait_ge(placed, DMA * SHUFFLES * (s + 1))
            keys = slice(kt * P, (kt + 1) * P)
            cols = slice(half * HALF, (half + 1) * HALF)
            nc.tensor.matmul(scores_ps[n % BANKS], k_full[:, par, h, keys], q_full[:, par, h, cols],
                             start=True, stop=False)
            if kt == 0 and half == 0:
                pe.wait_ge(shift_placed[h], DMA * (s + 1))
            nc.tensor.matmul(scores_ps[n % BANKS], k_rest[:, par, h, keys], q_rest[:, par, h, cols],
                             start=False, stop=True).then_inc(scores_ready, 1)

        def pv(p, par, kt, half):
            if half == 0:
                pe.wait_ge(probs_ready, SCORES * p + 4 * kt + 4)
                if kt == 0:
                    pe.wait_ge(v_loaded, DMA * (p + 1))
                    if not known(p, 1):
                        pe.wait_ge(out_copied, p)
            cols = slice(half * HALF, (half + 1) * HALF)
            for h in range(2):
                rows = slice(DK * h, DK * (h + 1))
                last = nc.tensor.matmul(out_ps[rows, cols], v_sb[:, par, kt, rows], probs[:, h, kt % 2, cols],
                                        start=(kt == 0), stop=(kt == KT - 1))
            if half == 1:
                last.then_inc(pv_done, 1)

        def item(st, par, k, what):
            s = st.s
            out = work[k % BANKS]
            kind = what[0]
            if st.reused(emptied, k):
                pe.wait_ge(*st.reused(emptied, k))
            if kind == "PJ":
                which, half = what[1] // 2, what[1] % 2
                cols = slice(half * HALF, (half + 1) * HALF)
                if what[1] == 0:
                    pe.wait_ge(x_loaded, DMA * x_loads(s + 2))
                    pe.wait_ge(w_loaded, 2 * DMA * (s + 3))
                terms = [(HIGH, HIGH), (LOW, HIGH), (HIGH, LOW)]
                for j, (wp, xp) in enumerate(terms):
                    for kd in range(KD):
                        last = nc.tensor.matmul(out, w_qk[:, par, which, wp, kd, :], x_t[:, xp, kd, cols],
                                                start=(j == 0 and kd == 0), stop=(j == 2 and kd == KD - 1))
            elif kind == "MAX":
                _, h, qt, half = what
                rows = slice(DK * h, DK * (h + 1))
                if (h, qt, half) == (0, 0, 0):
                    pe.wait_ge(highs_ready, 4 * (s + 2))
                last = nc.tensor.matmul(out, high[rows, 1 - par, 0, qt * P:(qt + 1) * P],
                                        high[rows, 1 - par, 1, half * HALF:(half + 1) * HALF], start=True, stop=True)
            elif kind == "MT":
                h = what[1]
                pe.wait_ge(maxima_merged, 2 * (s + 1) + h + 1)
                last = nc.tensor.matmul(out[0:KT, 0:P], merged[:, h * KT:(h + 1) * KT], ident[:],
                                        start=True, stop=True)
            elif kind == "SUM":
                cols = slice(what[1] * HALF, (what[1] + 1) * HALF)
                if what[1] == 0:
                    pe.wait_ge(sums_added, 14 * s)
                for h in range(2):
                    last = nc.tensor.matmul(out[DK * h:DK * (h + 1), :], ones[:], sums[:, 1 - par, h, cols],
                                            start=True, stop=True)
            elif kind == "XT":
                pe.wait_ge(tokens_loaded, DMA * (s + 1))
                for kd in range(KD):
                    last = nc.tensor.transpose(out[:, kd * P:(kd + 1) * P], x_e[:, par, kd * P:(kd + 1) * P], ident[:])
            elif kind == "GU":
                pe.wait_ge(experts_loaded, 4 * DMA * (s + 1))
                pe.wait_ge(*st.emptied(emptied, st.at(("XT",))))
                for kd in range(KD):
                    last = nc.tensor.matmul(out[:, 0:2 * F], x_et[:, kd, :], w_gu[:, par, kd, :],
                                            start=(kd == 0), stop=(kd == KD - 1))
            elif kind == "HT":
                pe.wait_ge(hidden_ready, s + 1)
                nc.tensor.matmul(out[:, 0:P], hidden[:, 0:P], ident[:], start=True, stop=True)
                last = nc.tensor.matmul(out[0:F2, P:2 * P], hidden[:, P:F], ident[:], start=True, stop=True)
            elif kind == "DN":
                pe.wait_ge(*st.emptied(emptied, st.at(("HT",))))
                nc.tensor.matmul(out[:, 0:D], hidden_t0[:], w_d0[:, par, :], start=True, stop=False)
                last = nc.tensor.matmul(out[:, 0:D], hidden_t1[:], w_d1[:, par, :], start=False, stop=True)
            last.then_inc(work_filled, 1)

        def step(st, par):
            s, (fin, att, nxt, prj) = st.s, st.flags
            k = 0
            for kt in range(KT):
                for part in range(len(PARTS)):
                    kind, which = PARTS[part]
                    if kind == "score" and att:
                        score(s, par, kt, *which)
                    elif kind == "out" and kt == 0 and fin:
                        pv(s - 1, 1 - par, KT - 1, which)
                    elif kind == "out" and kt > 0 and att:
                        pv(s, par, kt - 1, which)
                    while k < len(st.items) and st.items[k][:2] == (kt, part):
                        item(st, par, k, st.items[k][2])
                        k += 1

        run_steps(pe, step)

    @block.scalar
    def _(act):
        def read(st, par, k, what):
            s, bank, kind = st.s, work[k % BANKS], what[0]
            if EMPTIED_BY[kind] == ACTE or kind == "PJ":
                act.wait_ge(work_filled, st.base + k + 1)
            if kind == "PJ":
                which, half = what[1] // 2, what[1] % 2
                if what[1] == 0 and not known(s, 0):
                    act.wait_ge(placed, DMA * SHUFFLES * (s + 1))
                nc.scalar.activation(high[:, par, which, half * HALF:(half + 1) * HALF], bank,
                                     ACT.Identity, bias=bias[:, par, which:which + 1]
                                     ).then_inc(highs_ready, 1)
            elif kind == "SUM":
                nc.scalar.copy(sum_all[:, what[1] * HALF:(what[1] + 1) * HALF], bank).then_inc(emptied[ACTE], 1)
            elif kind == "XT":
                nc.scalar.copy(x_et[:].rearrange("p k c -> p (k c)"), bank[:, 0:D]).then_inc(emptied[ACTE], 1)
            elif kind == "GU":
                nc.scalar.activation(exp_g[:], bank[:, 0:F], ACT.Exp, scale=-1.0).then_inc(gate_ready, 1)
                nc.scalar.copy(gate_up[:], bank[:, 0:2 * F]).then_inc(emptied[ACTE], 1)
            elif kind == "HT":
                nc.scalar.copy(hidden_t0[:], bank[:, 0:P])
                nc.scalar.copy(hidden_t1[:], bank[0:F2, P:2 * P]).then_inc(emptied[ACTE], 1)
            elif kind == "DN":
                if not known(s, 2):
                    act.wait_ge(scattered, DMA * (s - 1))
                nc.scalar.activation(y_e[:, par, :], bank[:, 0:D], ACT.Copy, scale=x_e[:, par, bass.ds(s + D, 1)]
                                     ).then_inc(emptied[ACTE], 1)

        def step(st, par):
            s, (fin, att, nxt, prj) = st.s, st.flags
            k = 0
            for kt in range(KT):
                for part in range(len(PARTS)):
                    kind, which = PARTS[part]
                    if kind == "score" and att:
                        h, half = which
                        n = 4 * kt + 2 * h + half
                        act.wait_ge(scores_ready, SCORES * s + n + 1)
                        if half == 0 and not (isinstance(s, int) and s == 0 and kt < 2):
                            act.wait_ge(pv_done, 8 * s + kt - 1)
                            added = 14 * s + (2 * (kt - 3) + h if kt >= 3 else h if kt == 2 else
                                              2 * (kt + 5) + h - 14)
                            act.wait_ge(sums_added, added + 1)
                        nc.scalar.activation(probs[:, h, kt % 2, half * HALF:(half + 1) * HALF],
                                             scores_ps[n % BANKS], ACT.Exp, scale=SCALE).then_inc(probs_ready, 1)
                    while k < len(st.items) and st.items[k][:2] == (kt, part):
                        read(st, par, k, st.items[k][2])
                        k += 1
                if kt == 0 and fin:
                    act.wait_ge(pv_done, 8 * s)
                    if not known(s, 2):
                        act.wait_ge(out_ready, s - 1)
                    nc.scalar.copy(out_raw[:], out_ps).then_inc(out_copied, 1)

        run_steps(act, step)

    @block.vector
    def _(dve):
        nc.vector.memset(ones[:], 1.0).then_inc(set_up, 1)
        nc.vector.memset(maxima[:], 0.0).then_inc(set_up, 1)

        def read(st, par, k, what):
            s, bank, kind = st.s, work[k % BANKS], what[0]
            if EMPTIED_BY[kind] != DVE:
                return
            if kind == "MT":
                h = what[1]
                tiles = slice(h * KT, (h + 1) * KT)
                dve.wait_ge(*st.emptied(emptied, st.at(("MAX", h, KT - 1, 1))))
                nc.vector.tensor_reduce(out=merged[:, tiles], in_=maxima[:, tiles, :], axis=AX, op=ALU.max
                                        ).then_inc(maxima_merged, 1)
            dve.wait_ge(work_filled, st.base + k + 1)
            if kind == "PJ":
                which, half = what[1] // 2, what[1] % 2
                cols = slice(half * HALF, (half + 1) * HALF)
                dve.wait_ge(highs_ready, 4 * (s + 2) + what[1] + 1)
                last = nc.vector.scalar_tensor_tensor(
                    out=low[:, par, which, cols], in0=bank, scalar=bias[:, par, which:which + 1],
                    in1=f32(high[:, par, which, cols]), op0=ALU.add, op1=ALU.subtract)
            elif kind == "MAX":
                _, h, qt, half = what
                last = nc.vector.tensor_reduce(out=maxima[:, h * KT + qt, half:half + 1], in_=bank, axis=AX,
                                               op=ALU.max)
            elif kind == "MT":
                if not known(s, 0):
                    dve.wait_ge(shift_placed[h], DMA * (s + 1))
                last = nc.vector.tensor_scalar(minus_max[:, h, :], bank[0:KT, 0:P], -1.0, None, ALU.mult)
            last.then_inc(emptied[DVE], 1)

        def job(st, par, what):
            s, (kind, n) = st.s, what
            if kind == "RECIP":
                if n % 4 == 0:
                    dve.wait_ge(*st.emptied(emptied, st.at(("SUM", n // 4))))
                cols = slice(n * P, (n + 1) * P)
                last = nc.vector.reciprocal(recip[:, cols], sum_all[:, cols]).then_inc(recip_ready, 1)
            elif kind == "OUT":
                cols = slice(n * HALF, (n + 1) * HALF)
                if n == 0:
                    dve.wait_ge(recip_ready, 8 * s)
                    dve.wait_ge(out_copied, s)
                    if not known(s, 2):
                        dve.wait_ge(out_stored, DMA * (s - 1))
                last = nc.vector.tensor_tensor(out_t[:, cols], out_raw[:, cols], recip[:, cols], ALU.mult)
                if n == 1:
                    last.then_inc(out_ready, 1)
            elif kind == "SILU":
                if n == 0:
                    dve.wait_ge(*st.emptied(emptied, st.at(("GU",))))
                    nc.vector.tensor_scalar(silu[:], exp_g[:], 1.0, None, ALU.add).then_inc(silu_vec, 1)
                    return
                dve.wait_ge(silu_vec, 3 * s + n)
                if n == 1:
                    nc.vector.reciprocal(silu[:], silu[:]).then_inc(silu_vec, 1)
                elif n == 2:
                    nc.vector.tensor_tensor(silu[:], gate_up[:, 0:F], silu[:], ALU.mult).then_inc(silu_vec, 1)
                else:
                    nc.vector.tensor_tensor(hidden[:], gate_up[:, F:2 * F], silu[:], ALU.mult
                                            ).then_inc(hidden_ready, 1)
            elif kind == "TOKEN":
                e = s + 1
                if n == 0:
                    dve.wait_ge(counts_loaded, DMA * (s + 2))
                    nc.vector.tensor_scalar(is_before[:], count_rows[:], keep["rank"][:, bass.ds(e, 1)], None,
                                            ALU.is_le).then_inc(tokens_vec, 1)
                    return
                dve.wait_ge(tokens_vec, 2 * s + 2 + n)
                if n == 1:
                    nc.vector.tensor_reduce(out=n_before[:], in_=is_before[:], axis=AX, op=ALU.add
                                            ).then_inc(tokens_vec, 1)
                else:
                    if not known(s, 1):
                        dve.wait_ge(scattered, DMA * s)
                    nc.vector.tensor_scalar(token[:, 1 - par:2 - par], n_before[:], keep["valid"][:, bass.ds(e, 1)],
                                            keep["first"][:, bass.ds(e, 1)], ALU.mult, ALU.add
                                            ).then_inc(tokens_ready, 1)

        needs = {"RECIP": 0, "OUT": 0, "SILU": 1, "TOKEN": 2}

        def step(st, par):
            k = 0
            for kt in range(KT):
                for part in range(len(PARTS)):
                    for slot, place, name in places(DVE_PLAN):
                        if (slot, place) == (kt, part) and st.flags[needs[name[:-1]]]:
                            job(st, par, (name[:-1], int(name[-1])))
                    while k < len(st.items) and st.items[k][:2] == (kt, part):
                        read(st, par, k, st.items[k][2])
                        k += 1

        run_steps(dve, step)

    @block.gpsimd
    def _(pool):
        nc.gpsimd.memset(is_before[:], 0.0).then_inc(standing, 1)
        pool.wait_ge(standing, 1)
        nc.gpsimd.memset(f32(k_rest[DK:DK + 1, :, :, :]), 1.0).then_inc(ones_row, 1)
        pool.wait_ge(ones_row, 1)

        def step(st, par):
            s, (fin, att, nxt, prj) = st.s, st.flags
            if nxt:
                if not known(s, 0):
                    pool.wait_ge(tokens_ready, s + 1)
                nc.gpsimd.tensor_copy(count_slot[:], keep["count_row"][:, bass.ds(s + 1, 1)]).then_inc(slot_copied, 1)
                alone(pool, (standing, 1), (slot_copied, s + 2))
                nc.gpsimd.indirect_dma_start(
                    out=count_rows[:], out_offset=None, in_=io["counts"],
                    in_offset=bass.IndirectOffsetOnAxis(ap=count_slot[:, 0:1], axis=0)).then_inc(counts_loaded, DMA)
            for kt in range(1, KT) if att else ():
                for h in range(2):
                    pool.wait_ge(probs_ready, SCORES * s + 4 * kt + 2 * h + 2)
                    if kt == 1:
                        if not known(s, 2):
                            pool.wait_ge(out_ready, s - 1)
                        first = probs[:, h, 0, :]
                    else:
                        first = sums[:, par, h, :]
                        pool.wait_ge(sums_added, 14 * s + 2 * (kt - 2) + h + 1)
                    nc.gpsimd.tensor_tensor(sums[:, par, h, :], first, probs[:, h, kt % 2, :], ALU.add
                                            ).then_inc(sums_added, 1)
                if kt == 5 and nxt:
                    fetch(s, par)
            if nxt and not att:
                fetch(s, par)
            if att:
                waits = [st.emptied(emptied, st.at(("DN",)))]
                if not known(s, 1):
                    waits.append((scattered, DMA * s))
                alone(pool, (standing, 1), *waits)
                nc.gpsimd.indirect_dma_start(
                    out=io["moe"], out_offset=bass.IndirectOffsetOnAxis(ap=token[:, par:par + 1], axis=0),
                    in_=y_e[:, par, :], in_offset=None, compute_op=ALU.add).then_inc(scattered, DMA)

        def fetch(s, par):
            alone(pool, (standing, 1), (tokens_ready, s + 2))
            nc.gpsimd.indirect_dma_start(
                out=x_e[:, 1 - par, :], out_offset=None, in_=io["rows"],
                in_offset=bass.IndirectOffsetOnAxis(ap=token[:, 1 - par:2 - par], axis=0)
            ).then_inc(tokens_loaded, DMA)

        run_steps(pool, step)
        pool.wait_ge(scattered, DMA * NP)

    @block.sync
    def _(sp):
        def shift_out(st, par, h):
            sp.wait_ge(*st.emptied(emptied, st.at(("MT", h))))
            sp.dma_start(f32(q_rest[DK:DK + 1, 1 - par, h, :]), f32(minus_max[:, h, :])
                         ).then_inc(shift_placed[h], DMA)

        def step(st, par):
            s, (fin, att, nxt, prj) = st.s, st.flags
            if nxt:
                p, pp = s + 1, 1 - par
                e = p
                if att:
                    waits = [(placed, DMA * SHUFFLES * (s + 1)), (v_loaded, DMA * (s + 1)),
                             (experts_loaded, 4 * DMA * (s + 1)), (shift_placed[0], DMA * (s + 1)), (shift_placed[1], DMA * (s + 1))]
                    if fin:
                        waits.append((pv_done, 8 * s))
                    alone(sp, (standing, 1), *waits)
                sp.dma_start(v_sb[:, pp], one(io["v"], p, "p t c", "(o p) t c")).then_inc(v_loaded, DMA)
                if known(st.counts[ACTE], 1):
                    sp.wait_ge(emptied[DVE], st.counts[DVE])
                else:
                    alone(sp, (standing, 1), (emptied[DVE], st.counts[DVE]), (emptied[ACTE], st.counts[ACTE]))
                for h in range(2):
                    rows = slice(DK * h, DK * (h + 1))
                    top, bottom = slice(0, DK), slice(DK, P)
                    for dst, to, src, which in ((k_full, top, high, 1), (k_full, bottom, high, 1),
                                                (q_full, top, high, 0), (q_full, bottom, low, 0),
                                                (k_rest, top, low, 1), (q_rest, top, high, 0)):
                        sp.dma_start(f32(dst[to, pp, h, :]), f32(src[rows, pp, which, :])).then_inc(placed, DMA)
                sp.dma_start(w_gu[:, pp, :, 0:F], one(io["w_gate"], e, "(k p) f", "p (o k) f")
                             ).then_inc(experts_loaded, DMA)
                sp.dma_start(w_gu[:, pp, :, F:2 * F], one(io["w_up"], e, "(k p) f", "p (o k) f")
                             ).then_inc(experts_loaded, DMA)
                sp.dma_start(w_d0[:, pp, :], io["w_down"][bass.ds(e, 1), 0:P, :].rearrange("o p d -> (o p) d")
                             ).then_inc(experts_loaded, DMA)
                sp.dma_start(w_d1[:, pp, :], io["w_down"][bass.ds(e, 1), P:F, :].rearrange("o p d -> (o p) d")
                             ).then_inc(experts_loaded, DMA)
            if prj and not (isinstance(s, int) and s == NP - 3):
                alone(sp, (standing, 1), (x_loaded, DMA * x_loads(s + 2)), (w_loaded, 2 * DMA * (s + 3)),
                      st.emptied(emptied, st.at(("PJ", 3))))
                load_projection(sp, io, keep, s + 3, 1 - par)
            if nxt:
                shift_out(st, par, 0)
            if fin:
                if known(s, 2):
                    sp.wait_ge(out_ready, s)
                else:
                    alone(sp, (standing, 1), (out_stored, DMA * (s - 1)), (out_ready, s))
                sp.dma_start(one(io["ot"], s - 1, "p c", "(o p) c"), out_t[:]).then_inc(out_stored, DMA)
            if nxt:
                shift_out(st, par, 1)

        sp.dma_start(keep["wo32"][:], io["wo"].rearrange("(h p) d -> p h d", p=P)).then_inc(keep["loaded_w"], DMA)
        run_steps(sp, step)
        sp.wait_ge(out_stored, DMA * NP)


def output_stage(nc, ctx, io, keep):
    def sb(name, shape, dt=F32):
        return ctx.enter_context(nc.sbuf_tensor(name, shape, dt))

    def sem(name):
        return ctx.enter_context(nc.semaphore(name))

    psum, ident = keep["psum"], keep["ident"]
    wo32, loaded_w = keep["wo32"], keep["loaded_w"]
    wo = sb("wo", [P, 2, PAIRS, D], F32R)
    bv = sb("bv", [P, PAIRS])
    bo = sb("bo", [P, KD])
    const = sb("const", [P, KD])
    ot32 = sb("ot32", [P, 2, PAIRS, HALF])
    ot = sb("ot_sb", [P, 2, 2, PAIRS, HALF], F32R)
    projected = sb("projected", [P, 2, KD, HALF])
    x_in = sb("x_out", [P, 2, UNIT, D])
    moe = sb("moe_sb", [P, 2, UNIT, D])
    rest = sb("rest", [P, 2, UNIT, D])
    y = sb("y", [P, 2, UNIT, D])

    loaded_b = sem("loaded_b")
    wo_high = sem("wo_high")
    wo_low = sem("wo_low")
    const_filled = sem("const_filled")
    const_ready = sem("const_ready")
    ot_loaded = (sem("ot_loaded0"), sem("ot_loaded1"))
    ot_high = sem("ot_high")
    ot_low = sem("ot_low")
    xm_loaded = sem("xm_loaded")
    rest_ready = sem("rest_ready")
    project_filled = sem("project_filled")
    project_copied = sem("project_copied")
    y_filled = sem("y_filled")
    y_ready = sem("y_ready")
    y_stored = sem("y_stored")
    block = ctx.enter_context(nc.Block())

    x_v = io["x"].rearrange("(u t p) d -> u p t d", p=P, t=UNIT)
    moe_v = io["moe"][0:T, :].rearrange("(u t p) d -> u p t d", p=P, t=UNIT)
    out_v = io["out"].rearrange("(u t p) d -> u p t d", p=P, t=UNIT)
    parts = "o p t d -> (o p) t d"
    BATCH = 4

    def rounds(engine, unit):
        unit(0, 0)
        unit(0, 1)
        with engine.Fori(1, UNITS // 2) as i:
            unit(i, 0)
            unit(i, 1)

    @block.sync
    def _(sp):
        def unit(i, par):
            u = i * 2 + par
            waits = [(ot_loaded[0], DMA * u), (ot_loaded[1], DMA * u), (xm_loaded, 2 * DMA * u)] if not known(u, 1) else []
            if not known(u, 2):
                waits += [(ot_low, 2 * (u - 1)), (rest_ready, u - 1)]
            if waits:
                alone(sp, (loaded_w, DMA), *waits)
            for n in range(2):
                sp.dma_start(ot32[:, par, n * BATCH:(n + 1) * BATCH],
                             io["ot"][bass.ds(i * PAIRS + n * BATCH, BATCH), :, par * HALF:(par + 1) * HALF]
                             .rearrange("h p c -> p h c")).then_inc(ot_loaded[n], DMA)
            if known(u, 1):
                sp.dma_start(bv[:], io["bv"]).then_inc(loaded_b, DMA)
                sp.dma_start(bo[:], io["bo"]).then_inc(loaded_b, DMA)
            sp.dma_start(x_in[:, par], x_v[bass.ds(u, 1)].rearrange(parts)).then_inc(xm_loaded, DMA)
            sp.dma_start(moe[:, par], moe_v[bass.ds(u, 1)].rearrange(parts)).then_inc(xm_loaded, DMA)

        rounds(sp, unit)

    @block.gpsimd
    def _(pool):
        def unit(i, par):
            u = i * 2 + par
            pool.wait_ge(xm_loaded, 2 * DMA * (u + 1))
            if not known(u, 2):
                pool.wait_ge(y_ready, 2 * (u - 1))
            nc.gpsimd.tensor_tensor(rest[:, par], x_in[:, par], moe[:, par], ALU.add).then_inc(rest_ready, 1)

        rounds(pool, unit)

    @block.scalar
    def _(act):
        act.wait_ge(loaded_w, DMA)
        nc.scalar.copy(wo[:, HIGH], wo32[:]).then_inc(wo_high, 1)

        def project_out(u, par):
            for c in range(KD):
                act.wait_ge(project_filled, KD * u + c + 1)
                if c == 0 and not known(u, 2):
                    act.wait_ge(y_filled, 2 * (u - 1))
                nc.scalar.activation(projected[:, par, c, :], psum[:, 2 * par + c, :], ACT.Identity,
                                     bias=const[:, c:c + 1]).then_inc(project_copied, 1)

        def unit(i, par):
            u = i * 2 + par
            if not known(u, 2):
                act.wait_ge(project_filled, KD * (u - 1))
            for n in range(2):
                act.wait_ge(ot_loaded[n], DMA * (u + 1))
                pairs = slice(n * BATCH, (n + 1) * BATCH)
                nc.scalar.copy(ot[:, par, HIGH, pairs], ot32[:, par, pairs]).then_inc(ot_high, 1)
            if known(u, 1):
                act.wait_ge(const_ready, 1)
            else:
                project_out(u - 1, 1 - par)
                if not known(u, 2):
                    store(u - 2, par)

        def store(v, par):
            if not known(v, 1):
                act.wait_ge(y_stored, DMA * v)
            act.wait_ge(y_ready, 2 * (v + 1))
            act.dma_start(out_v[bass.ds(v, 1)].rearrange(parts), y[:, par]).then_inc(y_stored, DMA)

        unit(0, 0)
        unit(0, 1)
        unit(1, 0)
        unit(1, 1)
        with act.Fori(2, UNITS // 2) as i:
            unit(i, 0)
            unit(i, 1)
        project_out(UNITS - 1, 1)
        store(UNITS - 2, 0)
        store(UNITS - 1, 1)
        act.wait_ge(y_stored, DMA * UNITS)

    @block.vector
    def _(dve):
        dve.wait_ge(wo_high, 1)
        nc.vector.tensor_tensor(wo[:, LOW], wo32[:], f32(wo[:, HIGH]), ALU.subtract).then_inc(wo_low, 1)

        def add_rest(u, par):
            dve.wait_ge(rest_ready, u + 1)
            if not known(u, 2):
                dve.wait_ge(y_stored, DMA * (u - 1))
            for n in range(2):
                dve.wait_ge(y_filled, 2 * u + n + 1)
                nc.vector.tensor_tensor(y[:, par, 2 * n:2 * n + 2, :],
                                        psum[:, 4 + 2 * par + n, :].rearrange("p (t d) -> p t d", d=D),
                                        rest[:, par, 2 * n:2 * n + 2, :], ALU.add).then_inc(y_ready, 1)

        def unit(i, par):
            u = i * 2 + par
            for n in range(2):
                pairs = slice(n * BATCH, (n + 1) * BATCH)
                dve.wait_ge(ot_high, 2 * u + n + 1)
                nc.vector.tensor_tensor(ot[:, par, LOW, pairs], ot32[:, par, pairs], f32(ot[:, par, HIGH, pairs]),
                                        ALU.subtract).then_inc(ot_low, 1)
            if known(u, 1):
                dve.wait_ge(const_filled, 1)
                dve.wait_ge(loaded_b, 2 * DMA)
                nc.vector.tensor_tensor(const[:], psum[:, 7, 0:KD], bo[:], ALU.add).then_inc(const_ready, 1)
            elif not known(u, 2):
                add_rest(u - 2, par)

        unit(0, 0)
        unit(0, 1)
        unit(1, 0)
        unit(1, 1)
        with dve.Fori(2, UNITS // 2) as i:
            unit(i, 0)
            unit(i, 1)
        add_rest(UNITS - 2, 0)
        add_rest(UNITS - 1, 1)

    @block.tensor
    def _(pe):
        def project(u, par, c):
            if not known(u, 2):
                pe.wait_ge(project_copied, KD * (u - 2) + c + 1)
            n = 0
            for batch in range(2):
                for t, o in ((HIGH, HIGH), (LOW, HIGH), (HIGH, LOW)):
                    if c == 0:
                        if o == HIGH and t == HIGH:
                            pe.wait_ge(ot_high, 2 * u + batch + 1)
                        elif o == LOW:
                            pe.wait_ge(ot_low, 2 * u + batch + 1)
                    for h in range(batch * BATCH, (batch + 1) * BATCH):
                        last = nc.tensor.matmul(psum[:, 2 * par + c, :], wo[:, t, h, c * P:(c + 1) * P],
                                                ot[:, par, o, h, :], start=(n == 0), stop=(n == 3 * PAIRS - 1))
                        n += 1
            last.then_inc(project_filled, 1)

        def turn(u, par):
            pe.wait_ge(project_copied, KD * (u + 1))
            if not known(u, 2):
                pe.wait_ge(y_ready, 2 * (u - 1))
            for n in range(2):
                for t in range(2):
                    for c in range(KD):
                        tok = slice((2 * n + t) * P, (2 * n + t + 1) * P)
                        last = nc.tensor.transpose(psum[:, 4 + 2 * par + n, t * D + c * P:t * D + (c + 1) * P],
                                                   projected[:, par, c, tok], ident[:])
                last.then_inc(y_filled, 1)

        def unit(i, par):
            u = i * 2 + par
            project(u, par, 0)
            if known(u, 1):
                pe.wait_ge(loaded_b, 2 * DMA)
                for c in range(KD):
                    for h in range(PAIRS):
                        last = nc.tensor.matmul(psum[:, 7, c:c + 1], wo32[:, h, c * P:(c + 1) * P], bv[:, h:h + 1],
                                                start=(h == 0), stop=(h == PAIRS - 1))
                last.then_inc(const_filled, 1)
            project(u, par, 1)
            if not known(u, 1):
                turn(u - 1, 1 - par)

        pe.wait_ge(wo_high, 1)
        pe.wait_ge(wo_low, 1)
        rounds(pe, unit)
        turn(UNITS - 1, 1)


def build(nc, io):
    def dram(name, shape):
        return nc.dram_tensor(name, shape, F32, kind="Internal").ap()

    io["rows"] = dram("rows", [T + C, ROW])
    io["moe"] = dram("moe", [T + C, D])
    io["xt"] = dram("xt", [B, P, 2, KD, N])
    io["v"] = dram("v", [NP, P, KT, P])
    io["wqk"] = dram("wqk_parts", [PAIRS, P, 2, 2, KD, P])
    io["counts"] = dram("counts_rows", [TILES * E, P])
    io["ot"] = dram("ot", [NP, P, N])
    with ExitStack() as ctx:
        keep = {
            "psum": ctx.enter_context(nc.psum_tensor("psum", [P, 8, HALF], F32)),
            "ident": ctx.enter_context(nc.sbuf_tensor("ident", [P, P], F32)),
        }
        for name in ("rank", "valid", "first"):
            keep[name] = ctx.enter_context(nc.sbuf_tensor(name, [P, E], F32))
        keep["x_t"] = ctx.enter_context(nc.sbuf_tensor("x_t", [P, 2, KD, N], F32R))
        keep["w_qk"] = ctx.enter_context(nc.sbuf_tensor("w_qk", [P, 2, 2, 2, KD, P], F32R))
        keep["bias"] = ctx.enter_context(nc.sbuf_tensor("bias", [P, 2, 2], F32))
        keep["wo32"] = ctx.enter_context(nc.sbuf_tensor("wo32", [P, PAIRS, D], F32))
        keep["loaded_w"] = ctx.enter_context(nc.semaphore("loaded_w"))
        keep["x_loaded"] = ctx.enter_context(nc.semaphore("xt_loaded"))
        keep["w_loaded"] = ctx.enter_context(nc.semaphore("w_loaded"))
        keep["count_row"] = ctx.enter_context(nc.sbuf_tensor("count_row", [P, E], U32))
        with ExitStack() as mctx:
            keep["masks"] = mctx.enter_context(nc.sbuf_tensor("masks", [P, TILES, E], BF16))
            with ExitStack() as sub:
                norm_stage(nc, sub, io, keep)
            with ExitStack() as sub:
                table_stage(nc, sub, io, keep)
        with ExitStack() as sub:
            attention_stage(nc, sub, io, keep)
        with ExitStack() as sub:
            output_stage(nc, sub, io, keep)


def kernel(**inputs):
    import numpy as np
    import concourse.bacc as bacc
    from concourse.bass_utils import run_bass_kernel_spmd

    a = {k.replace("L0_", ""): np.asarray(v) for k, v in inputs.items()}
    arrays = {
        "x": a["attn_y"].reshape(T, D),
        "wq": a["attn_Wq"].T, "wk": a["attn_Wk"].T, "wv": a["attn_Wv"].T, "wo": a["attn_Wo"].T,
        "bqk": np.stack([a["attn_bq"].reshape(PAIRS, P), a["attn_bk"].reshape(PAIRS, P)], axis=-1),
        "bv": a["attn_bv"].reshape(PAIRS, P).T, "bo": a["attn_bo"].reshape(KD, P).T,
        "router": a["ffn_router_w"].T, "w_gate": a["ffn_w_gate"], "w_up": a["ffn_w_up"],
        "w_down": a["ffn_w_down"], "ws_gu": np.concatenate([a["ffn_ws_gate_up"][:, c] for c in (
            slice(0, P), slice(F, F + P), slice(P, F), slice(F + P, 2 * F))], axis=1), "ws_d": a["ffn_ws_down"],
    }
    nc = bacc.Bacc("TRN2", target_bir_lowering=False, num_devices=1)
    io, feed = {}, {}
    for name, v in arrays.items():
        v = np.ascontiguousarray(v)
        feed[f"in_{name}"] = v
        io[name] = nc.dram_tensor(f"in_{name}", v.shape, F32, kind="ExternalInput").ap()
    io["out"] = nc.dram_tensor("out_y", (T, D), F32, kind="ExternalOutput").ap()
    build(nc, io)
    got = run_bass_kernel_spmd(nc, [feed], core_ids=[0])
    return got.results[0]["out_y"].reshape(B, N, D)
```
